# Optimizing a Trainium2 kernel written in Bass

```python
import numpy as np
import jax
import jax.numpy as jnp

def _softmax(x, axis=-1):
    return jax.nn.softmax(x, axis=axis)

def _gelu(x):
    return jax.nn.gelu(x, approximate=True)

def _silu(x):
    return jax.nn.silu(x)

def _sigmoid(x):
    return jax.nn.sigmoid(x)

def _layernorm(x, axis=-1, eps=1e-05):
    m = jnp.mean(x, axis=axis, keepdims=True)
    v = jnp.var(x, axis=axis, keepdims=True)
    return (x - m) / jnp.sqrt(v + eps)

def _scatter_add(tgt, idx, src, axis=0):
    return tgt.at[idx].add(src)

def _segment_sum(src, seg, n):
    return jax.ops.segment_sum(src, seg, n)
kernel_name = 'mk_gnn_resnorm_d4_gnn_r8_680c00'

def setup_inputs(seed: int=0):
    np.random.seed(seed)
    _w = jnp.asarray

    def _rec_inputs():
        import jax
        import jax.numpy as jnp
        _gk = jax.random.key(seed)
        x = -0.0009044 + 1 * jax.random.normal(jax.random.fold_in(_gk, 1), (12500, 32), jnp.float32)
        _s = jax.random.randint(jax.random.fold_in(_gk, 2), (200000,), 0, 12500, jnp.int32)
        _d = jax.random.randint(jax.random.fold_in(_gk, 3), (200000,), 0, 12500, jnp.int32)
        _loop = jnp.arange(12500, dtype=jnp.int32)
        src = jnp.concatenate([_s, _d, _loop])
        dst = jnp.concatenate([_d, _s, _loop])
        _o = jnp.argsort(dst, stable=True)
        src = src[_o]
        dst = dst[_o]
        edge_attr_16 = 0.000196303 + 1.00016 * jax.random.normal(jax.random.fold_in(_gk, 12), (412500, 16), jnp.float32)
        edge_attr_3 = 0.000844983 + 0.999762 * jax.random.normal(jax.random.fold_in(_gk, 13), (412500, 3), jnp.float32)
        edge_weight = jax.random.uniform(jax.random.fold_in(_gk, 15), (412500,), jnp.float32, 0.0, 1)
        return (x, src, dst, edge_attr_16, edge_attr_3, edge_weight)
    x, src, dst, edge_attr_16, edge_attr_3, edge_weight = _rec_inputs()

    def _L0_gnn_setup():
        import jax, jax.numpy as jnp
        import numpy as np
        N = 6250
        E = 200000
        DN = 32
        DE = 16
        DI = DN + DE
        DH = 2 * DI

        def _linear_params(key, fan_in, fan_out, dtype=jnp.float32):
            k1, k2 = jax.random.split(key)
            bound = 1.0 / np.sqrt(fan_in)
            w = jax.random.uniform(k1, (fan_in, fan_out), dtype, -bound, bound)
            b = jax.random.uniform(k2, (fan_out,), dtype, -bound, bound)
            return (w, b)
        key = jax.random.key(seed)
        ks = jax.random.split(key, 7)
        x = jax.random.normal(ks[0], (N, DN), dtype=jnp.float32)
        edge_index = jax.random.randint(ks[1], (2, E), 0, N, dtype=jnp.int64)
        edge_attr = jax.random.normal(ks[2], (E, DE), dtype=jnp.float32)
        w1a, b1a = _linear_params(ks[3], DI, DH)
        w1b, b1b = _linear_params(ks[4], DH, DH)
        w2a, b2a = _linear_params(ks[5], DN + DH, DI)
        w2b, b2b = _linear_params(ks[6], DI, DN)
        return {'x': x, 'edge_index': edge_index, 'edge_attr': edge_attr, 'w1a': w1a, 'b1a': b1a, 'w1b': w1b, 'b1b': b1b, 'w2a': w2a, 'b2a': b2a, 'w2b': w2b, 'b2b': b2b}
    _L0_gnn_all = _L0_gnn_setup()
    _L0_gnn_in = {k: v for k, v in _L0_gnn_all.items() if k in ('w1a', 'b1a', 'w1b', 'b1b', 'w2a', 'b2a', 'w2b', 'b2b')}
    del _L0_gnn_all

    def _L1_gnn_setup():
        import jax, jax.numpy as jnp
        import numpy as np
        N_NODES = 12500
        N_EDGES = 200000
        D_FEAT = 32
        K = 10
        ALPHA = 0.1
        key = jax.random.key(seed)
        k1, k2, k3 = jax.random.split(key, 3)
        feat = jax.random.normal(k1, (N_NODES, D_FEAT), dtype=jnp.float32)
        src = jax.random.randint(k2, (N_EDGES,), 0, N_NODES, dtype=jnp.int64)
        dst = jax.random.randint(k3, (N_EDGES,), 0, N_NODES, dtype=jnp.int64)
        return {'feat': feat, 'src': src, 'dst': dst}
    _L1_gnn_all = _L1_gnn_setup()
    _L1_gnn_in = {k: v for k, v in _L1_gnn_all.items() if k in ()}
    del _L1_gnn_all

    def _L2_gnn_setup():
        import jax, jax.numpy as jnp
        import numpy as np
        N_NODES = 12500
        key = jax.random.key(seed)
        k1, k2 = jax.random.split(key)
        x = jax.random.normal(k1, (N_NODES, 32), dtype=jnp.float32)
        edge_index = jax.random.randint(k2, (2, 200000), 0, N_NODES, dtype=jnp.int64)
        return {'x': x, 'edge_index': edge_index}
    _L2_gnn_all = _L2_gnn_setup()
    _L2_gnn_in = {k: v for k, v in _L2_gnn_all.items() if k in ()}
    del _L2_gnn_all

    def _L3_gnn_setup():
        import jax, jax.numpy as jnp
        import numpy as np
        from math import factorial, pi, sqrt
        MUL = 8
        RS = [(MUL, 0), (MUL, 1)]
        N_NODES = 2500
        N_EDGES = 80000
        FEAT_DIM = sum((m * (2 * l + 1) for m, l in RS))
        R_DIM = sum((mo * mi * (2 * min(lo, li) + 1) for mo, lo in RS for mi, li in RS))
        HIDDEN = 64

        def _cg(j1, j2, j3, m1, m2, m3):
            if m1 + m2 != m3:
                return 0.0
            f = factorial
            pre = sqrt((2 * j3 + 1) * f(j3 + j1 - j2) * f(j3 - j1 + j2) * f(j1 + j2 - j3) / f(j1 + j2 + j3 + 1))
            pre *= sqrt(f(j3 + m3) * f(j3 - m3) * f(j1 - m1) * f(j1 + m1) * f(j2 - m2) * f(j2 + m2))
            kmin = max(0, j2 - j3 - m1, j1 - j3 + m2)
            kmax = min(j1 + j2 - j3, j1 - m1, j2 + m2)
            s = 0.0
            for k in range(kmin, kmax + 1):
                s += (-1) ** k / (f(k) * f(j1 + j2 - j3 - k) * f(j1 - m1 - k) * f(j2 + m2 - k) * f(j3 - j2 + m1 + k) * f(j3 - j1 - m2 + k))
            return pre * s

        def _w3j_complex(l1, l2, l3):
            w = np.zeros((2 * l1 + 1, 2 * l2 + 1, 2 * l3 + 1))
            for m1 in range(-l1, l1 + 1):
                for m2 in range(-l2, l2 + 1):
                    m3 = -(m1 + m2)
                    if abs(m3) <= l3:
                        w[m1 + l1, m2 + l2, m3 + l3] = (-1) ** (l1 - l2 - m3) / sqrt(2 * l3 + 1) * _cg(l1, l2, l3, m1, m2, -m3)
            return w

        def _A(l):
            A = np.zeros((2 * l + 1, 2 * l + 1), dtype=complex)
            A[l, l] = 1.0
            for m in range(1, l + 1):
                A[l + m, l + m] = (-1) ** m / sqrt(2)
                A[l + m, l - m] = 1.0 / sqrt(2)
                A[l - m, l - m] = 1j / sqrt(2)
                A[l - m, l + m] = -1j * (-1) ** m / sqrt(2)
            return A

        def real_w3j(l1, l2, l3):
            wc = _w3j_complex(l1, l2, l3).astype(complex)
            wr = np.einsum('abc,ma,nb,oc->mno', wc, _A(l1).conj(), _A(l2).conj(), _A(l3).conj())
            i = int(np.argmax(np.abs(wr)))
            ph = wr.flat[i] / abs(wr.flat[i])
            wr = wr / ph
            assert np.abs(wr.imag).max() < 1e-10
            return np.real(wr).astype(np.float32)
        _W3J = {}
        for _mo, _lo in RS:
            for _mi, _li in RS:
                for _lf in range(abs(_lo - _li), _lo + _li + 1):
                    if (_lo, _lf, _li) not in _W3J:
                        _W3J[_lo, _lf, _li] = jnp.asarray(real_w3j(_lo, _lf, _li))
        _NORM = []
        for _mo, _lo in RS:
            _num = sum((mi * (2 * min(_lo, li) + 1) for mi, li in RS))
            _NORM.append(sqrt(4.0 * pi) * sqrt(2.0 * _lo + 1.0) / sqrt(_num))
        _F_OFFS = [0] + list(np.cumsum([mi * (2 * li + 1) for mi, li in RS]))

        def spherical_harmonics(rel_vec):
            r = rel_vec / jnp.linalg.norm(rel_vec, axis=-1, keepdims=True)
            x, y, z = (r[:, 0], r[:, 1], r[:, 2])
            y0 = jnp.full_like(x, 0.5 / sqrt(pi))[:, None]
            c1 = sqrt(3.0 / (4.0 * pi))
            y1 = c1 * jnp.stack([y, z, x], axis=-1)
            c2a = 0.5 * sqrt(15.0 / pi)
            c2b = 0.25 * sqrt(5.0 / pi)
            c2c = 0.25 * sqrt(15.0 / pi)
            y2 = jnp.stack([c2a * x * y, c2a * y * z, c2b * (3.0 * z * z - 1.0), c2a * x * z, c2c * (x * x - y * y)], axis=-1)
            return jnp.concatenate([y0, y1, y2], axis=-1)
        key = jax.random.key(seed)
        ks = jax.random.split(key, 6)
        features = jax.random.normal(ks[0], (N_NODES, FEAT_DIM), dtype=jnp.float32)
        abs_distances = jax.random.uniform(ks[1], (N_EDGES,), dtype=jnp.float32, minval=0.1, maxval=1.0)
        rel_vec = jax.random.normal(ks[2], (N_EDGES, 3), dtype=jnp.float32)
        edge_index = jax.random.randint(ks[3], (2, N_EDGES), 0, N_NODES, dtype=jnp.int32)
        w1 = jax.random.normal(ks[4], (1, HIDDEN), dtype=jnp.float32)
        b1 = jnp.zeros((HIDDEN,), jnp.float32)
        w2 = jax.random.normal(ks[5], (HIDDEN, R_DIM), dtype=jnp.float32) / sqrt(HIDDEN)
        b2 = jnp.zeros((R_DIM,), jnp.float32)
        return {'features': features, 'abs_distances': abs_distances, 'rel_vec': rel_vec, 'edge_index': edge_index, 'w1': w1, 'b1': b1, 'w2': w2, 'b2': b2}
    _L3_gnn_all = _L3_gnn_setup()
    _L3_gnn_in = {k: v for k, v in _L3_gnn_all.items() if k in ('w1', 'b1', 'w2', 'b2')}
    del _L3_gnn_all
    return {'x': x, 'src': src, 'dst': dst, 'edge_attr_16': edge_attr_16, 'edge_attr_3': edge_attr_3, 'edge_weight': edge_weight, 'L0_gnn_w1a': _L0_gnn_in['w1a'], 'L0_gnn_b1a': _L0_gnn_in['b1a'], 'L0_gnn_w1b': _L0_gnn_in['w1b'], 'L0_gnn_b1b': _L0_gnn_in['b1b'], 'L0_gnn_w2a': _L0_gnn_in['w2a'], 'L0_gnn_b2a': _L0_gnn_in['b2a'], 'L0_gnn_w2b': _L0_gnn_in['w2b'], 'L0_gnn_b2b': _L0_gnn_in['b2b'], 'L3_gnn_w1': _L3_gnn_in['w1'], 'L3_gnn_b1': _L3_gnn_in['b1'], 'L3_gnn_w2': _L3_gnn_in['w2'], 'L3_gnn_b2': _L3_gnn_in['b2']}

def reference(x, src, dst, edge_attr_16, edge_attr_3, edge_weight, L0_gnn_w1a, L0_gnn_b1a, L0_gnn_w1b, L0_gnn_b1b, L0_gnn_w2a, L0_gnn_b2a, L0_gnn_w2b, L0_gnn_b2b, L3_gnn_w1, L3_gnn_b1, L3_gnn_w2, L3_gnn_b2):
    import jax
    import jax.numpy as jnp

    def _L0_gnn_ref(x, edge_index, edge_attr, w1a, b1a, w1b, b1b, w2a, b2a, w2b, b2b):
        import jax, jax.numpy as jnp
        import numpy as np
        N = 6250
        E = 200000
        DN = 32
        DE = 16
        DI = DN + DE
        DH = 2 * DI

        def _linear_params(key, fan_in, fan_out, dtype=jnp.float32):
            k1, k2 = jax.random.split(key)
            bound = 1.0 / np.sqrt(fan_in)
            w = jax.random.uniform(k1, (fan_in, fan_out), dtype, -bound, bound)
            b = jax.random.uniform(k2, (fan_out,), dtype, -bound, bound)
            return (w, b)
        row = edge_index[0]
        col = edge_index[1]
        h = jnp.concatenate([x[row], edge_attr], axis=1)
        h = jnp.maximum(h @ w1a + b1a, 0.0)
        h = h @ w1b + b1b
        s = jax.ops.segment_sum(h, col, num_segments=x.shape[0])
        cnt = jax.ops.segment_sum(jnp.ones((col.shape[0],), x.dtype), col, num_segments=x.shape[0])
        agg = s / jnp.maximum(cnt, 1.0)[:, None]
        h2 = jnp.concatenate([x, agg], axis=1)
        h2 = jnp.maximum(h2 @ w2a + b2a, 0.0)
        return h2 @ w2b + b2b

    def _L1_gnn_ref(feat, src, dst):
        import jax, jax.numpy as jnp
        import numpy as np
        N_NODES = 12500
        N_EDGES = 200000
        D_FEAT = 32
        K = 10
        ALPHA = 0.1
        n = feat.shape[0]
        ones = jnp.ones(src.shape[0], dtype=feat.dtype)
        out_deg = jax.ops.segment_sum(ones, src, num_segments=n)
        in_deg = jax.ops.segment_sum(ones, dst, num_segments=n)
        src_norm = jnp.clip(out_deg, 1.0, None) ** (-0.5)
        dst_norm = jnp.clip(in_deg, 1.0, None) ** (-0.5)
        feat0 = feat

        def step(f, _):
            f = f * src_norm[:, None]
            agg = jax.ops.segment_sum(f[src], dst, num_segments=n)
            f = agg * dst_norm[:, None]
            f = (1.0 - ALPHA) * f + ALPHA * feat0
            return (f, None)
        feat, _ = jax.lax.scan(step, feat, None, length=K)
        return feat

    def _L2_gnn_ref(x, edge_index):
        import jax, jax.numpy as jnp
        import numpy as np
        N_NODES = 12500
        src = edge_index[0]
        dst = edge_index[1]
        x_j = x[src]
        out = jax.ops.segment_sum(x_j, dst, num_segments=x.shape[0])
        return out

    def _L3_gnn_ref(features, abs_distances, rel_vec, edge_index, w1, b1, w2, b2):
        import jax, jax.numpy as jnp
        import numpy as np
        from math import factorial, pi, sqrt
        MUL = 8
        RS = [(MUL, 0), (MUL, 1)]
        N_NODES = 2500
        N_EDGES = 80000
        FEAT_DIM = sum((m * (2 * l + 1) for m, l in RS))
        R_DIM = sum((mo * mi * (2 * min(lo, li) + 1) for mo, lo in RS for mi, li in RS))
        HIDDEN = 64

        def _cg(j1, j2, j3, m1, m2, m3):
            if m1 + m2 != m3:
                return 0.0
            f = factorial
            pre = sqrt((2 * j3 + 1) * f(j3 + j1 - j2) * f(j3 - j1 + j2) * f(j1 + j2 - j3) / f(j1 + j2 + j3 + 1))
            pre *= sqrt(f(j3 + m3) * f(j3 - m3) * f(j1 - m1) * f(j1 + m1) * f(j2 - m2) * f(j2 + m2))
            kmin = max(0, j2 - j3 - m1, j1 - j3 + m2)
            kmax = min(j1 + j2 - j3, j1 - m1, j2 + m2)
            s = 0.0
            for k in range(kmin, kmax + 1):
                s += (-1) ** k / (f(k) * f(j1 + j2 - j3 - k) * f(j1 - m1 - k) * f(j2 + m2 - k) * f(j3 - j2 + m1 + k) * f(j3 - j1 - m2 + k))
            return pre * s

        def _w3j_complex(l1, l2, l3):
            w = np.zeros((2 * l1 + 1, 2 * l2 + 1, 2 * l3 + 1))
            for m1 in range(-l1, l1 + 1):
                for m2 in range(-l2, l2 + 1):
                    m3 = -(m1 + m2)
                    if abs(m3) <= l3:
                        w[m1 + l1, m2 + l2, m3 + l3] = (-1) ** (l1 - l2 - m3) / sqrt(2 * l3 + 1) * _cg(l1, l2, l3, m1, m2, -m3)
            return w

        def _A(l):
            A = np.zeros((2 * l + 1, 2 * l + 1), dtype=complex)
            A[l, l] = 1.0
            for m in range(1, l + 1):
                A[l + m, l + m] = (-1) ** m / sqrt(2)
                A[l + m, l - m] = 1.0 / sqrt(2)
                A[l - m, l - m] = 1j / sqrt(2)
                A[l - m, l + m] = -1j * (-1) ** m / sqrt(2)
            return A

        def real_w3j(l1, l2, l3):
            wc = _w3j_complex(l1, l2, l3).astype(complex)
            wr = np.einsum('abc,ma,nb,oc->mno', wc, _A(l1).conj(), _A(l2).conj(), _A(l3).conj())
            i = int(np.argmax(np.abs(wr)))
            ph = wr.flat[i] / abs(wr.flat[i])
            wr = wr / ph
            assert np.abs(wr.imag).max() < 1e-10
            return np.real(wr).astype(np.float32)
        _W3J = {}
        for _mo, _lo in RS:
            for _mi, _li in RS:
                for _lf in range(abs(_lo - _li), _lo + _li + 1):
                    if (_lo, _lf, _li) not in _W3J:
                        _W3J[_lo, _lf, _li] = jnp.asarray(real_w3j(_lo, _lf, _li))
        _NORM = []
        for _mo, _lo in RS:
            _num = sum((mi * (2 * min(_lo, li) + 1) for mi, li in RS))
            _NORM.append(sqrt(4.0 * pi) * sqrt(2.0 * _lo + 1.0) / sqrt(_num))
        _F_OFFS = [0] + list(np.cumsum([mi * (2 * li + 1) for mi, li in RS]))

        def spherical_harmonics(rel_vec):
            r = rel_vec / jnp.linalg.norm(rel_vec, axis=-1, keepdims=True)
            x, y, z = (r[:, 0], r[:, 1], r[:, 2])
            y0 = jnp.full_like(x, 0.5 / sqrt(pi))[:, None]
            c1 = sqrt(3.0 / (4.0 * pi))
            y1 = c1 * jnp.stack([y, z, x], axis=-1)
            c2a = 0.5 * sqrt(15.0 / pi)
            c2b = 0.25 * sqrt(5.0 / pi)
            c2c = 0.25 * sqrt(15.0 / pi)
            y2 = jnp.stack([c2a * x * y, c2a * y * z, c2b * (3.0 * z * z - 1.0), c2a * x * z, c2c * (x * x - y * y)], axis=-1)
            return jnp.concatenate([y0, y1, y2], axis=-1)
        src, dst = (edge_index[0], edge_index[1])
        R = jax.nn.relu(abs_distances[:, None] @ w1 + b1) @ w2 + b2
        Y = spherical_harmonics(rel_vec)
        Fj = features[src]
        E = Fj.shape[0]
        msg_blocks = []
        r_off = 0
        for i, (mo, lo) in enumerate(RS):
            acc = jnp.zeros((E, mo, 2 * lo + 1), dtype=features.dtype)
            for j, (mi, li) in enumerate(RS):
                n_lf = 2 * min(lo, li) + 1
                sz = mo * mi * n_lf
                Rb = R[:, r_off:r_off + sz].reshape(E, mo, mi, n_lf)
                r_off += sz
                Fb = Fj[:, _F_OFFS[j]:_F_OFFS[j + 1]].reshape(E, mi, 2 * li + 1)
                for k, lf in enumerate(range(abs(lo - li), lo + li + 1)):
                    C = _W3J[lo, lf, li]
                    Yf = Y[:, lf * lf:(lf + 1) * (lf + 1)]
                    acc = acc + _NORM[i] * jnp.einsum('euv,ef,evi,ofi->euo', Rb[..., k], Yf, Fb, C)
            msg_blocks.append(acc.reshape(E, -1))
        msg = jnp.concatenate(msg_blocks, axis=-1)
        out = jnp.zeros((features.shape[0], msg.shape[1]), dtype=features.dtype)
        out = out.at[dst].add(msg)
        return out
    edge_index = jnp.stack([src, dst])
    x = _layernorm(x + _L0_gnn_ref(x, edge_index, edge_attr_16, L0_gnn_w1a, L0_gnn_b1a, L0_gnn_w1b, L0_gnn_b1b, L0_gnn_w2a, L0_gnn_b2a, L0_gnn_w2b, L0_gnn_b2b), axis=-1)
    x = _layernorm(x + _L1_gnn_ref(x, src, dst), axis=-1)
    x = _layernorm(x + _L2_gnn_ref(x, edge_index), axis=-1)
    x = _layernorm(x + _L3_gnn_ref(x, edge_weight, edge_attr_3, edge_index, L3_gnn_w1, L3_gnn_b1, L3_gnn_w2, L3_gnn_b2), axis=-1)
    return x

_drawn_inputs = setup_inputs


def setup_inputs(seed=0):
    import zlib

    import numpy as np

    out = dict(_drawn_inputs(seed))
    spreads = {'L3_gnn_b1': (0.0, 0.1), 'L3_gnn_b2': (0.0, 0.1)}
    factors = {'edge_attr_16': 8.0, 'L0_gnn_w1a': 5.264, 'L0_gnn_b1a': 3.031}
    for name, (base, spread) in spreads.items():
        noise = np.random.default_rng([zlib.crc32(name.encode()), seed]).standard_normal(out[name].shape)
        drawn = base * np.exp(spread * noise) if base else spread * noise
        out[name] = jnp.asarray(drawn.astype(out[name].dtype))
    for name, factor in factors.items():
        out[name] = (out[name] * factor).astype(out[name].dtype)
    return out
```

```python
import math

import concourse.bass as bass
from concourse import mybir
from contextlib import ExitStack

F32 = mybir.dt.float32
BF16 = mybir.dt.bfloat16
FP8 = mybir.dt.float8e4
I32 = mybir.dt.int32
U8 = mybir.dt.uint8
ALU = mybir.AluOpType
ACT = mybir.ActivationFunctionType
AX = mybir.AxisListType

N, E, D = 12500, 412500, 32
P = 128
NB = (N + P - 1) // P
NPAD = NB * P
LAST = N - (NB - 1) * P
EP = 125
COLS = E // EP
G = 10
GE = G * EP
NG = E // GE
PAIRS = NG // 2
DE, DI, DH = 16, 48, 96
HID = 64
STEPS, ALPHA = 10, 0.1
EPS = 1e-5

CB = 7
CW = CB * P
HW = CW // 2
NCH = NB // CB
HH = 14
HG = NB // HH
PLANE = NCH * HG * P * HH * CW
SPARE = -(-PLANE // (1 << 19)) << 19
DIGITS = 5
BATCH = 30
KPAD = EP * (COLS + 20)
NODE_BITS = 14
DST_MASK = (1 << NODE_BITS) - 1
DIV_CB = (9363, 16)
DIV_HH = (4682, 16)
TESTS = [48, 64, 128, 512, 2048, 8192, 32768, 131072]
NT = len(TESTS)


def view(ap, offset, dims):
    return bass.AP(ap.tensor, ap.offset + offset, [list(ap.ap[0])] + [list(d) for d in dims])


def plane_part(plane, u):
    parts = plane[0:PLANE, :].rearrange("(u p n) o -> u p (n o)", u=NCH * HG, p=P)
    return parts[bass.ds(u, 1), :, :].rearrange("a p n -> (a p) n")


def await_alone(eng, passed, sem, value):
    eng.wait_ge(sem, value)
    eng.sem_inc(passed, 1)


class Build:
    pass


def build(nc, io, out):
    ctx = ExitStack()
    with ctx:
        k = Build()
        k.io, k.out = io, out

        def sem(name):
            return ctx.enter_context(nc.semaphore(name))

        def sb(name, shape, dt, stack=ctx):
            return stack.enter_context(nc.sbuf_tensor(name, shape, dt))

        def pb(name, shape, dt, stack):
            return stack.enter_context(nc.psum_tensor(name, shape, dt))

        k.sem, k.sb, k.pb = sem, sb, pb

        def dram(name, shape, dt):
            return nc.dram_tensor(name, shape, dt, kind="Internal").ap()

        k.planes = [dram(f"multiplicity_digit{d}", (SPARE + E, 1), U8) for d in range(DIGITS)]
        k.keys_d = dram("edge_keys", (KPAD + E + KPAD,), I32)
        k.dst_d = dram("dst_float", (E,), F32)
        k.hist_d = dram("src_split", (E, 2), BF16)
        k.xin_d = dram("edge_inputs", (NG, EP, G * DI), F32)
        k.dir_d = dram("edge_directions", (E, 5), F32)
        k.range_d = dram("block_ranges", (2, NG), I32)
        k.x3_d = dram("x_after_layer3", (NPAD, D), F32)

        k.passed_pool, k.passed_pe = sem("passed_pool"), sem("passed_pe")

        k.x = sb("x", [P, NB, D], F32)
        k.iota = sb("iota", [P, P], F32)
        k.ident = sb("ident", [P, P], F32)
        k.ctl = sb("ctl", [1, 8], I32)
        k.table = sb("block_table", [1, 2, NG], I32)
        k.small = sb("small", [P, NB, 2], F32)

        with ExitStack() as scatter_data:
            k.index = sb("scatter_index", [EP, COLS], I32, scatter_data)
            k.digit = sb("scatter_digit", [EP, DIGITS, COLS], U8, scatter_data)
            with ExitStack() as s:
                prepare(nc, k, s)
            with ExitStack() as s:
                edge_network(nc, k, s)
        with ExitStack() as s:
            propagate(nc, k, s)
        with ExitStack() as s:
            tensor_messages(nc, k, s)


def prepare(nc, k, s):
    sb, pb, sem, io = k.sb, k.pb, k.sem, k.io
    iota_i = sb("iota_i", [P, 2, P], I32, s)
    pcol = sb("pcol", [P, 1], F32, s)
    dst = sb("dst_i", [EP, COLS], I32, s)
    src = sb("src_i", [EP, COLS], I32, s)
    key = sb("key", [EP, COLS], I32, s)
    ta = sb("ta", [EP, COLS], I32, s)
    tb = sb("tb", [EP, COLS], I32, s)
    near = [sb(f"near_keys{n}", [EP, COLS], I32, s) for n in range(2)]
    zeros = sb("zeros_u8", [P, HH * CW], U8, s)
    minus = view(view(k.digit[:], 0, [[1, DIGITS * COLS]]).bitcast(I32), 0, [[1, KPAD // EP]])
    mult = view(ta[:], 0, [[1, COLS]]).bitcast(F32)
    behind = src[:].bitcast(F32)
    number = dst
    tests = sb("tests", [P, 16], F32, s)
    row = sb("row", [16, 32], F32, s)
    weights = sb("weights", [1, 16], F32, s)
    GR = 3
    RP = NG // GR
    dst_g = sb("dst_g", [RP, GR, GE], I32, s)
    rng = sb("rng", [RP, 2, GR], F32, s)
    rng_i = sb("rng_i", [RP, 2, GR], I32, s)
    idx = [sb(f"l0_idx{m}", [EP, G], I32, s) for m in range(2)]
    ea = [sb(f"l0_ea{m}", [EP, G, DE], F32, s) for m in range(2)]
    xin = [sb(f"l0_xin{m}", [EP, G, DI], F32, s) for m in range(2)]
    tp = pb("prep_ps", [16, P], F32, s)

    edges_loaded, ranges_loaded, x_loaded = sem("edges_loaded"), sem("ranges_loaded"), sem("x_loaded")
    iota_done, const_done, x_zero = sem("iota_done"), sem("const_done"), sem("x_zero")
    minus_ready, minus_stored = sem("minus_ready"), sem("minus_stored")
    zero_ready, planes_zeroed = sem("zero_ready"), sem("planes_zeroed")
    key_ready, key_stored = sem("key_ready"), sem("key_stored")
    packed_ready, packed_stored = sem("packed_ready"), sem("packed_stored")
    near_loaded = [sem(f"near_loaded{n}") for n in range(2)]
    near_used = sem("near_used")
    rng_ready, rng_stored, rng_back = sem("rng_ready"), sem("rng_stored"), sem("rng_back")
    tests_ready, tests_turned, best_ready, best_turned = (sem(x) for x in (
        "tests_ready", "tests_turned", "best_ready", "best_turned"))
    bound_ready = sem("bound_ready")
    idx_loaded = [sem(f"idx_loaded{m}") for m in range(2)]
    ea_loaded = [sem(f"ea_loaded{m}") for m in range(2)]
    gathered = [sem(f"gathered{m}") for m in range(2)]
    xin_stored = [sem(f"xin_stored{m}") for m in range(2)]
    ea_copied, dst_used = sem("ea_copied"), sem("dst_used")

    resident = lambda a: a.rearrange("(p c) -> p c", p=EP)
    k.idx_view = io["src"].rearrange("(g p j) -> g p j", p=EP, j=G)
    ea_view = io["edge_attr_16"].rearrange("(g p j) f -> g p (j f)", p=EP, j=G)

    with nc.Block() as block:

        @block.sync
        def _(sp):
            sp.dma_start(dst[:], resident(io["dst"])).then_inc(edges_loaded, 16)
            sp.dma_start(src[:], resident(io["src"])).then_inc(edges_loaded, 16)
            sp.dma_start(dst_g[:], io["dst"].rearrange("(p g c) -> p g c", p=RP, g=GR)).then_inc(ranges_loaded, 16)
            sp.wait_ge(minus_ready, 1)
            for at in (0, KPAD + E):
                sp.dma_start(k.keys_d[at:at + KPAD].rearrange("(p c) -> p c", p=EP), minus).then_inc(minus_stored, 16)
            sp.wait_ge(x_zero, 1)
            full = (NB - 1) * P
            sp.dma_start(k.x[:, 0:NB - 1, :], io["x"][0:full, :].rearrange("(b p) f -> p b f", p=P)).then_inc(x_loaded, 16)
            sp.dma_start(k.x[0:LAST, NB - 1, :], io["x"][full:N, :]).then_inc(x_loaded, 16)
            sp.wait_ge(key_ready, 1)
            sp.dma_start(resident(k.keys_d[KPAD:KPAD + E]), key[:]).then_inc(key_stored, 16)
            sp.wait_ge(packed_ready, 1)
            sp.dma_start(resident(k.dst_d), near[0][:].bitcast(F32)).then_inc(packed_stored, 16)
            sp.wait_ge(packed_ready, 2)
            sp.dma_start(k.hist_d.rearrange("(p c) t -> p (c t)", p=EP), near[1][:].bitcast(BF16)).then_inc(packed_stored, 16)
            sp.wait_ge(rng_ready, 1)
            sp.dma_start(k.range_d.rearrange("t (p g) -> p t g", g=GR), rng_i[:]).then_inc(rng_stored, 16)
            sp.wait_ge(rng_stored, 16)
            for t in range(2):
                sp.dma_start(k.table[0:1, t, :], k.range_d[t:t + 1, :]).then_inc(rng_back, 16)
            sp.wait_ge(x_loaded, 32)
            sp.wait_ge(rng_back, 32)
            sp.wait_ge(key_stored, 16)
            sp.wait_ge(minus_stored, 32)
            sp.wait_ge(packed_stored, 32)
            for n, far in enumerate(TESTS + [1]):
                if n >= 2:
                    sp.wait_ge(near_used, n - 1)
                sp.dma_start(near[n % 2][:], resident(k.keys_d[KPAD + far:KPAD + far + E])).then_inc(near_loaded[n % 2], 16)
            sp.wait_ge(bound_ready, 1)
            bound = sp.value_load(k.ctl[0:1, 0:1], min_val=2, max_val=E)
            sp.wait_ge(near_used, NT + 1)
            with sp.Fori(1, bound + 1) as far:
                for n in range(2):
                    if n == 0:
                        at = far * -1 + KPAD
                    else:
                        at = far + KPAD
                    sp.wait_ge(near_used, far * 2 + (NT - 2 + n))
                    sp.dma_start(near[n][:], resident(k.keys_d[bass.ds(at, E)])).then_inc(near_loaded[n], 16)

        @block.gpsimd
        def _(pool):
            pool.iota(iota_i[:, 0, :], [[1, P]], base=0, channel_multiplier=0).then_inc(iota_done, 1)
            pool.iota(iota_i[:, 1, 0:1], [[0, 1]], base=0, channel_multiplier=1).then_inc(iota_done, 1)
            pool.wait_ge(dst_used, 1)
            pool.iota(number[:], [[1, COLS]], base=0, channel_multiplier=COLS).then_inc(iota_done, 1)
            def gather(i, m, first):
                n = i + 1
                await_alone(pool, k.passed_pool, idx_loaded[m], n * 16)
                if not first:
                    await_alone(pool, k.passed_pool, xin_stored[m], i * 16)
                for j in range(G):
                    pool.indirect_dma_start(xin[m][:, j, 0:D], None, io["x"],
                                            bass.IndirectOffsetOnAxis(idx[m][:, j:j + 1], 0)).then_inc(gathered[m], 16)
            for m in range(2):
                gather(0, m, True)
            with pool.Fori(1, PAIRS) as i:
                for m in range(2):
                    gather(i, m, False)

        @block.scalar
        def _(act):
            def load(i, m):
                act.dma_start(idx[m][:], k.idx_view[bass.ds(i * 2 + m, 1), :, :].rearrange("a p j -> (a p) j")).then_inc(idx_loaded[m], 16)
                act.dma_start(view(ea[m][:], 0, [[1, G * DE]]), ea_view[bass.ds(i * 2 + m, 1), :, :].rearrange("a p j -> (a p) j")).then_inc(ea_loaded[m], 16)

            def group(i, m, first, last):
                if not (last and m == 1):
                    load(i + m, 1 - m)
                if not first:
                    act.wait_ge(xin_stored[m], i * 16)
                act.wait_ge(ea_loaded[m], (i + 1) * 16)
                nc.scalar.copy(xin[m][:, :, D:DI], ea[m][:]).then_inc(ea_copied, 1)
                act.wait_ge(gathered[m], (i + 1) * (16 * G))
                act.wait_ge(ea_copied, i * 2 + (m + 1))
                act.dma_start(k.xin_d[bass.ds(i * 2 + m, 1), :, :].rearrange("a p j -> (a p) j"),
                              view(xin[m][:], 0, [[1, G * DI]])).then_inc(xin_stored[m], 16)

            load(0, 0)
            for m in range(2):
                group(0, m, True, False)
            act.wait_ge(zero_ready, 1)
            with act.Fori(1, NCH * HG + 1) as i:
                for m in range(2):
                    group(i, m, False, False)
                act.dma_start(plane_part(k.planes[0], i - 1), zeros[:]).then_inc(planes_zeroed, 16)
            with act.Fori(NCH * HG + 1, PAIRS - 1) as i:
                for m in range(2):
                    group(i, m, False, False)
            for m in range(2):
                group(PAIRS - 1, m, False, True)
            for m in range(2):
                act.wait_ge(xin_stored[m], PAIRS * 16)
            act.wait_ge(planes_zeroed, NCH * HG * 16)

        @block.vector
        def _(dve):
            ts, tt = nc.vector.tensor_scalar, nc.vector.tensor_tensor
            nc.vector.memset(k.x[:, NB - 1, :], 0.0).then_inc(x_zero, 1)
            nc.vector.memset(minus, -1).then_inc(minus_ready, 1)
            nc.vector.memset(zeros[:].bitcast(I32), 0).then_inc(zero_ready, 1)
            nc.vector.memset(tests[:], 0.0)
            dve.wait_ge(iota_done, 2)
            nc.vector.tensor_copy(pcol[:], iota_i[:, 1, 0:1])
            nc.vector.tensor_copy(k.iota[:], iota_i[:, 0, :])
            dve.drain()
            ts(k.ident[:], k.iota[:], pcol[:, 0:1], None, ALU.is_equal)
            dve.wait_ge(edges_loaded, 32)
            ts(tb[:], src[:], NODE_BITS, None, ALU.logical_shift_left)
            dve.drain()
            tt(key[:], tb[:], dst[:], ALU.bitwise_or).then_inc(key_ready, 1)
            nc.vector.tensor_copy(near[0][:].bitcast(F32), dst[:]).then_inc(packed_ready, 1)
            pair = view(near[1][:].bitcast(BF16), 0, [[2, COLS]])
            pair_hi = view(near[1][:].bitcast(BF16), 1, [[2, COLS]])
            dve.drain()
            ts(tb[:], src[:], P - 1, None, ALU.bitwise_and)
            ts(ta[:], src[:], 7, None, ALU.logical_shift_right)
            dve.drain()
            nc.vector.tensor_copy(pair, tb[:])
            nc.vector.tensor_copy(pair_hi, ta[:])
            dve.drain().then_inc(packed_ready, 1)
            per_c = HG * P * HH * CB - CB
            per_h = P * HH * CB - HH * CB
            q = k.index
            ts(q[:], tb[:], float(HH * CB), None, ALU.mult)
            dve.drain()
            nc.vector.scalar_tensor_tensor(q[:], ta[:], float(CB), q[:], ALU.mult, ALU.add)
            dve.drain()
            ts(ta[:], ta[:], float(DIV_HH[0]), None, ALU.mult)
            dve.drain()
            ts(ta[:], ta[:], DIV_HH[1], None, ALU.logical_shift_right)
            dve.drain()
            nc.vector.scalar_tensor_tensor(q[:], ta[:], float(per_h), q[:], ALU.mult, ALU.add)
            dve.drain()
            ts(tb[:], dst[:], 7, None, ALU.logical_shift_right)
            dve.drain()
            tt(q[:], q[:], tb[:], ALU.add)
            dve.drain()
            ts(ta[:], tb[:], float(DIV_CB[0]), None, ALU.mult)
            dve.drain()
            ts(ta[:], ta[:], DIV_CB[1], None, ALU.logical_shift_right)
            dve.drain()
            nc.vector.scalar_tensor_tensor(q[:], ta[:], float(per_c), q[:], ALU.mult, ALU.add)
            dve.drain()
            ts(tb[:], dst[:], P - 1, None, ALU.bitwise_and)
            dve.drain()
            ts(q[:], q[:], 7, None, ALU.logical_shift_left)
            dve.drain()
            tt(q[:], q[:], tb[:], ALU.bitwise_or)
            dve.wait_ge(ranges_loaded, 16)
            nc.vector.tensor_reduce(rng[:, 0, :], dst_g[:], AX.X, ALU.min)
            nc.vector.tensor_reduce(rng[:, 1, :], dst_g[:], AX.X, ALU.max)
            dve.drain()
            nc.vector.tensor_copy(rng_i[:], rng[:])
            dve.drain()
            ts(rng_i[:], rng_i[:], 7, None, ALU.logical_shift_right)
            dve.drain()
            ts(rng_i[:, 1, :], rng_i[:, 1, :], 1.0, None, ALU.add).then_inc(rng_ready, 1)
            for n in range(NT + 1):
                b = near[n % 2]
                dve.wait_ge(near_loaded[n % 2], 16 * (n // 2 + 1))
                dve.drain()
                if n < NT:
                    tt(tb[:], key[:], b[:], ALU.bitwise_xor).then_inc(near_used, 1)
                    dve.drain()
                    ts(tb[:], tb[:], DST_MASK, None, ALU.bitwise_and)
                    dve.drain()
                else:
                    ts(ta[:], b[:], DST_MASK, None, ALU.bitwise_and).then_inc(near_used, 1)
                    dve.drain()
                    tt(tb[:], ta[:], dst[:], ALU.subtract)
                    dve.drain()
                nc.vector.tensor_reduce(tests[0:EP, n:n + 1], tb[:], AX.X, ALU.min)
            dve.drain()
            nc.vector.memset(behind, 0.0).then_inc(dst_used, 1)
            ts(tests[0:EP, 0:NT], tests[0:EP, 0:NT], 0.0, None, ALU.is_equal)
            ts(tests[0:EP, NT:NT + 1], tests[0:EP, NT:NT + 1], 0.0, None, ALU.is_lt).then_inc(tests_ready, 1)
            for n in range(NT):
                step = (TESTS + [E])[n + 1] - TESTS[n]
                nc.vector.memset(weights[0:1, n:n + 1], float(step))

            def over_partitions(n, count):
                dve.wait_ge(tests_turned, n)
                nc.vector.tensor_reduce(row[0:count, 16:17], tp[0:count, :], AX.X, ALU.max).then_inc(best_ready, 1)
                dve.wait_ge(best_turned, n)
            dve.drain()
            over_partitions(1, NT + 1)
            tt(row[0:1, 0:NT], tp[0:1, 0:NT], weights[0:1, 0:NT], ALU.mult)
            ts(row[0:1, NT:NT + 1], tp[0:1, NT:NT + 1], float(E), None, ALU.mult)
            dve.drain()
            nc.vector.tensor_reduce(row[0:1, NT + 1:NT + 2], row[0:1, 0:NT], AX.X, ALU.add)
            dve.drain()
            ts(row[0:1, NT + 1:NT + 2], row[0:1, NT + 1:NT + 2], float(TESTS[0]), None, ALU.add)
            dve.drain()
            tt(row[0:1, NT + 1:NT + 2], row[0:1, NT + 1:NT + 2], row[0:1, NT:NT + 1], ALU.max)
            dve.drain()
            nc.vector.tensor_copy(k.ctl[0:1, 0:1], row[0:1, NT + 1:NT + 2]).then_inc(bound_ready, 1)
            dve.drain()
            nc.vector.memset(mult, 1.0)
            dve.wait_ge(bound_ready, 1)
            bound = dve.value_load(k.ctl[0:1, 0:1], min_val=2, max_val=E)
            seen = [(NT + 2) // 2, (NT + 1) // 2]
            with dve.Fori(1, bound + 1) as far:
                for n in range(2):
                    dve.drain()
                    dve.wait_ge(near_loaded[n], (far + seen[n]) * 16)
                    tt(tb[:], key[:], near[n][:], ALU.bitwise_xor).then_inc(near_used, 1)
                    dve.drain()
                    same = behind if n == 0 else mult
                    nc.vector.scalar_tensor_tensor(same, tb[:], 0.0, same, ALU.is_equal, ALU.add)
            dve.drain()
            tt(mult, mult, behind, ALU.add)
            dve.wait_ge(iota_done, 3)
            ts(tb[:], behind, 0.0, -1.0, ALU.is_gt, ALU.mult)
            dve.drain()
            ts(number[:], number[:], SPARE, None, ALU.bitwise_or)
            dve.drain()
            tt(number[:], number[:], tb[:], ALU.bitwise_and)
            dve.drain()
            ts(tb[:], tb[:], -1, None, ALU.bitwise_xor)
            dve.drain()
            tt(q[:], q[:], tb[:], ALU.bitwise_and)
            dve.drain()
            tt(q[:], q[:], number[:], ALU.bitwise_or)
            dve.drain()
            nc.vector.tensor_reduce(tests[0:EP, 0:1], mult, AX.X, ALU.max).then_inc(tests_ready, 1)
            over_partitions(2, 1)
            nc.vector.memset(row[0:1, 0:1], 1.0)
            for d in range(1, DIGITS):
                dve.drain()
                nc.vector.scalar_tensor_tensor(row[0:1, 0:1], tp[0:1, 0:1], float(16 ** d), row[0:1, 0:1], ALU.is_ge, ALU.add)
            dve.drain()
            nc.vector.tensor_copy(k.ctl[0:1, 1:2], row[0:1, 0:1])
            nc.vector.tensor_copy(key[:], mult)
            dve.drain().then_inc(bound_ready, 1)
            dve.wait_ge(bound_ready, 2)
            planes = dve.value_load(k.ctl[0:1, 1:2], min_val=1, max_val=DIGITS)

            def digit(d):
                ts(tb[:], key[:], 4 * d, 15, ALU.logical_shift_right, ALU.bitwise_and)
                dve.drain()
                nc.vector.tensor_copy(k.digit[:, d, :].bitcast(FP8), tb[:], saturate=False)
                dve.drain()
            digit(0)
            for d in range(1, DIGITS):
                with dve.If(planes > d):
                    digit(d)

        @block.tensor
        def _(pe):
            for n, count in ((1, NT + 1), (2, 1)):
                pe.wait_ge(tests_ready, n)
                nc.tensor.matmul(tp[0:count, :], tests[:, 0:count], k.ident[:], start=True, stop=True).then_inc(tests_turned, 1)
                pe.wait_ge(best_ready, n)
                nc.tensor.matmul(tp[0:1, 0:count], row[0:count, 16:17], k.ident[0:count, 0:count], start=True, stop=True).then_inc(best_turned, 1)


class Visits:

    def __init__(self, nc, k, s, psum, name, rows):
        self.nc, self.k, self.name, self.rows = nc, k, name, rows
        self.nodes = k.sb(f"{name}_nodes", [EP, NPAD], F32, s)
        self.onehot = k.sb(f"{name}_onehot", [EP, 2, G, P], F32, s)
        self.total = k.sb(f"{name}_total", [rows, NPAD + P], F32, s)
        self.ps = k.pb(f"{name}_visit_ps", [rows, 2, 512], F32, psum)
        self.onehot_ready = k.sem(f"{name}_onehot_ready")
        self.product_done = k.sem(f"{name}_product_done")
        self.added = k.sem(f"{name}_added")
        self.rows_free = k.sem(f"{name}_rows_free")
        self.zero = k.sb(f"{name}_zero", [1, P], F32, s)
        self.zero_ready = k.sem(f"{name}_zero_ready")

    def start_dve(self, dve):
        nc = self.nc
        nc.vector.memset(self.zero[:], 0.0).then_inc(self.zero_ready, 1)
        nc.vector.memset(self.total[:], 0.0)
        nc.vector.tensor_copy(self.nodes[:, 0:P], self.k.iota[0:EP, :])
        with dve.Fori(1, NB) as b:
            dve.drain()
            nc.vector.tensor_scalar(self.nodes[:, bass.ds(b * P, P)], self.nodes[:, bass.ds(b * P - P, P)],
                                    float(P), None, ALU.add)
        dve.drain().then_inc(self.added, 1)
        self.count = dve.alloc_register(f"{self.name}_visits_dve")
        self.before = dve.alloc_register(f"{self.name}_block_before")
        dve.reg_mov(self.count, 0)
        dve.reg_mov(self.before, NB)

    def start_pe(self, pe):
        pe.wait_ge(self.zero_ready, 1)
        self.nc.tensor.matmul(self.ps[:, 1, 0:P], self.zero[0:1, 0:self.rows], self.zero[0:1, :],
                              start=True, stop=True).then_inc(self.product_done, 1)
        self.count_pe = pe.alloc_register(f"{self.name}_visits_pe")
        pe.reg_mov(self.count_pe, 0)

    def blocks(self, eng, g):
        table = self.k.table
        first = eng.value_load(table[0:1, 0, bass.ds(g, 1)], min_val=0, max_val=NB - 1)
        end = eng.value_load(table[0:1, 1, bass.ds(g, 1)], min_val=1, max_val=NB)
        return first, end

    def add(self, dve, v):
        at = dve.snap(self.before, min_val=0, max_val=NB)
        dve.wait_ge(self.product_done, v + 1)
        dve.wait_ge(self.added, v + 1)
        part = self.total[:, bass.ds(at * P, P)]
        self.nc.vector.tensor_tensor(part, part, view(self.ps[:], ((v + 1) % 2) * 512, [[1, P]]), ALU.add).then_inc(self.added, 1)

    def group_dve(self, dve, g, dst):
        first, end = self.blocks(dve, g)
        with dve.Fori(first, end) as b:
            v = dve.snap(self.count, min_val=0, max_val=NG * NB)
            self.nc.vector.tensor_tensor(view(self.onehot[:], (v % 2) * (G * P), [[P, G], [1, P]]),
                                         view(dst, 0, [[1, G], [0, P]]),
                                         view(self.nodes[:], b * P, [[0, G], [1, P]]),
                                         ALU.is_equal).then_inc(self.onehot_ready, 1)
            self.add(dve, v)
            dve.reg_mov(self.before, b)
            dve.reg_add(self.count, self.count, 1)

    def finish_dve(self, dve):
        self.add(dve, dve.snap(self.count, min_val=0, max_val=NG * NB))

    def group_pe(self, pe, g, rows):
        first, end = self.blocks(pe, g)
        with pe.Fori(first, end):
            v = pe.snap(self.count_pe, min_val=0, max_val=NG * NB)
            pe.wait_ge(self.onehot_ready, v + 1)
            pe.wait_ge(self.added, v + 1)
            for j in range(G):
                mm = self.nc.tensor.matmul(view(self.ps[:], (v % 2) * 512, [[1, P]]), rows(j),
                                           view(self.onehot[:], (v % 2) * (G * P) + j * P, [[1, P]]),
                                           start=(j == 0), stop=(j == G - 1))
            mm.then_inc(self.product_done, 1)
            pe.reg_add(self.count_pe, self.count_pe, 1)
        pe.drain().then_inc(self.rows_free, 1)


def layer_norm(nc, dve, act, k, y, scratch, mean, var, sems, turn):
    squares_ready, root_ready = sems
    per_node = lambda a: view(a[:], 0, [[1, NB], [0, D]])
    if dve is not None:
        nc.vector.tensor_reduce(mean[:], y[:], AX.X, ALU.add)
        dve.drain()
        nc.vector.tensor_scalar(mean[:], mean[:], 1.0 / D, None, ALU.mult)
        dve.drain()
        nc.vector.tensor_tensor(y[:], y[:], per_node(mean), ALU.subtract)
        dve.drain()
        nc.vector.tensor_tensor(scratch[:], y[:], y[:], ALU.mult)
        dve.drain()
        nc.vector.tensor_reduce(var[:], scratch[:], AX.X, ALU.add)
        dve.drain()
        nc.vector.tensor_scalar(var[:], var[:], 1.0 / D, EPS, ALU.mult, ALU.add).then_inc(squares_ready, 1)
        dve.wait_ge(root_ready, turn)
        nc.vector.reciprocal(var[:], var[:])
        dve.drain()
        nc.vector.tensor_tensor(y[:], y[:], per_node(var), ALU.mult)
        dve.drain()
    else:
        act.wait_ge(squares_ready, turn)
        nc.scalar.sqrt(var[:], var[:]).then_inc(root_ready, 1)


def edge_network(nc, k, s):
    sb, pb, sem, io = k.sb, k.pb, k.sem, k.io
    M1 = DH + 1
    xin = [sb(f"e_xin{m}", [EP, G, DI], F32, s) for m in range(2)]
    dst = [sb(f"e_dst{m}", [EP, G], F32, s) for m in range(2)]
    split = [sb(f"e_split{m}", [EP, G, 2], BF16, s) for m in range(2)]
    hist_lo = sb("hist_lo", [EP, G, P], BF16, s)
    hist_hi = sb("hist_hi", [EP, G, NB], BF16, s)
    iota_h = sb("iota_h", [EP, P], BF16, s)
    xt = sb("xt", [DI + 1, 2, GE], F32, s)
    hid = [sb(f"e_hidden{m}", [EP, G, M1], F32, s) for m in range(2)]
    w1a = sb("w1a", [DI + 1, DH], F32, s)
    w1b = sb("w1b", [M1, M1], F32, s)
    count_row = sb("count_row", [M1, DH], F32, s)
    w2x = sb("w2x", [D, DI], F32, s)
    w2g = sb("w2g", [DH, DI], F32, s)
    b2a = sb("b2a", [DI, 1], F32, s)
    w2b = sb("w2b", [DI + 1, D], F32, s)
    stage_i = [sb(f"stage_i{m}", [EP, BATCH], I32, s) for m in range(2)]
    stage_v = [sb(f"stage_v{m}", [EP, BATCH], U8, s) for m in range(2)]

    weights_zero, weights_loaded = sem("e_weights_zero"), sem("e_weights_loaded")
    loaded = [sem(f"e_loaded{m}") for m in range(2)]
    group_read = sem("e_group_read")
    xt_ready, xt_evac, h_ready, h_evac = (sem("e_" + x) for x in ("xt_ready", "xt_evac", "h_ready", "h_evac"))
    hist_ready, hist_done = sem("hist_ready"), sem("hist_done")
    staged = [sem(f"staged{m}") for m in range(2)]
    stored = [sem(f"digits_stored{m}") for m in range(2)]
    cleared, clear_ready = sem("cleared"), sem("clear_ready")
    SUB = [(0, 4), (4, 4), (8, 2)]
    HT = 5
    zeros = sb("e_zeros", [P, CW], U8, s)
    RC = 132
    rel = sb("rel", [EP, RC, 3], F32, s)
    square = sb("rel_square", [EP, RC, 3], F32, s)
    norm = sb("rel_norm", [EP, RC], F32, s)
    unit = sb("rel_unit", [EP, RC, 5], F32, s)
    rel_loaded, unit_stored, unit_ready, norm_ready, root_ready = (sem(x) for x in (
        "rel_loaded", "unit_stored", "unit_ready", "norm_ready", "rel_root_ready"))

    with ExitStack() as q:
        vis = Visits(nc, k, s, q, "e", M1)
        xt_ps = pb("xt_ps", [DI, 3, 512], F32, q)
        h_ps = pb("h_ps", [EP, 2, 512], F32, q)
        hist_ps = pb("hist_ps", [P, NB], F32, q)
        with nc.Block() as block:

            @block.gpsimd
            def _(pool):
                planes = pool.value_load(k.ctl[0:1, 1:2], min_val=1, max_val=DIGITS)
                pool.wait_ge(clear_ready, 1)
                batches = COLS // BATCH

                def store_plane(d):
                    def batch(i, m, first):
                        if not first:
                            await_alone(pool, k.passed_pool, stored[m], pool.snap(issued[m], min_val=16 * BATCH, max_val=1 << 24))
                        at = (i * 2 + m) * BATCH
                        nc.gpsimd.tensor_copy(stage_i[m][:], k.index[:, bass.ds(at, BATCH)]).then_inc(staged[m], 1)
                        nc.gpsimd.tensor_copy(stage_v[m][:], k.digit[:, d, bass.ds(at, BATCH)]).then_inc(staged[m], 1)
                        pool.reg_add(turns[m], turns[m], 2)
                        await_alone(pool, k.passed_pool, staged[m], pool.snap(turns[m], min_val=2, max_val=1 << 24))
                        for j in range(BATCH):
                            pool.indirect_dma_start(k.planes[d], bass.IndirectOffsetOnAxis(stage_i[m][:, j:j + 1], 0),
                                                    stage_v[m][:, j:j + 1], None).then_inc(stored[m], 16)
                        pool.reg_add(issued[m], issued[m], 16 * BATCH)
                    for m in range(2):
                        batch(0, m, d == 0)
                    with pool.Fori(1, batches // 2) as i:
                        for m in range(2):
                            batch(i, m, False)

                issued = [pool.alloc_register(f"issued{m}") for m in range(2)]
                turns = [pool.alloc_register(f"turns{m}") for m in range(2)]
                for r in issued + turns:
                    pool.reg_mov(r, 0)
                store_plane(0)
                for d in range(1, DIGITS):
                    with pool.If(planes > d):
                        with pool.Fori(0, NCH * HG * HH) as u:
                            part = k.planes[d][0:PLANE, :].rearrange("(u p n) o -> u p (n o)", p=P, n=CW)[bass.ds(u, 1), :, :]
                            pool.dma_start(part.rearrange("a p n -> (a p) n"), zeros[:]).then_inc(cleared, 16)
                        pool.wait_ge(cleared, NCH * HG * HH * 16 * d)
                        store_plane(d)
                for m in range(2):
                    await_alone(pool, k.passed_pool, stored[m], pool.snap(issued[m], min_val=16 * BATCH, max_val=1 << 24))

            @block.sync
            def _(sp):
                sp.wait_ge(weights_zero, 1)
                w = [(w1a[0:DI, :], io["L0_gnn_w1a"]), (w1a[DI:DI + 1, :], io["L0_gnn_b1a"].rearrange("(o n) -> o n", o=1)),
                     (w1b[0:DH, 0:DH], io["L0_gnn_w1b"]), (w1b[DH:M1, 0:DH], io["L0_gnn_b1b"].rearrange("(o n) -> o n", o=1)),
                     (w2x[:], io["L0_gnn_w2a"][0:D, :]), (w2g[:], io["L0_gnn_w2a"][D:D + DH, :]),
                     (b2a[:], io["L0_gnn_b2a"].rearrange("(n o) -> n o", o=1)),
                     (w2b[0:DI, :], io["L0_gnn_w2b"]), (w2b[DI:DI + 1, :], io["L0_gnn_b2b"].rearrange("(o n) -> o n", o=1))]
                for to, frm in w:
                    sp.dma_start(to, frm).then_inc(weights_loaded, 16)

                def columns(a, c, width):
                    return a.rearrange("(p e) f -> p (e f)", p=EP)[:, bass.ds(c * (RC * width), RC * width)]
                sp.dma_start(view(rel[:], 0, [[1, RC * 3]]), columns(io["edge_attr_3"], 0, 3)).then_inc(rel_loaded, 16)
                with sp.Fori(1, COLS // RC) as c:
                    sp.wait_ge(unit_ready, c)
                    sp.dma_start(columns(k.dir_d, c - 1, 5), view(unit[:], 0, [[1, RC * 5]])).then_inc(unit_stored, 16)
                    sp.dma_start(view(rel[:], 0, [[1, RC * 3]]), columns(io["edge_attr_3"], c, 3)).then_inc(rel_loaded, 16)
                sp.wait_ge(unit_ready, COLS // RC)
                sp.dma_start(columns(k.dir_d, COLS // RC - 1, 5), view(unit[:], 0, [[1, RC * 5]])).then_inc(unit_stored, 16)

                def load(i, m, first):
                    g = i * 2 + m
                    if not first:
                        sp.wait_ge(group_read, g - 1)
                        sp.wait_ge(xt_ready, g * 3 - 3)
                    def part(a):
                        return a[bass.ds(g, 1), :, :].rearrange("a p c -> (a p) c")
                    sp.dma_start(view(xin[m][:], 0, [[1, G * DI]]), part(k.xin_d)).then_inc(loaded[m], 16)
                    sp.dma_start(dst[m][:], part(k.dst_d.rearrange("(g p c) -> g p c", p=EP, c=G))).then_inc(loaded[m], 16)
                    sp.dma_start(view(split[m][:], 0, [[1, 2 * G]]),
                                 part(k.hist_d.rearrange("(g p c) t -> g p (c t)", p=EP, c=G))).then_inc(loaded[m], 16)
                for m in range(2):
                    load(0, m, True)
                with sp.Fori(1, PAIRS) as i:
                    for m in range(2):
                        load(i, m, False)
                sp.wait_ge(unit_stored, COLS // RC * 16)

            @block.tensor
            def _(pe):
                def group(i, m, first):
                    n = i * 2 + m
                    pe.wait_ge(loaded[m], (i + 1) * 48)
                    for b, (t0, tn) in enumerate(SUB):
                        if not first:
                            await_alone(pe, k.passed_pe, xt_evac, n * 3 + (b - 2))
                        for t in range(t0, t0 + tn):
                            mm = nc.tensor.transpose(xt_ps[:, b, (t - t0) * EP:(t - t0 + 1) * EP], xin[m][:, t, :],
                                                     k.ident[0:EP, 0:EP])
                        mm.then_inc(xt_ready, 1)
                    for b in range(2):
                        pe.wait_ge(xt_evac, n * 3 + (2 + b))
                        if not first:
                            pe.wait_ge(h_evac, n * 2 + (b - 1))
                        for t in range(HT):
                            mm = nc.tensor.matmul(h_ps[:, b, t * DH:(t + 1) * DH],
                                                  xt[:, m, (b * HT + t) * EP:(b * HT + t + 1) * EP], w1a[:],
                                                  start=True, stop=True)
                        mm.then_inc(h_ready, 1)
                    if not first:
                        pe.wait_ge(h_evac, n * 2)
                        vis.group_pe(pe, n - 1, lambda j: hid[1 - m][:, j, :])
                    pe.wait_ge(hist_ready, n + 1)
                    for j in range(G):
                        mm = nc.tensor.matmul(hist_ps[:], hist_lo[:, j, :], hist_hi[:, j, :], start=False,
                                              stop=False, skip_group_check=True)
                    mm.then_inc(hist_done, 1)

                pe.wait_ge(weights_loaded, 16 * 9)
                vis.start_pe(pe)
                nc.tensor.matmul(hist_ps[:], vis.zero[0:1, :], vis.zero[0:1, 0:NB], start=True, stop=False,
                                 skip_group_check=True)
                group(0, 0, True)
                group(0, 1, False)
                with pe.Fori(1, PAIRS) as i:
                    for m in range(2):
                        group(i, m, False)
                pe.wait_ge(h_evac, 2 * NG)
                vis.group_pe(pe, NG - 1, lambda j: hid[1][:, j, :])

            @block.scalar
            def _(act):
                with act.Fori(0, COLS // RC) as c:
                    act.wait_ge(norm_ready, c + 1)
                    nc.scalar.sqrt(norm[:], norm[:]).then_inc(root_ready, 1)
                act.wait_ge(weights_zero, 1)

                def group(i, m, first):
                    n = i * 2 + m
                    for b, (t0, tn) in enumerate(SUB):
                        act.wait_ge(xt_ready, n * 3 + (b + 1))
                        nc.scalar.copy(xt[0:DI, m, t0 * EP:(t0 + tn) * EP], xt_ps[:, b, 0:tn * EP]).then_inc(xt_evac, 1)
                    for b in range(2):
                        act.wait_ge(h_ready, n * 2 + (b + 1))
                        if not first and b == 0:
                            act.wait_ge(vis.rows_free, n - 1)
                        nc.scalar.activation(hid[m][:, b * HT:(b + 1) * HT, 0:DH],
                                             view(h_ps[:], b * 512, [[DH, HT], [1, DH]]), ACT.Relu).then_inc(h_evac, 1)
                for m in range(2):
                    group(0, m, True)
                with act.Fori(1, PAIRS) as i:
                    for m in range(2):
                        group(i, m, False)

            @block.vector
            def _(dve):
                tt = nc.vector.tensor_tensor
                nc.vector.memset(zeros[:].bitcast(I32), 0).then_inc(clear_ready, 1)
                for a in (w1b, count_row):
                    nc.vector.memset(a[:], 0.0)
                for a in (xt, w2b, *hid):
                    nc.vector.memset(a[:], 1.0)
                dve.drain()
                nc.vector.memset(w1b[DH:M1, DH:M1], 1.0)
                nc.vector.memset(count_row[DH:M1, :], 1.0)
                nc.vector.tensor_copy(iota_h[:], k.iota[0:EP, :])
                dve.drain().then_inc(weights_zero, 1)
                vis.start_dve(dve)

                def directions(c, first):
                    dve.wait_ge(rel_loaded, (c + 1) * 16)
                    tt(square[:], rel[:], rel[:], ALU.mult)
                    dve.drain()
                    nc.vector.tensor_reduce(norm[:], square[:], AX.X, ALU.add).then_inc(norm_ready, 1)
                    dve.wait_ge(root_ready, c + 1)
                    nc.vector.reciprocal(norm[:], norm[:])
                    dve.drain()
                    if not first:
                        dve.wait_ge(unit_stored, c * 16)
                    for to, frm, n in ((0, 1, 2), (2, 0, 1), (3, 1, 2)):
                        tt(unit[:, :, to:to + n], rel[:, :, frm:frm + n], view(norm[:], 0, [[1, RC], [0, n]]), ALU.mult)
                    dve.drain().then_inc(unit_ready, 1)
                directions(0, True)
                with dve.Fori(1, COLS // RC) as c:
                    directions(c, False)

                def group(i, m, first):
                    n = i * 2 + m
                    dve.wait_ge(loaded[m], (i + 1) * 48)
                    if not first:
                        dve.wait_ge(hist_done, n)
                    tt(hist_lo[:], view(split[m][:], 0, [[2, G], [0, P]]), view(iota_h[:], 0, [[0, G], [1, P]]), ALU.is_equal)
                    tt(hist_hi[:], view(split[m][:], 1, [[2, G], [0, NB]]), view(iota_h[:], 0, [[0, G], [1, NB]]),
                       ALU.is_equal).then_inc(hist_ready, 1)
                    vis.group_dve(dve, n, dst[m][:])
                    dve.drain().then_inc(group_read, 1)
                group(0, 0, True)
                group(0, 1, False)
                with dve.Fori(1, PAIRS) as i:
                    for m in range(2):
                        group(i, m, False)
                vis.finish_dve(dve)
                dve.wait_ge(hist_done, NG)
                nc.vector.tensor_copy(view(k.small[:], 1, [[2, NB]]), hist_ps[:])
    node_network(nc, k, vis, w1b, count_row, w2x, w2g, b2a, w2b, s)


HALVES = [(0, 4 * P), (4 * P, CW - 4 * P)]


def node_network(nc, k, vis, w1b, count_row, w2x, w2g, b2a, w2b, s):
    sb, pb, sem = k.sb, k.pb, k.sem
    M1 = DH + 1
    stage = sb("x_stage", [P, CB, D], F32, s)
    x_t = sb("x_t", [D, CW], F32, s)
    agg = sb("agg_t", [M1, CW], F32, s)
    inv = sb("inv_count", [DH, CW], F32, s)
    h2 = sb("h2", [DI + 1, CW], F32, s)
    names = ("staged", "turned", "turned_copied", "sums", "sums_copied", "counts", "mean", "h2", "h2_copied", "out", "taken")
    (staged, turned, turned_copied, sums_ready, sums_copied, counts_ready, mean_ready, h2_ready, h2_copied,
     out_ready, taken) = (sem("n_" + x) for x in names)
    ones_ready = sem("n_ones_ready")
    with ExitStack() as q:
        x_ps = pb("n_x_ps", [D, 2, 512], F32, q)
        a_ps = pb("n_a_ps", [M1, 2, 512], F32, q)
        c_ps = pb("n_c_ps", [DH, 2, 512], F32, q)
        o_ps = pb("n_o_ps", [P, 512], F32, q)
        with nc.Block() as block:

            @block.tensor
            def _(pe):
                def chunk(c, first):
                    await_alone(pe, k.passed_pe, staged, c + 1)
                    for j in range(CB):
                        mm = nc.tensor.transpose(x_ps[:, j // 4, (j % 4) * P:(j % 4 + 1) * P], stage[:, j, :], k.ident[:])
                    mm.then_inc(turned, 1)
                    for b, (at, n) in enumerate(HALVES):
                        mm = nc.tensor.matmul(a_ps[:, b, 0:n], w1b[:], vis.total[:, bass.ds(c * CW + at, n)], start=True, stop=True)
                    mm.then_inc(sums_ready, 1)
                    pe.wait_ge(sums_copied, c + 1)
                    for b, (at, n) in enumerate(HALVES):
                        mm = nc.tensor.matmul(c_ps[:, b, 0:n], count_row[:], agg[:, at:at + n], start=True, stop=True)
                    mm.then_inc(counts_ready, 1)
                    if not first:
                        pe.wait_ge(taken, c)
                    for j in range(CB):
                        mm = nc.tensor.matmul(o_ps[:, CB * D + j:CB * D + j + 1], agg[:, j * P:(j + 1) * P],
                                              k.ident[0:M1, DH:M1], start=True, stop=True)
                    mm.then_inc(counts_ready, 1)
                    pe.wait_ge(mean_ready, c + 1)
                    pe.wait_ge(turned_copied, c + 1)
                    for b, (at, n) in enumerate(HALVES):
                        nc.tensor.matmul(a_ps[0:DI, b, 0:n], w2g[:], agg[0:DH, at:at + n], start=True, stop=False)
                        mm = nc.tensor.matmul(a_ps[0:DI, b, 0:n], w2x[:], x_t[:, at:at + n], start=False, stop=True)
                    mm.then_inc(h2_ready, 1)
                    pe.wait_ge(h2_copied, c + 1)
                    for j in range(CB):
                        mm = nc.tensor.matmul(o_ps[:, j * D:(j + 1) * D], h2[:, j * P:(j + 1) * P], w2b[:], start=True, stop=True)
                    mm.then_inc(out_ready, 1)
                chunk(0, True)
                with pe.Fori(1, NCH) as c:
                    chunk(c, False)

            @block.scalar
            def _(act):
                act.wait_ge(ones_ready, 1)
                def chunk(c, first):
                    if not first:
                        act.wait_ge(taken, c)
                    nc.scalar.copy(stage[:], k.x[:, bass.ds(c * CB, CB), :]).then_inc(staged, 1)
                    act.wait_ge(turned, c + 1)
                    for b, (at, n) in enumerate(HALVES):
                        cp = nc.scalar.copy(x_t[:, at:at + n], x_ps[:, b, 0:n])
                    cp.then_inc(turned_copied, 1)
                    act.wait_ge(sums_ready, c + 1)
                    for b, (at, n) in enumerate(HALVES):
                        cp = nc.scalar.copy(agg[:, at:at + n], a_ps[:, b, 0:n])
                    cp.then_inc(sums_copied, 1)
                    act.wait_ge(h2_ready, c + 1)
                    for b, (at, n) in enumerate(HALVES):
                        cp = nc.scalar.activation(h2[0:DI, at:at + n], a_ps[0:DI, b, 0:n], ACT.Relu, bias=b2a[:, 0:1])
                    cp.then_inc(h2_copied, 1)
                chunk(0, True)
                with act.Fori(1, NCH) as c:
                    chunk(c, False)

            @block.vector
            def _(dve):
                nc.vector.memset(h2[:], 1.0).then_inc(ones_ready, 1)
                with dve.Fori(0, NCH) as c:
                    dve.wait_ge(counts_ready, c * 2 + 2)
                    for b, (at, n) in enumerate(HALVES):
                        nc.vector.tensor_scalar(inv[:, at:at + n], c_ps[:, b, 0:n], 1.0, None, ALU.max)
                    dve.drain()
                    nc.vector.reciprocal(inv[:], inv[:])
                    dve.drain()
                    nc.vector.tensor_tensor(agg[0:DH, :], agg[0:DH, :], inv[:], ALU.mult).then_inc(mean_ready, 1)
                    dve.wait_ge(out_ready, c + 1)
                    part = k.x[:, bass.ds(c * CB, CB), :]
                    nc.vector.tensor_copy(view(k.small[:], c * (2 * CB), [[2, CB]]), o_ps[:, CB * D:CB * D + CB])
                    nc.vector.tensor_tensor(part, part, view(o_ps[:], 0, [[D, CB], [1, D]]), ALU.add)
                    dve.drain().then_inc(taken, 1)


def propagate(nc, k, s):
    sb, pb, sem = k.sb, k.pb, k.sem
    passes = STEPS + 1
    slots = [sb(f"a_slot{h}", [P, HH, CW], U8, s) for h in range(HG)]
    parts = sb("f_parts", [P, NB, 3 * D], BF16, s)
    agg = sb("agg", [P, NB, D], F32, s)
    f = sb("f", [P, NB, D], F32, s)
    tenth = sb("x_tenth", [P, NB, D], F32, s)
    norms = sb("norms", [P, NB, 2], F32, s)
    mean, var = sb("mean", [P, NB], F32, s), sb("var", [P, NB], F32, s)
    turned = sb("turned", [3 * D, 2, CW], F32, s)
    select = sb("select", [3 * D, DIGITS * D], F32, s)
    a_loaded = [sem(f"a_loaded{h}") for h in range(HG)]
    a_used = sem("a_used")
    parts_ready = sem("parts_ready")
    product_ready, product_copied = sem("p_product_ready"), sem("p_product_copied")
    summed, taken = sem("p_summed"), sem("p_taken")
    norm_in, norm_out = sem("ln_in"), sem("ln_out")
    x_ready, x_stored = sem("p_x_ready"), sem("p_x_stored")

    with ExitStack() as q:
        prod = [pb(f"p_prod{m}", [3 * D, 2, 512], F32, q) for m in range(2)]
        back = [pb(f"p_back{m}", [P, CB * D], F32, q) for m in range(2)]
        with nc.Block() as block:

            def each_chunk(eng, u, planes, body):
                with eng.Fori(0, planes) as d:
                    with eng.Fori(0, NCH // 2) as c2:
                        n = eng.snap(u, min_val=0, max_val=passes * DIGITS * NCH)
                        body(n, d, c2)
                        eng.reg_add(u, u, 1)

            @block.sync
            def _(sp):
                planes = sp.value_load(k.ctl[0:1, 1:2], min_val=1, max_val=DIGITS)
                u = sp.alloc_register("pairs_sp")
                sp.reg_mov(u, 0)

                def load_plane(d):
                    with sp.Fori(0, NCH // 2) as c2:
                        n = sp.snap(u, min_val=0, max_val=passes * DIGITS * NCH)
                        for m in range(2):
                            for h in range(HG):
                                sp.wait_ge(a_used, n * (2 * HG) + (HG * m + h + 1))
                                sp.dma_start(view(slots[h][:], 0, [[1, HH * CW]]),
                                             plane_part(k.planes[d], c2 * (2 * HG) + (m * HG + h))).then_inc(a_loaded[h], 16)
                        sp.reg_add(u, u, 1)
                with sp.Fori(0, passes):
                    load_plane(0)
                    for d in range(1, DIGITS):
                        with sp.If(planes > d):
                            load_plane(d)
                sp.wait_ge(x_ready, 1)
                sp.dma_start(k.x3_d.rearrange("(b p) f -> p b f", p=P), k.x[:]).then_inc(x_stored, 16)
                sp.wait_ge(x_stored, 16)

            @block.tensor
            def _(pe):
                planes = pe.value_load(k.ctl[0:1, 1:2], min_val=1, max_val=DIGITS)
                u = pe.alloc_register("pairs_pe")
                pe.reg_mov(u, 0)
                pe.sem_inc(a_used, HG)
                pe.sem_inc(summed, 2)

                def body(n, d, c2):
                    for m in range(2):
                        pe.wait_ge(product_copied, n * 2 + (m + 1))
                        for h in range(HG):
                            await_alone(pe, k.passed_pe, a_loaded[h], n * 32 + 16 * (m + 1))
                            for j in range(HH):
                                for w in range(2):
                                    mm = nc.tensor.matmul(prod[m][:, w, 0:HW], parts[:, h * HH + j, :],
                                                          slots[h][:, j, w * HW:(w + 1) * HW].bitcast(FP8),
                                                          start=(h == 0 and j == 0), stop=(h == HG - 1 and j == HH - 1))
                            mm.then_inc(a_used, 1)
                        pe.drain().then_inc(product_ready, 1)
                    for m in range(2):
                        pe.wait_ge(product_copied, n * 2 + (m + 3))
                        pe.wait_ge(taken, n * 2 + (m + 1))
                        for j in range(CB):
                            mm = nc.tensor.matmul(back[m][:, j * D:(j + 1) * D], turned[:, m, j * P:(j + 1) * P],
                                                  select[:, bass.ds(d * D, D)], start=True, stop=True)
                        mm.then_inc(summed, 1)
                with pe.Fori(0, passes) as p:
                    await_alone(pe, k.passed_pe, parts_ready, p + 1)
                    each_chunk(pe, u, planes, body)

            @block.scalar
            def _(act):
                planes = act.value_load(k.ctl[0:1, 1:2], min_val=1, max_val=DIGITS)
                u = act.alloc_register("pairs_act")
                act.reg_mov(u, 0)
                act.sem_inc(product_copied, 2)
                layer_norm(nc, None, act, k, k.x, None, mean, var, (norm_in, norm_out), 1)
                act.wait_ge(norm_in, 2)
                nc.scalar.sqrt(norms[:], norms[:]).then_inc(norm_out, 1)

                def body(n, d, c2):
                    for m in range(2):
                        act.wait_ge(product_ready, n * 2 + (m + 1))
                        act.wait_ge(summed, n * 2 + (m + 1))
                        nc.scalar.copy(view(turned[:], m * CW, [[HW, 2], [1, HW]]),
                                       view(prod[m][:], 0, [[512, 2], [1, HW]])).then_inc(product_copied, 1)
                with act.Fori(0, STEPS):
                    each_chunk(act, u, planes, body)
                layer_norm(nc, None, act, k, k.x, None, mean, var, (norm_in, norm_out), 3)
                each_chunk(act, u, planes, body)
                layer_norm(nc, None, act, k, k.x, None, mean, var, (norm_in, norm_out), 4)

            @block.vector
            def _(dve):
                tt, ts = nc.vector.tensor_tensor, nc.vector.tensor_scalar
                planes = dve.value_load(k.ctl[0:1, 1:2], min_val=1, max_val=DIGITS)
                u = dve.alloc_register("pairs_dve")
                dve.reg_mov(u, 0)
                dve.sem_inc(taken, 2)
                for r in range(3):
                    for d in range(DIGITS):
                        ts(select[r * D:(r + 1) * D, d * D:(d + 1) * D], k.ident[r * D:(r + 1) * D, r * D:(r + 1) * D],
                           float(16 ** d), None, ALU.mult)
                norm = lambda turn: layer_norm(nc, dve, None, k, k.x, f, mean, var, (norm_in, norm_out), turn)
                of_src = view(norms[:], 1, [[2, NB], [0, D]])
                of_dst = view(norms[:], 0, [[2, NB], [0, D]])

                def split():
                    dve.drain()
                    for r in range(3):
                        nc.vector.tensor_copy(parts[:, :, r * D:(r + 1) * D], f[:])
                        if r < 2:
                            dve.drain()
                            tt(f[:], f[:], parts[:, :, r * D:(r + 1) * D], ALU.subtract)
                            dve.drain()
                    nc.vector.memset(agg[:], 0.0)
                    dve.drain().then_inc(parts_ready, 1)

                def body(n, d, c2):
                    for m in range(2):
                        dve.wait_ge(summed, n * 2 + (m + 3))
                        part = view(agg[:], c2 * (2 * CB * D) + m * CB * D, [[1, CB * D]])
                        tt(part, part, back[m][:], ALU.add).then_inc(taken, 1)

                norm(1)
                ts(norms[:], k.small[:], 1.0, None, ALU.max).then_inc(norm_in, 1)
                dve.wait_ge(norm_out, 2)
                nc.vector.reciprocal(norms[:], norms[:])
                ts(tenth[:], k.x[:], ALPHA, None, ALU.mult)
                dve.drain()
                tt(f[:], k.x[:], of_src, ALU.mult)
                split()

                def new_f():
                    dve.drain()
                    tt(agg[:], agg[:], of_dst, ALU.mult)
                    dve.drain()
                    nc.vector.scalar_tensor_tensor(f[:], agg[:], 1.0 - ALPHA, tenth[:], ALU.mult, ALU.add)
                    dve.drain()
                with dve.Fori(0, STEPS - 1):
                    each_chunk(dve, u, planes, body)
                    new_f()
                    tt(f[:], f[:], of_src, ALU.mult)
                    split()
                each_chunk(dve, u, planes, body)
                new_f()
                tt(k.x[:], k.x[:], f[:], ALU.add)
                dve.drain()
                norm(3)
                nc.vector.tensor_copy(f[:], k.x[:])
                split()
                each_chunk(dve, u, planes, body)
                dve.drain()
                tt(k.x[:], k.x[:], agg[:], ALU.add)
                dve.drain()
                norm(4)
                dve.drain().then_inc(x_ready, 1)


def tensor_messages(nc, k, s):
    sb, pb, sem, io = k.sb, k.pb, k.sem, k.io
    U = 8
    y0, c1, c2 = 0.5 / math.sqrt(math.pi), math.sqrt(3 / (4 * math.pi)), 0.5 * math.sqrt(15 / math.pi)
    norm0 = math.sqrt(4 * math.pi) / math.sqrt(2 * U)
    norm1 = math.sqrt(4 * math.pi) * math.sqrt(3) / math.sqrt(4 * U)
    RD = 6 * U * U
    raw = sb("raw_w2", [HID + 1, RD], F32, s)
    w2 = sb("radial_w2", [HID + 1, RD], F32, s)
    w1 = sb("radial_w1", [HID, 2], F32, s)
    edge_w = [sb(f"edge_w{m}", [HID, GE], F32, s) for m in range(2)]
    hid = [sb(f"radial_hidden{m}", [HID + 1, G, EP], F32, s) for m in range(2)]
    idx = [sb(f"m_idx{m}", [EP, G], I32, s) for m in range(2)]
    src = [sb(f"m_src{m}", [EP, G, D], F32, s) for m in range(2)]
    dst = [sb(f"m_dst{m}", [EP, G], F32, s) for m in range(2)]
    unit = [sb(f"m_unit{m}", [EP, G, 5], F32, s) for m in range(2)]
    fs = sb("f0_s", [EP, G, 2 * U], F32, s)
    small = sb("m_small", [EP, G, 3 * U], F32, s)
    pa = sb("products_a", [EP, G, 2 * U, 2 * U], F32, s)
    pbb = sb("products_b", [EP, G, 2 * U, 3 * U], F32, s)
    qa = sb("sums_a", [EP, G, 2 * U], F32, s)
    qb = sb("sums_b", [EP, G, U, 3], F32, s)
    q1 = sb("sums_1", [EP, G, U, 5], F32, s)
    msg = [sb(f"message{m}", [EP, G, 4 * U], F32, s) for m in range(2)]
    stage = sb("m_stage", [D, CW], F32, s)
    scratch = sb("m_scratch", [P, NB, D], F32, s)
    mean, var = sb("m_mean", [P, NB], F32, s), sb("m_var", [P, NB], F32, s)

    w_loaded, w_ready = sem("m_w_loaded"), sem("m_w_ready")
    loaded = [sem(f"m_loaded{m}") for m in range(2)]
    idx_loaded = [sem(f"m_idx_loaded{m}") for m in range(2)]
    gathered = [sem(f"m_gathered{m}") for m in range(2)]
    hid_ready, r_ready, r_used = sem("m_hid_ready"), sem("m_r_ready"), sem("m_r_used")
    msg_ready, features_used, group_read = sem("m_msg_ready"), sem("m_features_used"), sem("m_group_read")
    staged, turned_s, taken = sem("m_staged"), sem("m_turned"), sem("m_taken")
    norm_in, norm_out = sem("m_ln_in"), sem("m_ln_out")
    out_ready, out_stored = sem("m_out_ready"), sem("m_out_stored")
    RB = 2
    NBAT = G // RB

    with ExitStack() as q:
        vis = Visits(nc, k, s, q, "m", D)
        r_ps = pb("radial_ps", [EP, 2, RB, 512], F32, q)
        o_ps = pb("m_out_ps", [P, CB * D], F32, q)
        with nc.Block() as block:

            @block.gpsimd
            def _(pool):
                def gather(i, m, first):
                    await_alone(pool, k.passed_pool, idx_loaded[m], (i + 1) * 16)
                    if not first:
                        await_alone(pool, k.passed_pool, features_used, i * 2 + (m - 1))
                    for j in range(G):
                        pool.indirect_dma_start(src[m][:, j, :], None, k.x3_d,
                                                bass.IndirectOffsetOnAxis(idx[m][:, j:j + 1], 0)).then_inc(gathered[m], 16)
                for m in range(2):
                    gather(0, m, True)
                with pool.Fori(1, PAIRS) as i:
                    for m in range(2):
                        gather(i, m, False)

            @block.sync
            def _(sp):
                sp.dma_start(raw[0:HID, :], io["L3_gnn_w2"]).then_inc(w_loaded, 16)
                sp.dma_start(raw[HID:HID + 1, :], io["L3_gnn_b2"].rearrange("(o n) -> o n", o=1)).then_inc(w_loaded, 16)
                sp.dma_start(w1[:, 0:1], io["L3_gnn_w1"].rearrange("o n -> n o")).then_inc(w_loaded, 16)
                sp.dma_start(w1[:, 1:2], io["L3_gnn_b1"].rearrange("(n o) -> n o", o=1)).then_inc(w_loaded, 16)

                def load(i, m, first):
                    g = i * 2 + m
                    if not first:
                        sp.wait_ge(gathered[m], i * (16 * G))
                    sp.dma_start(idx[m][:], k.idx_view[bass.ds(g, 1), :, :].rearrange("a p j -> (a p) j")).then_inc(idx_loaded[m], 16)
                    if not first:
                        sp.wait_ge(group_read, g - 1)
                        sp.wait_ge(hid_ready, g - 1)
                    part = lambda a: a[bass.ds(g, 1), :, :].rearrange("a p c -> (a p) c")
                    sp.dma_start(edge_w[m][:], bass.AP(io["edge_weight"].tensor, g * GE, [[0, HID], [1, GE]])).then_inc(loaded[m], 16)
                    sp.dma_start(dst[m][:], part(k.dst_d.rearrange("(g p c) -> g p c", p=EP, c=G))).then_inc(loaded[m], 16)
                    sp.dma_start(view(unit[m][:], 0, [[1, 5 * G]]),
                                 part(k.dir_d.rearrange("(g p c) t -> g p (c t)", p=EP, c=G))).then_inc(loaded[m], 16)
                for m in range(2):
                    load(0, m, True)
                with sp.Fori(1, PAIRS) as i:
                    for m in range(2):
                        load(i, m, False)
                sp.wait_ge(out_ready, 1)
                full = (NB - 1) * P
                sp.dma_start(k.out[0:full, :].rearrange("(b p) f -> p b f", p=P), k.x[:, 0:NB - 1, :]).then_inc(out_stored, 16)
                sp.dma_start(k.out[full:N, :], k.x[0:LAST, NB - 1, :]).then_inc(out_stored, 16)
                sp.wait_ge(out_stored, 32)

            @block.scalar
            def _(act):
                act.wait_ge(w_loaded, 64)
                act.wait_ge(w_ready, 1)

                def group(i, m, first):
                    n = i * 2 + m
                    act.wait_ge(loaded[m], (i + 1) * 48)
                    if not first:
                        act.wait_ge(r_ready, n * NBAT - NBAT)
                    nc.scalar.activation(hid[m][0:HID, :, :], view(edge_w[m][:], 0, [[1, G], [G, EP]]), ACT.Relu,
                                         bias=w1[:, 1:2], scale=w1[:, 0:1]).then_inc(hid_ready, 1)
                for m in range(2):
                    group(0, m, True)
                with act.Fori(1, PAIRS) as i:
                    for m in range(2):
                        group(i, m, False)
                act.wait_ge(msg_ready, NG + 1)
                with act.Fori(0, NCH) as c:
                    act.wait_ge(taken, c + 1)
                    nc.scalar.copy(stage[:], vis.total[:, bass.ds(c * CW, CW)]).then_inc(staged, 1)
                layer_norm(nc, None, act, k, k.x, None, mean, var, (norm_in, norm_out), 1)

            @block.tensor
            def _(pe):
                pe.wait_ge(w_ready, 2)
                vis.start_pe(pe)

                def radial(n, m, batches, first):
                    pe.wait_ge(hid_ready, n + 1)
                    for b in batches:
                        half = (m * NBAT + b) % 2
                        if not (first and b < 2):
                            pe.wait_ge(r_used, n * NBAT + (b - 1))
                        for t in range(RB):
                            mm = nc.tensor.matmul(r_ps[:, half, t, 0:RD], hid[m][:, b * RB + t, :], w2[:], start=True, stop=True)
                        mm.then_inc(r_ready, 1)

                def sums(n, m):
                    pe.wait_ge(msg_ready, n + 1)
                    vis.group_pe(pe, n, lambda j: msg[m][:, j, :])
                radial(0, 0, range(NBAT), True)

                def group(n, m):
                    radial(n, m, range(2), False)
                    sums(n - 1, 1 - m)
                    radial(n, m, range(2, NBAT), False)
                group(1, 1)
                with pe.Fori(1, PAIRS) as i:
                    for m in range(2):
                        group(i * 2 + m, m)
                sums(NG - 1, 1)
                with pe.Fori(0, NCH) as c:
                    await_alone(pe, k.passed_pe, staged, c + 1)
                    for j in range(CB):
                        mm = nc.tensor.transpose(o_ps[:, j * D:(j + 1) * D], stage[:, j * P:(j + 1) * P], k.ident[0:D, 0:D])
                    mm.then_inc(turned_s, 1)

            @block.vector
            def _(dve):
                tt, ts, red = nc.vector.tensor_tensor, nc.vector.tensor_scalar, nc.vector.tensor_reduce
                for a in hid:
                    nc.vector.memset(a[:], 1.0)
                dve.drain().then_inc(w_ready, 1)
                dve.wait_ge(w_loaded, 64)
                s1 = norm1 * c1 / math.sqrt(3)
                k2 = norm1 * c2 / math.sqrt(10)
                uv = lambda at, step: view(raw[:], at, [[step * U, U], [step, U]])
                for block_at, frm, scale in ((0, uv(0, 1), norm0 * y0), (U, uv(U * U, 1), norm0 * c1 / math.sqrt(3)),
                                             (2 * U * U, uv(2 * U * U, 1), s1), (2 * U * U + U, uv(3 * U * U + 2, 3), k2)):
                    ts(view(w2[:], block_at, [[2 * U, U], [1, U]]), frm, scale, None, ALU.mult)
                for part, scale in ((0, norm1 * y0 / math.sqrt(3)), (1, norm1 * c1 / math.sqrt(6))):
                    ts(view(w2[:], 4 * U * U + part * U * U, [[U, U], [1, U]]), uv(3 * U * U + part, 3), scale, None, ALU.mult)
                dve.drain()
                r0 = view(w2[:], 4 * U * U, [[U, U], [1, U]])
                nc.vector.scalar_tensor_tensor(r0, uv(3 * U * U + 2, 3), -k2 / 3, r0, ALU.mult, ALU.add)
                vis.start_dve(dve)
                dve.drain().then_inc(w_ready, 1)

                def group(i, m, first):
                    n = i * 2 + m
                    dve.drain()
                    dve.wait_ge(loaded[m], (i + 1) * 48)
                    dve.wait_ge(gathered[m], (i + 1) * (16 * G))
                    f1 = view(src[m][:], U, [[D, G], [3, U], [1, 3]])
                    r_o = lambda at: view(unit[m][:], at, [[5, G], [0, U], [1, 3]])
                    small3 = view(small[:], 0, [[3 * U, G], [3, U], [1, 3]])
                    tt(small3, f1, r_o(0), ALU.mult)
                    nc.vector.tensor_copy(fs[:, :, 0:U], src[m][:, :, 0:U])
                    dve.drain()
                    red(fs[:, :, U:2 * U], small3, AX.X, ALU.add)
                    dve.drain()
                    for b in range(NBAT):
                        half = (m * NBAT + b) % 2
                        t0 = b * RB
                        at = half * RB * 512
                        dve.wait_ge(r_ready, n * NBAT + (b + 1))
                        tt(pa[:, t0:t0 + RB, :, :], view(r_ps[:], at, [[512, RB], [2 * U, 2 * U], [1, 2 * U]]),
                           view(fs[:], t0 * 2 * U, [[2 * U, RB], [0, 2 * U], [1, 2 * U]]), ALU.mult)
                        for t in range(RB):
                            mul = tt(view(pbb[:], (t0 + t) * 6 * U * U, [[3 * U, 2 * U], [U, 3], [1, U]]),
                                     view(r_ps[:], at + 512 * t + 4 * U * U, [[U, 2 * U], [0, 3], [1, U]]),
                                     view(src[m][:], (t0 + t) * D + U, [[0, 2 * U], [1, 3], [3, U]]), ALU.mult)
                        mul.then_inc(r_used, 1)
                    dve.drain().then_inc(features_used, 1)
                    red(view(qa[:], 0, [[1, G * 2 * U]]), view(pa[:], 0, [[2 * U, G * 2 * U], [1, 2 * U]]), AX.X, ALU.add)
                    red(view(qb[:], 0, [[3 * U, G], [1, 3 * U]]), view(pbb[:], 0, [[6 * U * U, G], [U, 3 * U], [1, U]]), AX.X, ALU.add)
                    red(view(q1[:], 0, [[5 * U, G], [5, U], [1, 3]]),
                        view(pbb[:], 3 * U * U, [[6 * U * U, G], [3 * U, U], [U, 3], [1, U]]), AX.X, ALU.add)
                    dve.drain()
                    nc.vector.tensor_copy(q1[:, :, :, 3:5], q1[:, :, :, 0:2])
                    if not first:
                        dve.wait_ge(vis.rows_free, n - 1)
                    nc.vector.tensor_copy(msg[m][:, :, 0:U], qa[:, :, 0:U])
                    tt(small3, view(qa[:], U, [[2 * U, G], [1, U], [0, 3]]), r_o(0), ALU.mult)
                    dve.drain()
                    out1 = view(msg[m][:], U, [[4 * U, G], [3, U], [1, 3]])
                    qb3 = view(qb[:], 0, [[3 * U, G], [3, U], [1, 3]])
                    tt(out1, small3, qb3, ALU.add)
                    shifted = lambda at: view(q1[:], at, [[5 * U, G], [5, U], [1, 3]])
                    dve.drain()
                    tt(small3, shifted(2), r_o(1), ALU.mult)
                    tt(qb3, shifted(1), r_o(2), ALU.mult)
                    dve.drain()
                    tt(out1, out1, small3, ALU.add)
                    dve.drain()
                    tt(out1, out1, qb3, ALU.subtract).then_inc(msg_ready, 1)
                    vis.group_dve(dve, n, dst[m][:])
                    dve.drain().then_inc(group_read, 1)
                group(0, 0, True)
                group(0, 1, True)
                with dve.Fori(1, PAIRS) as i:
                    for m in range(2):
                        group(i, m, False)
                vis.finish_dve(dve)
                dve.drain().then_inc(msg_ready, 1)
                dve.sem_inc(taken, 1)
                with dve.Fori(0, NCH) as c:
                    dve.wait_ge(turned_s, c + 1)
                    part = view(k.x[:], c * (CB * D), [[1, CB * D]])
                    tt(part, part, o_ps[:], ALU.add).then_inc(taken, 1)
                dve.drain()
                layer_norm(nc, dve, None, k, k.x, scratch, mean, var, (norm_in, norm_out), 1)
                dve.drain().then_inc(out_ready, 1)


_INPUTS = ["x", "src", "dst", "edge_attr_16", "edge_attr_3", "edge_weight",
           "L0_gnn_w1a", "L0_gnn_b1a", "L0_gnn_w1b", "L0_gnn_b1b", "L0_gnn_w2a", "L0_gnn_b2a", "L0_gnn_w2b", "L0_gnn_b2b",
           "L3_gnn_w1", "L3_gnn_b1", "L3_gnn_w2", "L3_gnn_b2"]


def kernel(**inputs):
    import numpy as np
    import concourse.bacc as bacc
    from concourse.bass_utils import run_bass_kernel_spmd

    nc = bacc.Bacc("TRN2", target_bir_lowering=False, num_devices=1)
    arrays, io = {}, {}
    for name in _INPUTS:
        a = np.ascontiguousarray(inputs[name])
        arrays[f"in_{name}"] = a
        io[name] = nc.dram_tensor(f"in_{name}", a.shape, mybir.dt.from_np(a.dtype), kind="ExternalInput").ap()
    out = nc.dram_tensor("out_x", (N, D), F32, kind="ExternalOutput").ap()
    build(nc, io, out)
    result = run_bass_kernel_spmd(nc, [arrays], core_ids=[0])
    return result.results[0]["out_x"]
```

```python
import math

import concourse.bass as bass
from concourse import mybir
from contextlib import ExitStack

F32 = mybir.dt.float32
BF16 = mybir.dt.bfloat16
FP8 = mybir.dt.float8e4
I32 = mybir.dt.int32
U8 = mybir.dt.uint8
ALU = mybir.AluOpType
ACT = mybir.ActivationFunctionType
AX = mybir.AxisListType

N, E, D = 12500, 412500, 32
P = 128
NB = (N + P - 1) // P
NPAD = NB * P
LAST = N - (NB - 1) * P
EP = 125
COLS = E // EP
G = 10
GE = G * EP
NG = E // GE
PAIRS = NG // 2
DE, DI, DH = 16, 48, 96
HID = 64
STEPS, ALPHA = 10, 0.1
EPS = 1e-5

CB = 7
CW = CB * P
HW = CW // 2
NCH = NB // CB
HH = 14
HG = NB // HH
PLANE = NCH * HG * P * HH * CW
SPARE = -(-PLANE // (1 << 19)) << 19
DIGITS = 5
BATCH = 30
KPAD = EP * (COLS + 20)
NODE_BITS = 14
DST_MASK = (1 << NODE_BITS) - 1
DIV_CB = (9363, 16)
DIV_HH = (4682, 16)
TESTS = [48, 64, 128, 512, 2048, 8192, 32768, 131072]
NT = len(TESTS)


def view(ap, offset, dims):
    return bass.AP(ap.tensor, ap.offset + offset, [list(ap.ap[0])] + [list(d) for d in dims])


def plane_part(plane, u):
    parts = plane[0:PLANE, :].rearrange("(u p n) o -> u p (n o)", u=NCH * HG, p=P)
    return parts[bass.ds(u, 1), :, :].rearrange("a p n -> (a p) n")


def await_alone(eng, passed, sem, value):
    eng.wait_ge(sem, value)
    eng.sem_inc(passed, 1)


class Build:
    pass


def build(nc, io, out):
    ctx = ExitStack()
    with ctx:
        k = Build()
        k.io, k.out = io, out

        def sem(name):
            return ctx.enter_context(nc.semaphore(name))

        def sb(name, shape, dt, stack=ctx):
            return stack.enter_context(nc.sbuf_tensor(name, shape, dt))

        def pb(name, shape, dt, stack):
            return stack.enter_context(nc.psum_tensor(name, shape, dt))

        k.sem, k.sb, k.pb = sem, sb, pb

        def dram(name, shape, dt):
            return nc.dram_tensor(name, shape, dt, kind="Internal").ap()

        k.planes = [dram(f"multiplicity_digit{d}", (SPARE + E, 1), U8) for d in range(DIGITS)]
        k.keys_d = dram("edge_keys", (KPAD + E + KPAD,), I32)
        k.dst_d = dram("dst_float", (E,), F32)
        k.hist_d = dram("src_split", (E, 2), BF16)
        k.xin_d = dram("edge_inputs", (NG, EP, G * DI), F32)
        k.dir_d = dram("edge_directions", (E, 5), F32)
        k.range_d = dram("block_ranges", (2, NG), I32)
        k.x3_d = dram("x_after_layer3", (NPAD, D), F32)

        k.passed_pool, k.passed_pe, k.passed_dve = sem("passed_pool"), sem("passed_pe"), sem("passed_dve")

        k.x = sb("x", [P, NB, D], F32)
        k.iota = sb("iota", [P, P], F32)
        k.ident = sb("ident", [P, P], F32)
        k.ctl = sb("ctl", [1, 8], I32)
        k.table = sb("block_table", [1, 2, NG], I32)
        k.small = sb("small", [P, NB, 2], F32)

        with ExitStack() as scatter_data:
            k.index = sb("scatter_index", [EP, COLS], I32, scatter_data)
            k.digit = sb("scatter_digit", [EP, DIGITS, COLS], U8, scatter_data)
            with ExitStack() as s:
                prepare(nc, k, s)
            with ExitStack() as s:
                edge_network(nc, k, s)
        with ExitStack() as s:
            propagate(nc, k, s)
        with ExitStack() as s:
            tensor_messages(nc, k, s)


def prepare(nc, k, s):
    sb, pb, sem, io = k.sb, k.pb, k.sem, k.io
    iota_i = sb("iota_i", [P, 2, P], I32, s)
    pcol = sb("pcol", [P, 1], F32, s)
    dst = sb("dst_i", [EP, COLS], I32, s)
    src = sb("src_i", [EP, COLS], I32, s)
    key = sb("key", [EP, COLS], I32, s)
    ta = sb("ta", [EP, COLS], I32, s)
    tb = sb("tb", [EP, COLS], I32, s)
    near = [sb(f"near_keys{n}", [EP, COLS], I32, s) for n in range(2)]
    zeros = sb("zeros_u8", [P, HH * CW], U8, s)
    minus = view(view(k.digit[:], 0, [[1, DIGITS * COLS]]).bitcast(I32), 0, [[1, KPAD // EP]])
    mult = view(ta[:], 0, [[1, COLS]]).bitcast(F32)
    behind = src[:].bitcast(F32)
    number = dst
    tests = sb("tests", [P, 16], F32, s)
    row = sb("row", [16, 32], F32, s)
    weights = sb("weights", [1, 16], F32, s)
    GR = 3
    RP = NG // GR
    dst_g = sb("dst_g", [RP, GR, GE], I32, s)
    rng = sb("rng", [RP, 2, GR], F32, s)
    rng_i = sb("rng_i", [RP, 2, GR], I32, s)
    idx = [sb(f"l0_idx{m}", [EP, G], I32, s) for m in range(2)]
    ea = [sb(f"l0_ea{m}", [EP, G, DE], F32, s) for m in range(2)]
    xin = [sb(f"l0_xin{m}", [EP, G, DI], F32, s) for m in range(2)]
    tp = pb("prep_ps", [16, P], F32, s)

    edges_loaded, ranges_loaded, x_loaded = sem("edges_loaded"), sem("ranges_loaded"), sem("x_loaded")
    iota_done, const_done, x_zero = sem("iota_done"), sem("const_done"), sem("x_zero")
    minus_ready, minus_stored = sem("minus_ready"), sem("minus_stored")
    zero_ready, planes_zeroed = sem("zero_ready"), sem("planes_zeroed")
    key_ready, key_stored = sem("key_ready"), sem("key_stored")
    packed_ready, packed_stored = sem("packed_ready"), sem("packed_stored")
    near_loaded = [sem(f"near_loaded{n}") for n in range(2)]
    near_used = sem("near_used")
    rng_ready, rng_stored, rng_back = sem("rng_ready"), sem("rng_stored"), sem("rng_back")
    tests_ready, tests_turned, best_ready, best_turned = (sem(x) for x in (
        "tests_ready", "tests_turned", "best_ready", "best_turned"))
    bound_ready = sem("bound_ready")
    idx_loaded = [sem(f"idx_loaded{m}") for m in range(2)]
    ea_loaded = [sem(f"ea_loaded{m}") for m in range(2)]
    gathered = [sem(f"gathered{m}") for m in range(2)]
    xin_stored = [sem(f"xin_stored{m}") for m in range(2)]
    ea_copied, dst_used = sem("ea_copied"), sem("dst_used")

    resident = lambda a: a.rearrange("(p c) -> p c", p=EP)
    k.idx_view = io["src"].rearrange("(g p j) -> g p j", p=EP, j=G)
    ea_view = io["edge_attr_16"].rearrange("(g p j) f -> g p (j f)", p=EP, j=G)

    with nc.Block() as block:

        @block.sync
        def _(sp):
            sp.dma_start(dst[:], resident(io["dst"])).then_inc(edges_loaded, 16)
            sp.dma_start(src[:], resident(io["src"])).then_inc(edges_loaded, 16)
            sp.dma_start(dst_g[:], io["dst"].rearrange("(p g c) -> p g c", p=RP, g=GR)).then_inc(ranges_loaded, 16)
            sp.wait_ge(minus_ready, 1)
            for at in (0, KPAD + E):
                sp.dma_start(k.keys_d[at:at + KPAD].rearrange("(p c) -> p c", p=EP), minus).then_inc(minus_stored, 16)
            sp.wait_ge(x_zero, 1)
            full = (NB - 1) * P
            sp.dma_start(k.x[:, 0:NB - 1, :], io["x"][0:full, :].rearrange("(b p) f -> p b f", p=P)).then_inc(x_loaded, 16)
            sp.dma_start(k.x[0:LAST, NB - 1, :], io["x"][full:N, :]).then_inc(x_loaded, 16)
            sp.wait_ge(key_ready, 1)
            sp.dma_start(resident(k.keys_d[KPAD:KPAD + E]), key[:]).then_inc(key_stored, 16)
            sp.wait_ge(packed_ready, 1)
            sp.dma_start(resident(k.dst_d), near[0][:].bitcast(F32)).then_inc(packed_stored, 16)
            sp.wait_ge(packed_ready, 2)
            sp.dma_start(k.hist_d.rearrange("(p c) t -> p (c t)", p=EP), near[1][:].bitcast(BF16)).then_inc(packed_stored, 16)
            sp.wait_ge(rng_ready, 1)
            sp.dma_start(k.range_d.rearrange("t (p g) -> p t g", g=GR), rng_i[:]).then_inc(rng_stored, 16)
            sp.wait_ge(rng_stored, 16)
            for t in range(2):
                sp.dma_start(k.table[0:1, t, :], k.range_d[t:t + 1, :]).then_inc(rng_back, 16)
            sp.wait_ge(x_loaded, 32)
            sp.wait_ge(rng_back, 32)
            sp.wait_ge(key_stored, 16)
            sp.wait_ge(minus_stored, 32)
            sp.wait_ge(packed_stored, 32)
            for n, far in enumerate(TESTS + [1]):
                if n >= 2:
                    sp.wait_ge(near_used, n - 1)
                sp.dma_start(near[n % 2][:], resident(k.keys_d[KPAD + far:KPAD + far + E])).then_inc(near_loaded[n % 2], 16)
            sp.wait_ge(bound_ready, 1)
            bound = sp.value_load(k.ctl[0:1, 0:1], min_val=2, max_val=E)
            sp.wait_ge(near_used, NT + 1)
            with sp.Fori(1, bound + 1) as far:
                for n in range(2):
                    if n == 0:
                        at = far * -1 + KPAD
                    else:
                        at = far + KPAD
                    sp.wait_ge(near_used, far * 2 + (NT - 2 + n))
                    sp.dma_start(near[n][:], resident(k.keys_d[bass.ds(at, E)])).then_inc(near_loaded[n], 16)

        @block.gpsimd
        def _(pool):
            pool.iota(iota_i[:, 0, :], [[1, P]], base=0, channel_multiplier=0).then_inc(iota_done, 1)
            pool.iota(iota_i[:, 1, 0:1], [[0, 1]], base=0, channel_multiplier=1).then_inc(iota_done, 1)
            pool.wait_ge(dst_used, 1)
            pool.iota(number[:], [[1, COLS]], base=0, channel_multiplier=COLS).then_inc(iota_done, 1)
            def gather(i, m, first):
                n = i + 1
                await_alone(pool, k.passed_pool, idx_loaded[m], n * 16)
                if not first:
                    await_alone(pool, k.passed_pool, xin_stored[m], i * 16)
                for j in range(G):
                    pool.indirect_dma_start(xin[m][:, j, 0:D], None, io["x"],
                                            bass.IndirectOffsetOnAxis(idx[m][:, j:j + 1], 0)).then_inc(gathered[m], 16)
            for m in range(2):
                gather(0, m, True)
            with pool.Fori(1, PAIRS) as i:
                for m in range(2):
                    gather(i, m, False)

        @block.scalar
        def _(act):
            def load(i, m):
                act.dma_start(idx[m][:], k.idx_view[bass.ds(i * 2 + m, 1), :, :].rearrange("a p j -> (a p) j")).then_inc(idx_loaded[m], 16)
                act.dma_start(view(ea[m][:], 0, [[1, G * DE]]), ea_view[bass.ds(i * 2 + m, 1), :, :].rearrange("a p j -> (a p) j")).then_inc(ea_loaded[m], 16)

            def group(i, m, first, last):
                if not (last and m == 1):
                    load(i + m, 1 - m)
                if not first:
                    act.wait_ge(xin_stored[m], i * 16)
                act.wait_ge(ea_loaded[m], (i + 1) * 16)
                nc.scalar.copy(xin[m][:, :, D:DI], ea[m][:]).then_inc(ea_copied, 1)
                act.wait_ge(gathered[m], (i + 1) * (16 * G))
                act.wait_ge(ea_copied, i * 2 + (m + 1))
                act.dma_start(k.xin_d[bass.ds(i * 2 + m, 1), :, :].rearrange("a p j -> (a p) j"),
                              view(xin[m][:], 0, [[1, G * DI]])).then_inc(xin_stored[m], 16)

            load(0, 0)
            for m in range(2):
                group(0, m, True, False)
            act.wait_ge(zero_ready, 1)
            with act.Fori(1, NCH * HG + 1) as i:
                for m in range(2):
                    group(i, m, False, False)
                act.dma_start(plane_part(k.planes[0], i - 1), zeros[:]).then_inc(planes_zeroed, 16)
            with act.Fori(NCH * HG + 1, PAIRS - 1) as i:
                for m in range(2):
                    group(i, m, False, False)
            for m in range(2):
                group(PAIRS - 1, m, False, True)
            for m in range(2):
                act.wait_ge(xin_stored[m], PAIRS * 16)
            act.wait_ge(planes_zeroed, NCH * HG * 16)

        @block.vector
        def _(dve):
            ts, tt = nc.vector.tensor_scalar, nc.vector.tensor_tensor
            nc.vector.memset(k.x[:, NB - 1, :], 0.0).then_inc(x_zero, 1)
            nc.vector.memset(minus, -1).then_inc(minus_ready, 1)
            nc.vector.memset(zeros[:].bitcast(I32), 0).then_inc(zero_ready, 1)
            nc.vector.memset(tests[:], 0.0)
            dve.wait_ge(iota_done, 2)
            nc.vector.tensor_copy(pcol[:], iota_i[:, 1, 0:1])
            nc.vector.tensor_copy(k.iota[:], iota_i[:, 0, :])
            dve.drain()
            ts(k.ident[:], k.iota[:], pcol[:, 0:1], None, ALU.is_equal)
            dve.wait_ge(edges_loaded, 32)
            ts(tb[:], src[:], NODE_BITS, None, ALU.logical_shift_left)
            dve.drain()
            tt(key[:], tb[:], dst[:], ALU.bitwise_or).then_inc(key_ready, 1)
            nc.vector.tensor_copy(near[0][:].bitcast(F32), dst[:]).then_inc(packed_ready, 1)
            pair = view(near[1][:].bitcast(BF16), 0, [[2, COLS]])
            pair_hi = view(near[1][:].bitcast(BF16), 1, [[2, COLS]])
            dve.drain()
            ts(tb[:], src[:], P - 1, None, ALU.bitwise_and)
            ts(ta[:], src[:], 7, None, ALU.logical_shift_right)
            dve.drain()
            nc.vector.tensor_copy(pair, tb[:])
            nc.vector.tensor_copy(pair_hi, ta[:])
            dve.drain().then_inc(packed_ready, 1)
            per_c = HG * P * HH * CB - CB
            per_h = P * HH * CB - HH * CB
            q = k.index
            ts(q[:], tb[:], float(HH * CB), None, ALU.mult)
            dve.drain()
            nc.vector.scalar_tensor_tensor(q[:], ta[:], float(CB), q[:], ALU.mult, ALU.add)
            dve.drain()
            ts(ta[:], ta[:], float(DIV_HH[0]), None, ALU.mult)
            dve.drain()
            ts(ta[:], ta[:], DIV_HH[1], None, ALU.logical_shift_right)
            dve.drain()
            nc.vector.scalar_tensor_tensor(q[:], ta[:], float(per_h), q[:], ALU.mult, ALU.add)
            dve.drain()
            ts(tb[:], dst[:], 7, None, ALU.logical_shift_right)
            dve.drain()
            tt(q[:], q[:], tb[:], ALU.add)
            dve.drain()
            ts(ta[:], tb[:], float(DIV_CB[0]), None, ALU.mult)
            dve.drain()
            ts(ta[:], ta[:], DIV_CB[1], None, ALU.logical_shift_right)
            dve.drain()
            nc.vector.scalar_tensor_tensor(q[:], ta[:], float(per_c), q[:], ALU.mult, ALU.add)
            dve.drain()
            ts(tb[:], dst[:], P - 1, None, ALU.bitwise_and)
            dve.drain()
            ts(q[:], q[:], 7, None, ALU.logical_shift_left)
            dve.drain()
            tt(q[:], q[:], tb[:], ALU.bitwise_or)
            dve.wait_ge(ranges_loaded, 16)
            nc.vector.tensor_reduce(rng[:, 0, :], dst_g[:], AX.X, ALU.min)
            nc.vector.tensor_reduce(rng[:, 1, :], dst_g[:], AX.X, ALU.max)
            dve.drain()
            nc.vector.tensor_copy(rng_i[:], rng[:])
            dve.drain()
            ts(rng_i[:], rng_i[:], 7, None, ALU.logical_shift_right)
            dve.drain()
            ts(rng_i[:, 1, :], rng_i[:, 1, :], 1.0, None, ALU.add).then_inc(rng_ready, 1)
            for n in range(NT + 1):
                b = near[n % 2]
                dve.wait_ge(near_loaded[n % 2], 16 * (n // 2 + 1))
                dve.drain()
                if n < NT:
                    tt(tb[:], key[:], b[:], ALU.bitwise_xor).then_inc(near_used, 1)
                    dve.drain()
                    ts(tb[:], tb[:], DST_MASK, None, ALU.bitwise_and)
                    dve.drain()
                else:
                    ts(ta[:], b[:], DST_MASK, None, ALU.bitwise_and).then_inc(near_used, 1)
                    dve.drain()
                    tt(tb[:], ta[:], dst[:], ALU.subtract)
                    dve.drain()
                nc.vector.tensor_reduce(tests[0:EP, n:n + 1], tb[:], AX.X, ALU.min)
            dve.drain()
            nc.vector.memset(behind, 0.0).then_inc(dst_used, 1)
            ts(tests[0:EP, 0:NT], tests[0:EP, 0:NT], 0.0, None, ALU.is_equal)
            ts(tests[0:EP, NT:NT + 1], tests[0:EP, NT:NT + 1], 0.0, None, ALU.is_lt).then_inc(tests_ready, 1)
            for n in range(NT):
                step = (TESTS + [E])[n + 1] - TESTS[n]
                nc.vector.memset(weights[0:1, n:n + 1], float(step))

            def over_partitions(n, count):
                dve.wait_ge(tests_turned, n)
                nc.vector.tensor_reduce(row[0:count, 16:17], tp[0:count, :], AX.X, ALU.max).then_inc(best_ready, 1)
                dve.wait_ge(best_turned, n)
            dve.drain()
            over_partitions(1, NT + 1)
            tt(row[0:1, 0:NT], tp[0:1, 0:NT], weights[0:1, 0:NT], ALU.mult)
            ts(row[0:1, NT:NT + 1], tp[0:1, NT:NT + 1], float(E), None, ALU.mult)
            dve.drain()
            nc.vector.tensor_reduce(row[0:1, NT + 1:NT + 2], row[0:1, 0:NT], AX.X, ALU.add)
            dve.drain()
            ts(row[0:1, NT + 1:NT + 2], row[0:1, NT + 1:NT + 2], float(TESTS[0]), None, ALU.add)
            dve.drain()
            tt(row[0:1, NT + 1:NT + 2], row[0:1, NT + 1:NT + 2], row[0:1, NT:NT + 1], ALU.max)
            dve.drain()
            nc.vector.tensor_copy(k.ctl[0:1, 0:1], row[0:1, NT + 1:NT + 2]).then_inc(bound_ready, 1)
            dve.drain()
            nc.vector.memset(mult, 1.0)
            dve.wait_ge(bound_ready, 1)
            bound = dve.value_load(k.ctl[0:1, 0:1], min_val=2, max_val=E)
            seen = [(NT + 2) // 2, (NT + 1) // 2]
            with dve.Fori(1, bound + 1) as far:
                for n in range(2):
                    dve.drain()
                    dve.wait_ge(near_loaded[n], (far + seen[n]) * 16)
                    tt(tb[:], key[:], near[n][:], ALU.bitwise_xor).then_inc(near_used, 1)
                    dve.drain()
                    same = behind if n == 0 else mult
                    nc.vector.scalar_tensor_tensor(same, tb[:], 0.0, same, ALU.is_equal, ALU.add)
            dve.drain()
            tt(mult, mult, behind, ALU.add)
            dve.wait_ge(iota_done, 3)
            ts(tb[:], behind, 0.0, -1.0, ALU.is_gt, ALU.mult)
            dve.drain()
            ts(number[:], number[:], SPARE, None, ALU.bitwise_or)
            dve.drain()
            tt(number[:], number[:], tb[:], ALU.bitwise_and)
            dve.drain()
            ts(tb[:], tb[:], -1, None, ALU.bitwise_xor)
            dve.drain()
            tt(q[:], q[:], tb[:], ALU.bitwise_and)
            dve.drain()
            tt(q[:], q[:], number[:], ALU.bitwise_or)
            dve.drain()
            nc.vector.tensor_reduce(tests[0:EP, 0:1], mult, AX.X, ALU.max).then_inc(tests_ready, 1)
            over_partitions(2, 1)
            nc.vector.memset(row[0:1, 0:1], 1.0)
            for d in range(1, DIGITS):
                dve.drain()
                nc.vector.scalar_tensor_tensor(row[0:1, 0:1], tp[0:1, 0:1], float(16 ** d), row[0:1, 0:1], ALU.is_ge, ALU.add)
            dve.drain()
            nc.vector.tensor_copy(k.ctl[0:1, 1:2], row[0:1, 0:1])
            nc.vector.tensor_copy(key[:], mult)
            dve.drain().then_inc(bound_ready, 1)
            dve.wait_ge(bound_ready, 2)
            planes = dve.value_load(k.ctl[0:1, 1:2], min_val=1, max_val=DIGITS)

            def digit(d):
                ts(tb[:], key[:], 4 * d, 15, ALU.logical_shift_right, ALU.bitwise_and)
                dve.drain()
                nc.vector.tensor_copy(k.digit[:, d, :].bitcast(FP8), tb[:], saturate=False)
                dve.drain()
            digit(0)
            for d in range(1, DIGITS):
                with dve.If(planes > d):
                    digit(d)

        @block.tensor
        def _(pe):
            for n, count in ((1, NT + 1), (2, 1)):
                pe.wait_ge(tests_ready, n)
                nc.tensor.matmul(tp[0:count, :], tests[:, 0:count], k.ident[:], start=True, stop=True).then_inc(tests_turned, 1)
                pe.wait_ge(best_ready, n)
                nc.tensor.matmul(tp[0:1, 0:count], row[0:count, 16:17], k.ident[0:count, 0:count], start=True, stop=True).then_inc(best_turned, 1)


class Visits:

    def __init__(self, nc, k, s, psum, name, rows):
        self.nc, self.k, self.name, self.rows = nc, k, name, rows
        self.nodes = k.sb(f"{name}_nodes", [EP, NPAD], F32, s)
        self.onehot = k.sb(f"{name}_onehot", [EP, 2, G, P], F32, s)
        self.total = k.sb(f"{name}_total", [rows, NPAD + P], F32, s)
        self.ps = k.pb(f"{name}_visit_ps", [rows, 2, 512], F32, psum)
        self.onehot_ready = k.sem(f"{name}_onehot_ready")
        self.product_done = k.sem(f"{name}_product_done")
        self.added = k.sem(f"{name}_added")
        self.rows_free = k.sem(f"{name}_rows_free")
        self.zero = k.sb(f"{name}_zero", [1, P], F32, s)
        self.zero_ready = k.sem(f"{name}_zero_ready")

    def start_dve(self, dve):
        nc = self.nc
        nc.vector.memset(self.zero[:], 0.0).then_inc(self.zero_ready, 1)
        nc.vector.memset(self.total[:], 0.0)
        nc.vector.tensor_copy(self.nodes[:, 0:P], self.k.iota[0:EP, :])
        with dve.Fori(1, NB) as b:
            dve.drain()
            nc.vector.tensor_scalar(self.nodes[:, bass.ds(b * P, P)], self.nodes[:, bass.ds(b * P - P, P)],
                                    float(P), None, ALU.add)
        dve.drain().then_inc(self.added, 1)
        self.count = dve.alloc_register(f"{self.name}_visits_dve")
        self.before = dve.alloc_register(f"{self.name}_block_before")
        dve.reg_mov(self.count, 0)
        dve.reg_mov(self.before, NB)

    def start_pe(self, pe):
        pe.wait_ge(self.zero_ready, 1)
        self.nc.tensor.matmul(self.ps[:, 1, 0:P], self.zero[0:1, 0:self.rows], self.zero[0:1, :],
                              start=True, stop=True).then_inc(self.product_done, 1)
        self.count_pe = pe.alloc_register(f"{self.name}_visits_pe")
        pe.reg_mov(self.count_pe, 0)

    def blocks(self, eng, g):
        table = self.k.table
        first = eng.value_load(table[0:1, 0, bass.ds(g, 1)], min_val=0, max_val=NB - 1)
        end = eng.value_load(table[0:1, 1, bass.ds(g, 1)], min_val=1, max_val=NB)
        return first, end

    def add(self, dve, v):
        at = dve.snap(self.before, min_val=0, max_val=NB)
        dve.wait_ge(self.product_done, v + 1)
        dve.wait_ge(self.added, v + 1)
        part = self.total[:, bass.ds(at * P, P)]
        self.nc.vector.tensor_tensor(part, part, view(self.ps[:], ((v + 1) % 2) * 512, [[1, P]]), ALU.add).then_inc(self.added, 1)

    def group_dve(self, dve, g, dst):
        first, end = self.blocks(dve, g)
        with dve.Fori(first, end) as b:
            v = dve.snap(self.count, min_val=0, max_val=NG * NB)
            self.nc.vector.tensor_tensor(view(self.onehot[:], (v % 2) * (G * P), [[P, G], [1, P]]),
                                         view(dst, 0, [[1, G], [0, P]]),
                                         view(self.nodes[:], b * P, [[0, G], [1, P]]),
                                         ALU.is_equal).then_inc(self.onehot_ready, 1)
            self.add(dve, v)
            dve.reg_mov(self.before, b)
            dve.reg_add(self.count, self.count, 1)

    def finish_dve(self, dve):
        self.add(dve, dve.snap(self.count, min_val=0, max_val=NG * NB))

    def group_pe(self, pe, g, rows):
        first, end = self.blocks(pe, g)
        with pe.Fori(first, end):
            v = pe.snap(self.count_pe, min_val=0, max_val=NG * NB)
            pe.wait_ge(self.onehot_ready, v + 1)
            pe.wait_ge(self.added, v + 1)
            for j in range(G):
                mm = self.nc.tensor.matmul(view(self.ps[:], (v % 2) * 512, [[1, P]]), rows(j),
                                           view(self.onehot[:], (v % 2) * (G * P) + j * P, [[1, P]]),
                                           start=(j == 0), stop=(j == G - 1))
            mm.then_inc(self.product_done, 1)
            pe.reg_add(self.count_pe, self.count_pe, 1)
        pe.drain().then_inc(self.rows_free, 1)


def layer_norm(nc, dve, act, k, y, scratch, mean, var, sems, turn):
    squares_ready, root_ready = sems
    per_node = lambda a: view(a[:], 0, [[1, NB], [0, D]])
    if dve is not None:
        nc.vector.tensor_reduce(mean[:], y[:], AX.X, ALU.add)
        dve.drain()
        nc.vector.tensor_scalar(mean[:], mean[:], 1.0 / D, None, ALU.mult)
        dve.drain()
        nc.vector.tensor_tensor(y[:], y[:], per_node(mean), ALU.subtract)
        dve.drain()
        nc.vector.tensor_tensor(scratch[:], y[:], y[:], ALU.mult)
        dve.drain()
        nc.vector.tensor_reduce(var[:], scratch[:], AX.X, ALU.add)
        dve.drain()
        nc.vector.tensor_scalar(var[:], var[:], 1.0 / D, EPS, ALU.mult, ALU.add).then_inc(squares_ready, 1)
        dve.wait_ge(root_ready, turn)
        nc.vector.reciprocal(var[:], var[:])
        dve.drain()
        nc.vector.tensor_tensor(y[:], y[:], per_node(var), ALU.mult)
        dve.drain()
    else:
        act.wait_ge(squares_ready, turn)
        nc.scalar.sqrt(var[:], var[:]).then_inc(root_ready, 1)


def edge_network(nc, k, s):
    sb, pb, sem, io = k.sb, k.pb, k.sem, k.io
    M1 = DH + 1
    xin = [sb(f"e_xin{m}", [EP, G, DI], F32, s) for m in range(2)]
    dst = [sb(f"e_dst{m}", [EP, G], F32, s) for m in range(2)]
    split = [sb(f"e_split{m}", [EP, G, 2], BF16, s) for m in range(2)]
    hist_lo = sb("hist_lo", [EP, G, P], BF16, s)
    hist_hi = sb("hist_hi", [EP, G, NB], BF16, s)
    iota_h = sb("iota_h", [EP, P], BF16, s)
    xt = sb("xt", [DI + 1, 2, GE], F32, s)
    hid = [sb(f"e_hidden{m}", [EP, G, M1], F32, s) for m in range(2)]
    w1a = sb("w1a", [DI + 1, DH], F32, s)
    w1b = sb("w1b", [M1, M1], F32, s)
    count_row = sb("count_row", [M1, DH], F32, s)
    w2x = sb("w2x", [D, DI], F32, s)
    w2g = sb("w2g", [DH, DI], F32, s)
    b2a = sb("b2a", [DI, 1], F32, s)
    w2b = sb("w2b", [DI + 1, D], F32, s)
    stage_i = [sb(f"stage_i{m}", [EP, BATCH], I32, s) for m in range(2)]
    stage_v = [sb(f"stage_v{m}", [EP, BATCH], U8, s) for m in range(2)]

    weights_zero, weights_loaded = sem("e_weights_zero"), sem("e_weights_loaded")
    loaded = [sem(f"e_loaded{m}") for m in range(2)]
    group_read = sem("e_group_read")
    xt_ready, xt_evac, h_ready, h_evac = (sem("e_" + x) for x in ("xt_ready", "xt_evac", "h_ready", "h_evac"))
    hist_ready, hist_done = sem("hist_ready"), sem("hist_done")
    staged = [sem(f"staged{m}") for m in range(2)]
    stored = [sem(f"digits_stored{m}") for m in range(2)]
    cleared, clear_ready = sem("cleared"), sem("clear_ready")
    SUB = [(0, 4), (4, 4), (8, 2)]
    HT = 5
    zeros = sb("e_zeros", [P, CW], U8, s)
    RC = 132
    rel = sb("rel", [EP, RC, 3], F32, s)
    square = sb("rel_square", [EP, RC, 3], F32, s)
    norm = sb("rel_norm", [EP, RC], F32, s)
    unit = sb("rel_unit", [EP, RC, 5], F32, s)
    rel_loaded, unit_stored, unit_ready, norm_ready, root_ready = (sem(x) for x in (
        "rel_loaded", "unit_stored", "unit_ready", "norm_ready", "rel_root_ready"))

    with ExitStack() as q:
        vis = Visits(nc, k, s, q, "e", M1)
        xt_ps = pb("xt_ps", [DI, 3, 512], F32, q)
        h_ps = pb("h_ps", [EP, 2, 512], F32, q)
        hist_ps = pb("hist_ps", [P, NB], F32, q)
        with nc.Block() as block:

            @block.gpsimd
            def _(pool):
                planes = pool.value_load(k.ctl[0:1, 1:2], min_val=1, max_val=DIGITS)
                pool.wait_ge(clear_ready, 1)
                batches = COLS // BATCH

                def store_plane(d):
                    def batch(i, m, first):
                        if not first:
                            await_alone(pool, k.passed_pool, stored[m], pool.snap(issued[m], min_val=16 * BATCH, max_val=1 << 24))
                        at = (i * 2 + m) * BATCH
                        nc.gpsimd.tensor_copy(stage_i[m][:], k.index[:, bass.ds(at, BATCH)]).then_inc(staged[m], 1)
                        nc.gpsimd.tensor_copy(stage_v[m][:], k.digit[:, d, bass.ds(at, BATCH)]).then_inc(staged[m], 1)
                        pool.reg_add(turns[m], turns[m], 2)
                        await_alone(pool, k.passed_pool, staged[m], pool.snap(turns[m], min_val=2, max_val=1 << 24))
                        for j in range(BATCH):
                            pool.indirect_dma_start(k.planes[d], bass.IndirectOffsetOnAxis(stage_i[m][:, j:j + 1], 0),
                                                    stage_v[m][:, j:j + 1], None).then_inc(stored[m], 16)
                        pool.reg_add(issued[m], issued[m], 16 * BATCH)
                    for m in range(2):
                        batch(0, m, d == 0)
                    with pool.Fori(1, batches // 2) as i:
                        for m in range(2):
                            batch(i, m, False)

                issued = [pool.alloc_register(f"issued{m}") for m in range(2)]
                turns = [pool.alloc_register(f"turns{m}") for m in range(2)]
                for r in issued + turns:
                    pool.reg_mov(r, 0)
                store_plane(0)
                for d in range(1, DIGITS):
                    with pool.If(planes > d):
                        with pool.Fori(0, NCH * HG * HH) as u:
                            part = k.planes[d][0:PLANE, :].rearrange("(u p n) o -> u p (n o)", p=P, n=CW)[bass.ds(u, 1), :, :]
                            pool.dma_start(part.rearrange("a p n -> (a p) n"), zeros[:]).then_inc(cleared, 16)
                        pool.wait_ge(cleared, NCH * HG * HH * 16 * d)
                        store_plane(d)
                for m in range(2):
                    await_alone(pool, k.passed_pool, stored[m], pool.snap(issued[m], min_val=16 * BATCH, max_val=1 << 24))

            @block.sync
            def _(sp):
                sp.wait_ge(weights_zero, 1)
                w = [(w1a[0:DI, :], io["L0_gnn_w1a"]), (w1a[DI:DI + 1, :], io["L0_gnn_b1a"].rearrange("(o n) -> o n", o=1)),
                     (w1b[0:DH, 0:DH], io["L0_gnn_w1b"]), (w1b[DH:M1, 0:DH], io["L0_gnn_b1b"].rearrange("(o n) -> o n", o=1)),
                     (w2x[:], io["L0_gnn_w2a"][0:D, :]), (w2g[:], io["L0_gnn_w2a"][D:D + DH, :]),
                     (b2a[:], io["L0_gnn_b2a"].rearrange("(n o) -> n o", o=1)),
                     (w2b[0:DI, :], io["L0_gnn_w2b"]), (w2b[DI:DI + 1, :], io["L0_gnn_b2b"].rearrange("(o n) -> o n", o=1))]
                for to, frm in w:
                    sp.dma_start(to, frm).then_inc(weights_loaded, 16)

                def columns(a, c, width):
                    return a.rearrange("(p e) f -> p (e f)", p=EP)[:, bass.ds(c * (RC * width), RC * width)]
                sp.dma_start(view(rel[:], 0, [[1, RC * 3]]), columns(io["edge_attr_3"], 0, 3)).then_inc(rel_loaded, 16)
                with sp.Fori(1, COLS // RC) as c:
                    sp.wait_ge(unit_ready, c)
                    sp.dma_start(columns(k.dir_d, c - 1, 5), view(unit[:], 0, [[1, RC * 5]])).then_inc(unit_stored, 16)
                    sp.dma_start(view(rel[:], 0, [[1, RC * 3]]), columns(io["edge_attr_3"], c, 3)).then_inc(rel_loaded, 16)
                sp.wait_ge(unit_ready, COLS // RC)
                sp.dma_start(columns(k.dir_d, COLS // RC - 1, 5), view(unit[:], 0, [[1, RC * 5]])).then_inc(unit_stored, 16)

                def load(i, m, first):
                    g = i * 2 + m
                    if not first:
                        sp.wait_ge(group_read, g - 1)
                        sp.wait_ge(xt_ready, g * 3 - 3)
                    def part(a):
                        return a[bass.ds(g, 1), :, :].rearrange("a p c -> (a p) c")
                    sp.dma_start(view(xin[m][:], 0, [[1, G * DI]]), part(k.xin_d)).then_inc(loaded[m], 16)
                    sp.dma_start(dst[m][:], part(k.dst_d.rearrange("(g p c) -> g p c", p=EP, c=G))).then_inc(loaded[m], 16)
                    sp.dma_start(view(split[m][:], 0, [[1, 2 * G]]),
                                 part(k.hist_d.rearrange("(g p c) t -> g p (c t)", p=EP, c=G))).then_inc(loaded[m], 16)
                for m in range(2):
                    load(0, m, True)
                with sp.Fori(1, PAIRS) as i:
                    for m in range(2):
                        load(i, m, False)
                sp.wait_ge(unit_stored, COLS // RC * 16)

            @block.tensor
            def _(pe):
                def group(i, m, first):
                    n = i * 2 + m
                    pe.wait_ge(loaded[m], (i + 1) * 48)
                    for b, (t0, tn) in enumerate(SUB):
                        if not first:
                            await_alone(pe, k.passed_pe, xt_evac, n * 3 + (b - 2))
                        for t in range(t0, t0 + tn):
                            mm = nc.tensor.transpose(xt_ps[:, b, (t - t0) * EP:(t - t0 + 1) * EP], xin[m][:, t, :],
                                                     k.ident[0:EP, 0:EP])
                        mm.then_inc(xt_ready, 1)
                    for b in range(2):
                        pe.wait_ge(xt_evac, n * 3 + (2 + b))
                        if not first:
                            pe.wait_ge(h_evac, n * 2 + (b - 1))
                        for t in range(HT):
                            mm = nc.tensor.matmul(h_ps[:, b, t * DH:(t + 1) * DH],
                                                  xt[:, m, (b * HT + t) * EP:(b * HT + t + 1) * EP], w1a[:],
                                                  start=True, stop=True)
                        mm.then_inc(h_ready, 1)
                    if not first:
                        pe.wait_ge(h_evac, n * 2)
                        vis.group_pe(pe, n - 1, lambda j: hid[1 - m][:, j, :])
                    pe.wait_ge(hist_ready, n + 1)
                    for j in range(G):
                        mm = nc.tensor.matmul(hist_ps[:], hist_lo[:, j, :], hist_hi[:, j, :], start=False,
                                              stop=False, skip_group_check=True)
                    mm.then_inc(hist_done, 1)

                pe.wait_ge(weights_loaded, 16 * 9)
                vis.start_pe(pe)
                nc.tensor.matmul(hist_ps[:], vis.zero[0:1, :], vis.zero[0:1, 0:NB], start=True, stop=False,
                                 skip_group_check=True)
                group(0, 0, True)
                group(0, 1, False)
                with pe.Fori(1, PAIRS) as i:
                    for m in range(2):
                        group(i, m, False)
                pe.wait_ge(h_evac, 2 * NG)
                vis.group_pe(pe, NG - 1, lambda j: hid[1][:, j, :])

            @block.scalar
            def _(act):
                with act.Fori(0, COLS // RC) as c:
                    act.wait_ge(norm_ready, c + 1)
                    nc.scalar.sqrt(norm[:], norm[:]).then_inc(root_ready, 1)
                act.wait_ge(weights_zero, 1)

                def group(i, m, first):
                    n = i * 2 + m
                    for b, (t0, tn) in enumerate(SUB):
                        act.wait_ge(xt_ready, n * 3 + (b + 1))
                        nc.scalar.copy(xt[0:DI, m, t0 * EP:(t0 + tn) * EP], xt_ps[:, b, 0:tn * EP]).then_inc(xt_evac, 1)
                    for b in range(2):
                        act.wait_ge(h_ready, n * 2 + (b + 1))
                        if not first and b == 0:
                            act.wait_ge(vis.rows_free, n - 1)
                        nc.scalar.activation(hid[m][:, b * HT:(b + 1) * HT, 0:DH],
                                             view(h_ps[:], b * 512, [[DH, HT], [1, DH]]), ACT.Relu).then_inc(h_evac, 1)
                for m in range(2):
                    group(0, m, True)
                with act.Fori(1, PAIRS) as i:
                    for m in range(2):
                        group(i, m, False)

            @block.vector
            def _(dve):
                tt = nc.vector.tensor_tensor
                nc.vector.memset(zeros[:].bitcast(I32), 0).then_inc(clear_ready, 1)
                for a in (w1b, count_row):
                    nc.vector.memset(a[:], 0.0)
                for a in (xt, w2b, *hid):
                    nc.vector.memset(a[:], 1.0)
                dve.drain()
                nc.vector.memset(w1b[DH:M1, DH:M1], 1.0)
                nc.vector.memset(count_row[DH:M1, :], 1.0)
                nc.vector.tensor_copy(iota_h[:], k.iota[0:EP, :])
                dve.drain().then_inc(weights_zero, 1)
                vis.start_dve(dve)

                def directions(c, first):
                    dve.wait_ge(rel_loaded, (c + 1) * 16)
                    tt(square[:], rel[:], rel[:], ALU.mult)
                    dve.drain()
                    nc.vector.tensor_reduce(norm[:], square[:], AX.X, ALU.add).then_inc(norm_ready, 1)
                    dve.wait_ge(root_ready, c + 1)
                    nc.vector.reciprocal(norm[:], norm[:])
                    dve.drain()
                    if not first:
                        dve.wait_ge(unit_stored, c * 16)
                    for to, frm, n in ((0, 1, 2), (2, 0, 1), (3, 1, 2)):
                        tt(unit[:, :, to:to + n], rel[:, :, frm:frm + n], view(norm[:], 0, [[1, RC], [0, n]]), ALU.mult)
                    dve.drain().then_inc(unit_ready, 1)
                directions(0, True)
                with dve.Fori(1, COLS // RC) as c:
                    directions(c, False)

                def group(i, m, first):
                    n = i * 2 + m
                    dve.wait_ge(loaded[m], (i + 1) * 48)
                    if not first:
                        dve.wait_ge(hist_done, n)
                    tt(hist_lo[:], view(split[m][:], 0, [[2, G], [0, P]]), view(iota_h[:], 0, [[0, G], [1, P]]), ALU.is_equal)
                    tt(hist_hi[:], view(split[m][:], 1, [[2, G], [0, NB]]), view(iota_h[:], 0, [[0, G], [1, NB]]),
                       ALU.is_equal).then_inc(hist_ready, 1)
                    vis.group_dve(dve, n, dst[m][:])
                    dve.drain().then_inc(group_read, 1)
                group(0, 0, True)
                group(0, 1, False)
                with dve.Fori(1, PAIRS) as i:
                    for m in range(2):
                        group(i, m, False)
                vis.finish_dve(dve)
                dve.wait_ge(hist_done, NG)
                nc.vector.tensor_copy(view(k.small[:], 1, [[2, NB]]), hist_ps[:])
    node_network(nc, k, vis, w1b, count_row, w2x, w2g, b2a, w2b, s)


HALVES = [(0, 4 * P), (4 * P, CW - 4 * P)]


def node_network(nc, k, vis, w1b, count_row, w2x, w2g, b2a, w2b, s):
    sb, pb, sem = k.sb, k.pb, k.sem
    M1 = DH + 1
    stage = sb("x_stage", [P, CB, D], F32, s)
    x_t = sb("x_t", [D, CW], F32, s)
    agg = sb("agg_t", [M1, CW], F32, s)
    inv = sb("inv_count", [DH, CW], F32, s)
    h2 = sb("h2", [DI + 1, CW], F32, s)
    names = ("staged", "turned", "turned_copied", "sums", "sums_copied", "counts", "mean", "h2", "h2_copied", "out", "taken")
    (staged, turned, turned_copied, sums_ready, sums_copied, counts_ready, mean_ready, h2_ready, h2_copied,
     out_ready, taken) = (sem("n_" + x) for x in names)
    ones_ready = sem("n_ones_ready")
    with ExitStack() as q:
        x_ps = pb("n_x_ps", [D, 2, 512], F32, q)
        a_ps = pb("n_a_ps", [M1, 2, 512], F32, q)
        c_ps = pb("n_c_ps", [DH, 2, 512], F32, q)
        o_ps = pb("n_o_ps", [P, 512], F32, q)
        with nc.Block() as block:

            @block.tensor
            def _(pe):
                def chunk(c, first):
                    await_alone(pe, k.passed_pe, staged, c + 1)
                    for j in range(CB):
                        mm = nc.tensor.transpose(x_ps[:, j // 4, (j % 4) * P:(j % 4 + 1) * P], stage[:, j, :], k.ident[:])
                    mm.then_inc(turned, 1)
                    for b, (at, n) in enumerate(HALVES):
                        mm = nc.tensor.matmul(a_ps[:, b, 0:n], w1b[:], vis.total[:, bass.ds(c * CW + at, n)], start=True, stop=True)
                    mm.then_inc(sums_ready, 1)
                    pe.wait_ge(sums_copied, c + 1)
                    for b, (at, n) in enumerate(HALVES):
                        mm = nc.tensor.matmul(c_ps[:, b, 0:n], count_row[:], agg[:, at:at + n], start=True, stop=True)
                    mm.then_inc(counts_ready, 1)
                    if not first:
                        pe.wait_ge(taken, c)
                    for j in range(CB):
                        mm = nc.tensor.matmul(o_ps[:, CB * D + j:CB * D + j + 1], agg[:, j * P:(j + 1) * P],
                                              k.ident[0:M1, DH:M1], start=True, stop=True)
                    mm.then_inc(counts_ready, 1)
                    pe.wait_ge(mean_ready, c + 1)
                    pe.wait_ge(turned_copied, c + 1)
                    for b, (at, n) in enumerate(HALVES):
                        nc.tensor.matmul(a_ps[0:DI, b, 0:n], w2g[:], agg[0:DH, at:at + n], start=True, stop=False)
                        mm = nc.tensor.matmul(a_ps[0:DI, b, 0:n], w2x[:], x_t[:, at:at + n], start=False, stop=True)
                    mm.then_inc(h2_ready, 1)
                    pe.wait_ge(h2_copied, c + 1)
                    for j in range(CB):
                        mm = nc.tensor.matmul(o_ps[:, j * D:(j + 1) * D], h2[:, j * P:(j + 1) * P], w2b[:], start=True, stop=True)
                    mm.then_inc(out_ready, 1)
                chunk(0, True)
                with pe.Fori(1, NCH) as c:
                    chunk(c, False)

            @block.scalar
            def _(act):
                act.wait_ge(ones_ready, 1)
                def chunk(c, first):
                    if not first:
                        act.wait_ge(taken, c)
                    nc.scalar.copy(stage[:], k.x[:, bass.ds(c * CB, CB), :]).then_inc(staged, 1)
                    act.wait_ge(turned, c + 1)
                    for b, (at, n) in enumerate(HALVES):
                        cp = nc.scalar.copy(x_t[:, at:at + n], x_ps[:, b, 0:n])
                    cp.then_inc(turned_copied, 1)
                    act.wait_ge(sums_ready, c + 1)
                    for b, (at, n) in enumerate(HALVES):
                        cp = nc.scalar.copy(agg[:, at:at + n], a_ps[:, b, 0:n])
                    cp.then_inc(sums_copied, 1)
                    act.wait_ge(h2_ready, c + 1)
                    for b, (at, n) in enumerate(HALVES):
                        cp = nc.scalar.activation(h2[0:DI, at:at + n], a_ps[0:DI, b, 0:n], ACT.Relu, bias=b2a[:, 0:1])
                    cp.then_inc(h2_copied, 1)
                chunk(0, True)
                with act.Fori(1, NCH) as c:
                    chunk(c, False)

            @block.vector
            def _(dve):
                nc.vector.memset(h2[:], 1.0).then_inc(ones_ready, 1)
                with dve.Fori(0, NCH) as c:
                    dve.wait_ge(counts_ready, c * 2 + 2)
                    for b, (at, n) in enumerate(HALVES):
                        nc.vector.tensor_scalar(inv[:, at:at + n], c_ps[:, b, 0:n], 1.0, None, ALU.max)
                    dve.drain()
                    nc.vector.reciprocal(inv[:], inv[:])
                    dve.drain()
                    nc.vector.tensor_tensor(agg[0:DH, :], agg[0:DH, :], inv[:], ALU.mult).then_inc(mean_ready, 1)
                    dve.wait_ge(out_ready, c + 1)
                    part = k.x[:, bass.ds(c * CB, CB), :]
                    nc.vector.tensor_copy(view(k.small[:], c * (2 * CB), [[2, CB]]), o_ps[:, CB * D:CB * D + CB])
                    nc.vector.tensor_tensor(part, part, view(o_ps[:], 0, [[D, CB], [1, D]]), ALU.add)
                    dve.drain().then_inc(taken, 1)


def propagate(nc, k, s):
    sb, pb, sem = k.sb, k.pb, k.sem
    passes = STEPS + 1
    slots = [sb(f"a_slot{h}", [P, HH, CW], U8, s) for h in range(HG)]
    parts = sb("f_parts", [P, NB, 3 * D], BF16, s)
    agg = sb("agg", [P, NB, D], F32, s)
    f = sb("f", [P, NB, D], F32, s)
    tenth = sb("x_tenth", [P, NB, D], F32, s)
    norms = sb("norms", [P, NB, 2], F32, s)
    mean, var = sb("mean", [P, NB], F32, s), sb("var", [P, NB], F32, s)
    turned = sb("turned", [3 * D, 2, CW], F32, s)
    select = sb("select", [3 * D, DIGITS * D], F32, s)
    a_loaded = [sem(f"a_loaded{h}") for h in range(HG)]
    a_used = sem("a_used")
    parts_ready = sem("parts_ready")
    product_ready, product_copied = sem("p_product_ready"), sem("p_product_copied")
    summed, taken = sem("p_summed"), sem("p_taken")
    norm_in, norm_out = sem("ln_in"), sem("ln_out")
    x_ready, x_stored = sem("p_x_ready"), sem("p_x_stored")

    with ExitStack() as q:
        prod = [pb(f"p_prod{m}", [3 * D, 2, 512], F32, q) for m in range(2)]
        back = [pb(f"p_back{m}", [P, CB * D], F32, q) for m in range(2)]
        with nc.Block() as block:

            def each_chunk(eng, u, planes, body):
                with eng.Fori(0, planes) as d:
                    with eng.Fori(0, NCH // 2) as c2:
                        n = eng.snap(u, min_val=0, max_val=passes * DIGITS * NCH)
                        body(n, d, c2)
                        eng.reg_add(u, u, 1)

            @block.sync
            def _(sp):
                planes = sp.value_load(k.ctl[0:1, 1:2], min_val=1, max_val=DIGITS)
                u = sp.alloc_register("pairs_sp")
                sp.reg_mov(u, 0)

                def load_plane(d):
                    with sp.Fori(0, NCH // 2) as c2:
                        n = sp.snap(u, min_val=0, max_val=passes * DIGITS * NCH)
                        for m in range(2):
                            for h in range(HG):
                                sp.wait_ge(a_used, n * (2 * HG) + (HG * m + h + 1))
                                sp.dma_start(view(slots[h][:], 0, [[1, HH * CW]]),
                                             plane_part(k.planes[d], c2 * (2 * HG) + (m * HG + h))).then_inc(a_loaded[h], 16)
                        sp.reg_add(u, u, 1)
                with sp.Fori(0, passes):
                    load_plane(0)
                    for d in range(1, DIGITS):
                        with sp.If(planes > d):
                            load_plane(d)
                sp.wait_ge(x_ready, 1)
                sp.dma_start(k.x3_d.rearrange("(b p) f -> p b f", p=P), k.x[:]).then_inc(x_stored, 16)
                sp.wait_ge(x_stored, 16)

            @block.tensor
            def _(pe):
                planes = pe.value_load(k.ctl[0:1, 1:2], min_val=1, max_val=DIGITS)
                u = pe.alloc_register("pairs_pe")
                pe.reg_mov(u, 0)
                pe.sem_inc(a_used, HG)
                pe.sem_inc(summed, 2)

                def body(n, d, c2):
                    for m in range(2):
                        pe.wait_ge(product_copied, n * 2 + (m + 1))
                        for h in range(HG):
                            await_alone(pe, k.passed_pe, a_loaded[h], n * 32 + 16 * (m + 1))
                            for j in range(HH):
                                for w in range(2):
                                    mm = nc.tensor.matmul(prod[m][:, w, 0:HW], parts[:, h * HH + j, :],
                                                          slots[h][:, j, w * HW:(w + 1) * HW].bitcast(FP8),
                                                          start=(h == 0 and j == 0), stop=(h == HG - 1 and j == HH - 1))
                            mm.then_inc(a_used, 1)
                        pe.drain().then_inc(product_ready, 1)
                    for m in range(2):
                        pe.wait_ge(product_copied, n * 2 + (m + 3))
                        pe.wait_ge(taken, n * 2 + (m + 1))
                        for j in range(CB):
                            mm = nc.tensor.matmul(back[m][:, j * D:(j + 1) * D], turned[:, m, j * P:(j + 1) * P],
                                                  select[:, bass.ds(d * D, D)], start=True, stop=True)
                        mm.then_inc(summed, 1)
                with pe.Fori(0, passes) as p:
                    await_alone(pe, k.passed_pe, parts_ready, p + 1)
                    each_chunk(pe, u, planes, body)

            @block.scalar
            def _(act):
                planes = act.value_load(k.ctl[0:1, 1:2], min_val=1, max_val=DIGITS)
                u = act.alloc_register("pairs_act")
                act.reg_mov(u, 0)
                act.sem_inc(product_copied, 2)
                layer_norm(nc, None, act, k, k.x, None, mean, var, (norm_in, norm_out), 1)
                act.wait_ge(norm_in, 2)
                nc.scalar.sqrt(norms[:], norms[:]).then_inc(norm_out, 1)

                def body(n, d, c2):
                    for m in range(2):
                        act.wait_ge(product_ready, n * 2 + (m + 1))
                        act.wait_ge(summed, n * 2 + (m + 1))
                        nc.scalar.copy(view(turned[:], m * CW, [[HW, 2], [1, HW]]),
                                       view(prod[m][:], 0, [[512, 2], [1, HW]])).then_inc(product_copied, 1)
                with act.Fori(0, STEPS):
                    each_chunk(act, u, planes, body)
                layer_norm(nc, None, act, k, k.x, None, mean, var, (norm_in, norm_out), 3)
                each_chunk(act, u, planes, body)
                layer_norm(nc, None, act, k, k.x, None, mean, var, (norm_in, norm_out), 4)

            @block.vector
            def _(dve):
                tt, ts = nc.vector.tensor_tensor, nc.vector.tensor_scalar
                planes = dve.value_load(k.ctl[0:1, 1:2], min_val=1, max_val=DIGITS)
                u = dve.alloc_register("pairs_dve")
                dve.reg_mov(u, 0)
                dve.sem_inc(taken, 2)
                for r in range(3):
                    for d in range(DIGITS):
                        ts(select[r * D:(r + 1) * D, d * D:(d + 1) * D], k.ident[r * D:(r + 1) * D, r * D:(r + 1) * D],
                           float(16 ** d), None, ALU.mult)
                norm = lambda turn: layer_norm(nc, dve, None, k, k.x, f, mean, var, (norm_in, norm_out), turn)
                of_src = view(norms[:], 1, [[2, NB], [0, D]])
                of_dst = view(norms[:], 0, [[2, NB], [0, D]])

                def split():
                    dve.drain()
                    for r in range(3):
                        nc.vector.tensor_copy(parts[:, :, r * D:(r + 1) * D], f[:])
                        if r < 2:
                            dve.drain()
                            tt(f[:], f[:], parts[:, :, r * D:(r + 1) * D], ALU.subtract)
                            dve.drain()
                    nc.vector.memset(agg[:], 0.0)
                    dve.drain().then_inc(parts_ready, 1)

                def body(n, d, c2):
                    for m in range(2):
                        dve.wait_ge(summed, n * 2 + (m + 3))
                        part = view(agg[:], c2 * (2 * CB * D) + m * CB * D, [[1, CB * D]])
                        tt(part, part, back[m][:], ALU.add).then_inc(taken, 1)

                norm(1)
                ts(norms[:], k.small[:], 1.0, None, ALU.max).then_inc(norm_in, 1)
                dve.wait_ge(norm_out, 2)
                nc.vector.reciprocal(norms[:], norms[:])
                ts(tenth[:], k.x[:], ALPHA, None, ALU.mult)
                dve.drain()
                tt(f[:], k.x[:], of_src, ALU.mult)
                split()

                def new_f():
                    dve.drain()
                    tt(agg[:], agg[:], of_dst, ALU.mult)
                    dve.drain()
                    nc.vector.scalar_tensor_tensor(f[:], agg[:], 1.0 - ALPHA, tenth[:], ALU.mult, ALU.add)
                    dve.drain()
                with dve.Fori(0, STEPS - 1):
                    each_chunk(dve, u, planes, body)
                    new_f()
                    tt(f[:], f[:], of_src, ALU.mult)
                    split()
                each_chunk(dve, u, planes, body)
                new_f()
                tt(k.x[:], k.x[:], f[:], ALU.add)
                dve.drain()
                norm(3)
                nc.vector.tensor_copy(f[:], k.x[:])
                split()
                each_chunk(dve, u, planes, body)
                dve.drain()
                tt(k.x[:], k.x[:], agg[:], ALU.add)
                dve.drain()
                norm(4)
                dve.drain().then_inc(x_ready, 1)


def tensor_messages(nc, k, s):
    sb, pb, sem, io = k.sb, k.pb, k.sem, k.io
    U = 8
    y0, c1, c2 = 0.5 / math.sqrt(math.pi), math.sqrt(3 / (4 * math.pi)), 0.5 * math.sqrt(15 / math.pi)
    norm0 = math.sqrt(4 * math.pi) / math.sqrt(2 * U)
    norm1 = math.sqrt(4 * math.pi) * math.sqrt(3) / math.sqrt(4 * U)
    RD = 6 * U * U
    raw = sb("raw_w2", [HID + 1, RD], F32, s)
    w2 = sb("radial_w2", [HID + 1, RD], F32, s)
    w1 = sb("radial_w1", [HID, 2], F32, s)
    edge_w = [sb(f"edge_w{m}", [HID, GE], F32, s) for m in range(2)]
    hid = [sb(f"radial_hidden{m}", [HID + 1, G, EP], F32, s) for m in range(2)]
    idx = [sb(f"m_idx{m}", [EP, G], I32, s) for m in range(2)]
    src = [sb(f"m_src{m}", [EP, G, D], F32, s) for m in range(2)]
    dst = [sb(f"m_dst{m}", [EP, G], F32, s) for m in range(2)]
    kept = [sb(f"m_dst_kept{m}", [EP, G], F32, s) for m in range(2)]
    unit = [sb(f"m_unit{m}", [EP, G, 5], F32, s) for m in range(2)]
    FX = 8 * U
    feat = [sb(f"m_features{m}", [EP, G, FX], F32, s) for m in range(2)]
    cyclic = [sb(f"f1_cyclic{m}", [EP, G, U, 5], F32, s) for m in range(2)]
    pool_t = [sb(f"pool_t{n}", [EP, G, U, 3], F32, s) for n in range(3)]
    CW1, CW0, CWF = 2 * U * U, 2 * U * U, 3 * U * U
    PW = CW1 + CW0 + 2 * CWF
    SUMMED = CW0 + CWF + 3 * U
    prod = [sb(f"m_products{m}", [EP, G, PW], F32, s) for m in range(2)]
    along = sb("m_along", [EP, G, U], F32, s)
    crossed = sb("m_crossed", [EP, G, 3 * U], F32, s)
    nodes = sb("m_nodes", [EP, NPAD], F32, s)
    onehot = [sb(f"m_onehot{m}", [EP, G, P], F32, s) for m in range(3)]
    visit = sb("m_visit", [P, D], F32, s)
    sums = sb("m_sums", [P, NB + 1, D], F32, s)
    zero = sb("m_zero", [1, SUMMED], F32, s)
    mean, var = sb("m_mean", [P, NB], F32, s), sb("m_var", [P, NB], F32, s)

    w_loaded, w_ready = sem("m_w_loaded"), sem("m_w_ready")
    loaded = [sem(f"m_loaded{m}") for m in range(2)]
    idx_loaded = [sem(f"m_idx_loaded{m}") for m in range(2)]
    gathered = [sem(f"m_gathered{m}") for m in range(2)]
    hid_ready, r_ready, r_used = sem("m_hid_ready"), sem("m_r_ready"), sem("m_r_used")
    copied, pool_step, features_ready = sem("m_copied"), sem("m_pool_step"), sem("m_features_ready")
    rows_ready, features_used = sem("m_rows_ready"), sem("m_features_used")
    extra_ready, rows_free = sem("m_extra_ready"), sem("m_rows_free")
    product_done, added = sem("m_product_done"), sem("m_added")
    norm_in, norm_out = sem("m_ln_in"), sem("m_ln_out")
    out_ready, out_stored = sem("m_out_ready"), sem("m_out_stored")
    RB = 2
    NBAT = G // RB

    def blocks(eng, g):
        first = eng.value_load(k.table[0:1, 0, bass.ds(g, 1)], min_val=0, max_val=NB - 1)
        end = eng.value_load(k.table[0:1, 1, bass.ds(g, 1)], min_val=1, max_val=NB)
        return first, end

    with ExitStack() as q:
        r_ps = pb("radial_ps", [EP, 2, RB, 512], F32, q)
        v_ps = pb("m_visit_ps", [P, 4, 512], F32, q)
        with nc.Block() as block:

            @block.gpsimd
            def _(pool):
                def gather(i, m, first):
                    await_alone(pool, k.passed_pool, idx_loaded[m], (i + 1) * 16)
                    if not first:
                        await_alone(pool, k.passed_pool, copied, i * 2 + (m - 1))
                    for j in range(G):
                        pool.indirect_dma_start(src[m][:, j, :], None, k.x3_d,
                                                bass.IndirectOffsetOnAxis(idx[m][:, j:j + 1], 0)).then_inc(gathered[m], 16)

                def features(n, turn, m, first):
                    mul = lambda to, a, b: nc.gpsimd.tensor_tensor(to, a, b, ALU.mult).then_inc(pool_step, 1)
                    shifted = lambda at: view(cyclic[m][:], at, [[5 * U, G], [5, U], [1, 3]])
                    r_o = lambda at: view(unit[m][:], at, [[5, G], [0, U], [1, 3]])
                    await_alone(pool, k.passed_pool, loaded[m], turn * 48)
                    if not first:
                        await_alone(pool, k.passed_pool, features_ready, n)
                    await_alone(pool, k.passed_pool, copied, n + 1)
                    mul(pool_t[0][:], shifted(0), r_o(0))
                    mul(pool_t[1][:], shifted(2), r_o(1))
                    mul(pool_t[2][:], shifted(1), r_o(2))
                    part = lambda i: view(pool_t[0][:], i, [[3 * U, G], [3, U]])
                    s_out = view(feat[m][:], U, [[FX, G], [1, U]])
                    await_alone(pool, k.passed_pool, pool_step, n * 5 + 3)
                    nc.gpsimd.tensor_tensor(s_out, part(0), part(1), ALU.add).then_inc(pool_step, 1)
                    nc.gpsimd.tensor_tensor(view(feat[m][:], 5 * U, [[FX, G], [3, U], [1, 3]]), pool_t[1][:], pool_t[2][:],
                                            ALU.subtract).then_inc(pool_step, 1)
                    await_alone(pool, k.passed_pool, pool_step, n * 5 + 5)
                    nc.gpsimd.tensor_tensor(s_out, s_out, part(2), ALU.add).then_inc(features_ready, 1)
                gather(0, 0, True)
                gather(0, 1, True)
                features(0, 1, 0, True)
                with pool.Fori(1, PAIRS) as i:
                    gather(i, 0, False)
                    features(i * 2 - 1, i, 1, False)
                    gather(i, 1, False)
                    features(i * 2, i + 1, 0, False)
                features(NG - 1, PAIRS, 1, False)

            @block.sync
            def _(sp):
                sp.dma_start(raw[0:HID, :], io["L3_gnn_w2"]).then_inc(w_loaded, 16)
                sp.dma_start(raw[HID:HID + 1, :], io["L3_gnn_b2"].rearrange("(o n) -> o n", o=1)).then_inc(w_loaded, 16)
                sp.dma_start(w1[:, 0:1], io["L3_gnn_w1"].rearrange("o n -> n o")).then_inc(w_loaded, 16)
                sp.dma_start(w1[:, 1:2], io["L3_gnn_b1"].rearrange("(n o) -> n o", o=1)).then_inc(w_loaded, 16)

                def load(i, m, first):
                    g = i * 2 + m
                    if not first:
                        sp.wait_ge(gathered[m], i * (16 * G))
                    sp.dma_start(idx[m][:], k.idx_view[bass.ds(g, 1), :, :].rearrange("a p j -> (a p) j")).then_inc(idx_loaded[m], 16)
                    if not first:
                        sp.wait_ge(hid_ready, g - 1)
                        sp.wait_ge(rows_ready, g - 1)
                    part = lambda a: a[bass.ds(g, 1), :, :].rearrange("a p c -> (a p) c")
                    sp.dma_start(edge_w[m][:], bass.AP(io["edge_weight"].tensor, g * GE, [[0, HID], [1, GE]])).then_inc(loaded[m], 16)
                    sp.dma_start(dst[m][:], part(k.dst_d.rearrange("(g p c) -> g p c", p=EP, c=G))).then_inc(loaded[m], 16)
                    sp.dma_start(view(unit[m][:], 0, [[1, 5 * G]]),
                                 part(k.dir_d.rearrange("(g p c) t -> g p (c t)", p=EP, c=G))).then_inc(loaded[m], 16)
                for m in range(2):
                    load(0, m, True)
                with sp.Fori(1, PAIRS) as i:
                    for m in range(2):
                        load(i, m, False)
                sp.wait_ge(out_ready, 1)
                full = (NB - 1) * P
                sp.dma_start(k.out[0:full, :].rearrange("(b p) f -> p b f", p=P), k.x[:, 0:NB - 1, :]).then_inc(out_stored, 16)
                sp.dma_start(k.out[full:N, :], k.x[0:LAST, NB - 1, :]).then_inc(out_stored, 16)
                sp.wait_ge(out_stored, 32)

            @block.scalar
            def _(act):
                act.wait_ge(w_loaded, 64)
                act.wait_ge(w_ready, 1)

                def group(i, m, first):
                    n = i * 2 + m
                    act.wait_ge(loaded[m], (i + 1) * 48)
                    if not first:
                        act.wait_ge(r_ready, n * NBAT - NBAT)
                    nc.scalar.activation(hid[m][0:HID, :, :], view(edge_w[m][:], 0, [[1, G], [G, EP]]), ACT.Relu,
                                         bias=w1[:, 1:2], scale=w1[:, 0:1]).then_inc(hid_ready, 1)
                    act.wait_ge(gathered[m], (i + 1) * (16 * G))
                    if not first:
                        act.wait_ge(features_used, n - 1)
                    f1 = view(src[m][:], U, [[D, G], [3, U], [1, 3]])
                    nc.scalar.copy(feat[m][:, :, 0:U], src[m][:, :, 0:U])
                    nc.scalar.copy(feat[m][:, :, 2 * U:5 * U], src[m][:, :, U:D])
                    nc.scalar.copy(cyclic[m][:, :, :, 0:3], f1)
                    nc.scalar.copy(cyclic[m][:, :, :, 3:5], view(src[m][:], U, [[D, G], [3, U], [1, 2]])).then_inc(copied, 1)
                for m in range(2):
                    group(0, m, True)
                with act.Fori(1, PAIRS) as i:
                    for m in range(2):
                        group(i, m, False)
                layer_norm(nc, None, act, k, k.x, None, mean, var, (norm_in, norm_out), 1)

            @block.tensor
            def _(pe):
                pe.wait_ge(w_ready, 2)
                count, extras = pe.alloc_register("m_visits_pe"), pe.alloc_register("m_extras_pe")
                pe.reg_mov(count, 0)
                pe.reg_mov(extras, 0)
                for bank in (2, 3):
                    nc.tensor.matmul(v_ps[:, bank, 0:SUMMED], zero[0:1, 0:P], zero[0:1, :],
                                     start=True, stop=True).then_inc(product_done, 1)

                def radial(n, m, first):
                    pe.wait_ge(hid_ready, n + 1)
                    for b in range(NBAT):
                        half = (m * NBAT + b) % 2
                        if not (first and b < 2):
                            pe.wait_ge(r_used, n * NBAT + (b - 1))
                        for t in range(RB):
                            mm = nc.tensor.matmul(r_ps[:, half, t, 0:RD], hid[m][:, b * RB + t, :], w2[:], start=True, stop=True)
                        mm.then_inc(r_ready, 1)

                def product(one, m):
                    v = pe.snap(count, min_val=0, max_val=NG * NB)
                    await_alone(pe, k.passed_pe, added, v + 1)
                    for j in range(G):
                        mm = nc.tensor.matmul(view(v_ps[:], (v % 4) * 512, [[1, SUMMED]]), onehot[one][:, j, :],
                                              prod[m][:, j, CW1:CW1 + SUMMED], start=(j == 0), stop=(j == G - 1))
                    mm.then_inc(product_done, 1)
                    pe.reg_add(count, count, 1)

                def segment_sums(n, m):
                    pe.wait_ge(rows_ready, n + 1)
                    product(m, m)
                    first, end = blocks(pe, n)
                    with pe.If(end - first > 1):
                        with pe.Fori(first + 1, end):
                            x = pe.snap(extras, min_val=0, max_val=NG * NB)
                            pe.wait_ge(extra_ready, x + 1)
                            pe.reg_add(extras, extras, 1)
                            product(2, m)
                    pe.drain().then_inc(rows_free, 1)
                radial(0, 0, True)

                def group(n, m):
                    radial(n, m, False)
                    segment_sums(n - 1, 1 - m)
                group(1, 1)
                with pe.Fori(1, PAIRS) as i:
                    for m in range(2):
                        group(i * 2 + m, m)
                segment_sums(NG - 1, 1)

            @block.vector
            def _(dve):
                tt, ts, red = nc.vector.tensor_tensor, nc.vector.tensor_scalar, nc.vector.tensor_reduce
                for a in hid:
                    nc.vector.memset(a[:], 1.0)
                dve.drain().then_inc(w_ready, 1)
                dve.wait_ge(w_loaded, 64)
                s1 = norm1 * c1 / math.sqrt(3)
                k2 = norm1 * c2 / math.sqrt(10)
                uv = lambda at, step: view(raw[:], at, [[step * U, U], [step, U]])
                to = lambda part, half: view(w2[:], part * 2 * U * U + half * U, [[2 * U, U], [1, U]])
                for part, half, frm, scale in (
                        (1, 0, uv(0, 1), norm0 * y0), (1, 1, uv(U * U, 1), norm0 * c1 / math.sqrt(3)),
                        (0, 0, uv(2 * U * U, 1), s1), (0, 1, uv(3 * U * U + 2, 3), k2),
                        (2, 0, uv(3 * U * U, 3), norm1 * y0 / math.sqrt(3)), (2, 1, uv(3 * U * U + 1, 3), norm1 * c1 / math.sqrt(6))):
                    ts(to(part, half), frm, scale, None, ALU.mult)
                dve.drain()
                nc.vector.scalar_tensor_tensor(to(2, 0), uv(3 * U * U + 2, 3), -k2 / 3, to(2, 0), ALU.mult, ALU.add)
                nc.vector.memset(zero[:], 0.0)
                nc.vector.memset(sums[:], 0.0)
                nc.vector.tensor_copy(nodes[:, 0:P], k.iota[0:EP, :])
                with dve.Fori(1, NB) as b:
                    dve.drain()
                    ts(nodes[:, bass.ds(b * P, P)], nodes[:, bass.ds(b * P - P, P)], float(P), None, ALU.add)
                dve.drain().then_inc(w_ready, 1)
                dve.sem_inc(added, 2)
                names = ("m_visits_dve", "m_block_1", "m_block_2", "m_extra_used", "m_first", "m_end")
                count, block_1, block_2, extra_used, first_r, end_r = (dve.alloc_register(x) for x in names)
                dve.reg_mov(count, 0)
                dve.reg_mov(block_1, NB)
                dve.reg_mov(block_2, NB)
                dve.reg_mov(extra_used, 2)

                def add(v):
                    at = dve.snap(block_2, min_val=0, max_val=NB)
                    bank = ((v + 2) % 4) * 512
                    dve.drain()
                    await_alone(dve, k.passed_dve, product_done, v + 1)
                    red(visit[:, 0:U], view(v_ps[:], bank, [[2 * U, U], [1, 2 * U]]), AX.X, ALU.add)
                    red(visit[:, U:D], view(v_ps[:], bank + CW0, [[1, 3 * U], [3 * U, U + 1]]), AX.X, ALU.add)
                    dve.drain()
                    part = view(sums[:], at * D, [[1, D]])
                    tt(part, part, visit[:], ALU.add).then_inc(added, 1)
                    dve.reg_mov(block_2, block_1)

                def one_hot(to, m, b):
                    return tt(to[:], view(kept[m][:], 0, [[1, G], [0, P]]), view(nodes[:], b * P, [[0, G], [1, P]]), ALU.is_equal)

                def visits(m):
                    add(dve.snap(count, min_val=0, max_val=NG * NB))
                    dve.reg_mov(block_1, first_r)
                    dve.reg_add(count, count, 1)
                    block, end = dve.snap(first_r, min_val=0, max_val=NB - 1), dve.snap(end_r, min_val=1, max_val=NB)
                    with dve.If(end - block > 1):
                        with dve.Fori(block + 1, end) as b:
                            v = dve.snap(count, min_val=0, max_val=NG * NB)
                            dve.wait_ge(product_done, dve.snap(extra_used, min_val=2, max_val=NG * NB))
                            one_hot(onehot[2], m, b).then_inc(extra_ready, 1)
                            add(v)
                            dve.reg_mov(block_1, b)
                            dve.reg_mov(extra_used, v)
                            dve.reg_add(extra_used, extra_used, 3)
                            dve.reg_add(count, count, 1)

                def group(i, m, first):
                    n = i * 2 + m
                    fe = feat[m][:]
                    dve.drain()
                    dve.wait_ge(loaded[m], (i + 1) * 48)
                    nc.vector.tensor_copy(kept[m][:], dst[m][:])
                    dve.wait_ge(features_ready, n + 1)
                    if not first:
                        dve.wait_ge(rows_free, n - 1)
                    for b in range(NBAT):
                        t0 = b * RB
                        at = ((m * NBAT + b) % 2) * RB * 512
                        dve.wait_ge(r_ready, n * NBAT + (b + 1))
                        tt(view(prod[m][:], t0 * PW, [[PW, RB], [2 * U, 2 * U], [1, 2 * U]]),
                           view(r_ps[:], at, [[512, RB], [2 * U, 2 * U], [1, 2 * U]]),
                           view(fe, t0 * FX, [[FX, RB], [0, 2 * U], [1, 2 * U]]), ALU.mult)
                        for t in range(RB):
                            mul = tt(view(prod[m][:], (t0 + t) * PW + CW1 + CW0, [[3, U], [1, 3], [3 * U, 2 * U]]),
                                     view(r_ps[:], at + 512 * t + 4 * U * U, [[2 * U, U], [0, 3], [1, 2 * U]]),
                                     view(fe, (t0 + t) * FX + 2 * U, [[0, U], [1, 3], [3, 2 * U]]), ALU.mult)
                        mul.then_inc(r_used, 1)
                    table_first, table_end = blocks(dve, n)
                    dve.drain().then_inc(features_used, 1)
                    if not (first and m == 0):
                        visits(1 - m)
                    dve.reg_mov(first_r, table_first)
                    dve.reg_mov(end_r, table_end)
                    red(along[:], view(prod[m][:], 0, [[PW, G], [2 * U, U], [1, 2 * U]]), AX.X, ALU.add)
                    red(crossed[:], view(prod[m][:], CW1 + CW0 + CWF, [[PW, G], [1, 3 * U], [3 * U, U]]), AX.X, ALU.add)
                    one_hot(onehot[m], m, dve.snap(first_r, min_val=0, max_val=NB - 1))
                    dve.drain()
                    ready = view(prod[m][:], CW1 + CW0 + CWF, [[PW, G], [3, U], [1, 3]])
                    tt(ready, view(along[:], 0, [[U, G], [1, U], [0, 3]]), view(unit[m][:], 0, [[5, G], [0, U], [1, 3]]), ALU.mult)
                    dve.drain()
                    ready = view(prod[m][:], CW1 + CW0 + CWF, [[PW, G], [1, 3 * U]])
                    tt(ready, ready, crossed[:], ALU.add).then_inc(rows_ready, 1)
                group(0, 0, True)
                group(0, 1, True)
                with dve.Fori(1, PAIRS) as i:
                    for m in range(2):
                        group(i, m, False)
                visits(1)
                for last in range(2):
                    add(dve.snap(count, min_val=0, max_val=NG * NB))
                    dve.reg_mov(block_1, NB)
                    dve.reg_add(count, count, 1)
                dve.drain()
                tt(k.x[:], k.x[:], sums[:, 0:NB, :], ALU.add)
                dve.drain()
                layer_norm(nc, dve, None, k, k.x, sums[:, 0:NB, :], mean, var, (norm_in, norm_out), 1)
                dve.drain().then_inc(out_ready, 1)


_INPUTS = ["x", "src", "dst", "edge_attr_16", "edge_attr_3", "edge_weight",
           "L0_gnn_w1a", "L0_gnn_b1a", "L0_gnn_w1b", "L0_gnn_b1b", "L0_gnn_w2a", "L0_gnn_b2a", "L0_gnn_w2b", "L0_gnn_b2b",
           "L3_gnn_w1", "L3_gnn_b1", "L3_gnn_w2", "L3_gnn_b2"]


def kernel(**inputs):
    import numpy as np
    import concourse.bacc as bacc
    from concourse.bass_utils import run_bass_kernel_spmd

    nc = bacc.Bacc("TRN2", target_bir_lowering=False, num_devices=1)
    arrays, io = {}, {}
    for name in _INPUTS:
        a = np.ascontiguousarray(inputs[name])
        arrays[f"in_{name}"] = a
        io[name] = nc.dram_tensor(f"in_{name}", a.shape, mybir.dt.from_np(a.dtype), kind="ExternalInput").ap()
    out = nc.dram_tensor("out_x", (N, D), F32, kind="ExternalOutput").ap()
    build(nc, io, out)
    result = run_bass_kernel_spmd(nc, [arrays], core_ids=[0])
    return result.results[0]["out_x"]
```

```python
import math

import concourse.bass as bass
from concourse import mybir
from contextlib import ExitStack

F32 = mybir.dt.float32
BF16 = mybir.dt.bfloat16
FP8 = mybir.dt.float8e4
I32 = mybir.dt.int32
U8 = mybir.dt.uint8
ALU = mybir.AluOpType
ACT = mybir.ActivationFunctionType
AX = mybir.AxisListType

N, E, D = 12500, 412500, 32
P = 128
NB = (N + P - 1) // P
NPAD = NB * P
LAST = N - (NB - 1) * P
EP = 125
COLS = E // EP
G = 10
GE = G * EP
NG = E // GE
PAIRS = NG // 2
DE, DI, DH = 16, 48, 96
HID = 64
STEPS, ALPHA = 10, 0.1
EPS = 1e-5

CB = 7
CW = CB * P
HW = CW // 2
NCH = NB // CB
HH = 14
HG = NB // HH
PLANE = NCH * HG * P * HH * CW
SPARE = -(-PLANE // (1 << 19)) << 19
DIGITS = 5
BATCH = 30
KPAD = EP * (COLS + 20)
NODE_BITS = 14
DST_MASK = (1 << NODE_BITS) - 1
DIV_CB = (9363, 16)
DIV_HH = (4682, 16)
TESTS = [48, 64, 128, 512, 2048, 8192, 32768, 131072]
NT = len(TESTS)


def view(ap, offset, dims):
    return bass.AP(ap.tensor, ap.offset + offset, [list(ap.ap[0])] + [list(d) for d in dims])


def plane_part(plane, u):
    parts = plane[0:PLANE, :].rearrange("(u p n) o -> u p (n o)", u=NCH * HG, p=P)
    return parts[bass.ds(u, 1), :, :].rearrange("a p n -> (a p) n")


def await_alone(eng, passed, sem, value):
    eng.wait_ge(sem, value)
    eng.sem_inc(passed, 1)


class Build:
    pass


def build(nc, io, out):
    ctx = ExitStack()
    with ctx:
        k = Build()
        k.io, k.out = io, out

        def sem(name):
            return ctx.enter_context(nc.semaphore(name))

        def sb(name, shape, dt, stack=ctx):
            return stack.enter_context(nc.sbuf_tensor(name, shape, dt))

        def pb(name, shape, dt, stack):
            return stack.enter_context(nc.psum_tensor(name, shape, dt))

        k.sem, k.sb, k.pb = sem, sb, pb

        def dram(name, shape, dt):
            return nc.dram_tensor(name, shape, dt, kind="Internal").ap()

        k.planes = [dram(f"multiplicity_digit{d}", (SPARE + E, 1), U8) for d in range(DIGITS)]
        k.keys_d = dram("edge_keys", (KPAD + E + KPAD,), I32)
        k.dst_d = dram("dst_float", (E,), F32)
        k.hist_d = dram("src_split", (E, 2), BF16)
        k.xin_d = dram("edge_inputs", (NG, EP, G * DI), F32)
        k.dir_d = dram("edge_directions", (E, 5), F32)
        k.range_d = dram("block_ranges", (2, NG), I32)
        k.x3_d = dram("x_after_layer3", (NPAD, D), F32)

        k.passed_pool, k.passed_pe, k.passed_dve = sem("passed_pool"), sem("passed_pe"), sem("passed_dve")

        k.x = sb("x", [P, NB, D], F32)
        k.iota = sb("iota", [P, P], F32)
        k.ident = sb("ident", [P, P], F32)
        k.ctl = sb("ctl", [1, 8], I32)
        k.table = sb("block_table", [1, 2, NG], I32)
        k.small = sb("small", [P, NB, 2], F32)

        with ExitStack() as scatter_data:
            k.index = sb("scatter_index", [EP, COLS], I32, scatter_data)
            k.digit = sb("scatter_digit", [EP, DIGITS, COLS], U8, scatter_data)
            with ExitStack() as s:
                prepare(nc, k, s)
            with ExitStack() as s:
                edge_network(nc, k, s)
        with ExitStack() as s:
            propagate(nc, k, s)
        with ExitStack() as s:
            tensor_messages(nc, k, s)


def prepare(nc, k, s):
    sb, pb, sem, io = k.sb, k.pb, k.sem, k.io
    iota_i = sb("iota_i", [P, 2, P], I32, s)
    pcol = sb("pcol", [P, 1], F32, s)
    dst = sb("dst_i", [EP, COLS], I32, s)
    src = sb("src_i", [EP, COLS], I32, s)
    key = sb("key", [EP, COLS], I32, s)
    ta = sb("ta", [EP, COLS], I32, s)
    tb = sb("tb", [EP, COLS], I32, s)
    near = [sb(f"near_keys{n}", [EP, COLS], I32, s) for n in range(2)]
    zeros = sb("zeros_u8", [P, HH * CW], U8, s)
    minus = view(view(k.digit[:], 0, [[1, DIGITS * COLS]]).bitcast(I32), 0, [[1, KPAD // EP]])
    mult = view(ta[:], 0, [[1, COLS]]).bitcast(F32)
    behind = src[:].bitcast(F32)
    number = dst
    tests = sb("tests", [P, 16], F32, s)
    row = sb("row", [16, 32], F32, s)
    weights = sb("weights", [1, 16], F32, s)
    GR = 3
    RP = NG // GR
    dst_g = sb("dst_g", [RP, GR, GE], I32, s)
    rng = sb("rng", [RP, 2, GR], F32, s)
    rng_i = sb("rng_i", [RP, 2, GR], I32, s)
    idx = [sb(f"l0_idx{m}", [EP, G], I32, s) for m in range(2)]
    ea = [sb(f"l0_ea{m}", [EP, G, DE], F32, s) for m in range(2)]
    xin = [sb(f"l0_xin{m}", [EP, G, DI], F32, s) for m in range(2)]
    tp = pb("prep_ps", [16, P], F32, s)

    edges_loaded, ranges_loaded, x_loaded = sem("edges_loaded"), sem("ranges_loaded"), sem("x_loaded")
    iota_done, const_done, x_zero = sem("iota_done"), sem("const_done"), sem("x_zero")
    minus_ready, minus_stored = sem("minus_ready"), sem("minus_stored")
    zero_ready, planes_zeroed = sem("zero_ready"), sem("planes_zeroed")
    key_ready, key_stored = sem("key_ready"), sem("key_stored")
    packed_ready, packed_stored = sem("packed_ready"), sem("packed_stored")
    near_loaded = [sem(f"near_loaded{n}") for n in range(2)]
    near_used = sem("near_used")
    rng_ready, rng_stored, rng_back = sem("rng_ready"), sem("rng_stored"), sem("rng_back")
    tests_ready, tests_turned, best_ready, best_turned = (sem(x) for x in (
        "tests_ready", "tests_turned", "best_ready", "best_turned"))
    bound_ready = sem("bound_ready")
    idx_loaded = [sem(f"idx_loaded{m}") for m in range(2)]
    ea_loaded = [sem(f"ea_loaded{m}") for m in range(2)]
    gathered = [sem(f"gathered{m}") for m in range(2)]
    xin_stored = [sem(f"xin_stored{m}") for m in range(2)]
    ea_copied, dst_used = sem("ea_copied"), sem("dst_used")

    resident = lambda a: a.rearrange("(p c) -> p c", p=EP)
    k.idx_view = io["src"].rearrange("(g p j) -> g p j", p=EP, j=G)
    ea_view = io["edge_attr_16"].rearrange("(g p j) f -> g p (j f)", p=EP, j=G)

    with nc.Block() as block:

        @block.sync
        def _(sp):
            sp.dma_start(dst[:], resident(io["dst"])).then_inc(edges_loaded, 16)
            sp.dma_start(src[:], resident(io["src"])).then_inc(edges_loaded, 16)
            sp.dma_start(dst_g[:], io["dst"].rearrange("(p g c) -> p g c", p=RP, g=GR)).then_inc(ranges_loaded, 16)
            sp.wait_ge(minus_ready, 1)
            for at in (0, KPAD + E):
                sp.dma_start(k.keys_d[at:at + KPAD].rearrange("(p c) -> p c", p=EP), minus).then_inc(minus_stored, 16)
            sp.wait_ge(x_zero, 1)
            full = (NB - 1) * P
            sp.dma_start(k.x[:, 0:NB - 1, :], io["x"][0:full, :].rearrange("(b p) f -> p b f", p=P)).then_inc(x_loaded, 16)
            sp.dma_start(k.x[0:LAST, NB - 1, :], io["x"][full:N, :]).then_inc(x_loaded, 16)
            sp.wait_ge(key_ready, 1)
            sp.dma_start(resident(k.keys_d[KPAD:KPAD + E]), key[:]).then_inc(key_stored, 16)
            sp.wait_ge(packed_ready, 1)
            sp.dma_start(resident(k.dst_d), near[0][:].bitcast(F32)).then_inc(packed_stored, 16)
            sp.wait_ge(packed_ready, 2)
            sp.dma_start(k.hist_d.rearrange("(p c) t -> p (c t)", p=EP), near[1][:].bitcast(BF16)).then_inc(packed_stored, 16)
            sp.wait_ge(rng_ready, 1)
            sp.dma_start(k.range_d.rearrange("t (p g) -> p t g", g=GR), rng_i[:]).then_inc(rng_stored, 16)
            sp.wait_ge(rng_stored, 16)
            for t in range(2):
                sp.dma_start(k.table[0:1, t, :], k.range_d[t:t + 1, :]).then_inc(rng_back, 16)
            sp.wait_ge(x_loaded, 32)
            sp.wait_ge(rng_back, 32)
            sp.wait_ge(key_stored, 16)
            sp.wait_ge(minus_stored, 32)
            sp.wait_ge(packed_stored, 32)
            for n, far in enumerate(TESTS + [1]):
                if n >= 2:
                    sp.wait_ge(near_used, n - 1)
                sp.dma_start(near[n % 2][:], resident(k.keys_d[KPAD + far:KPAD + far + E])).then_inc(near_loaded[n % 2], 16)
            sp.wait_ge(bound_ready, 1)
            bound = sp.value_load(k.ctl[0:1, 0:1], min_val=2, max_val=E)
            sp.wait_ge(near_used, NT + 1)
            with sp.Fori(1, bound + 1) as far:
                for n in range(2):
                    if n == 0:
                        at = far * -1 + KPAD
                    else:
                        at = far + KPAD
                    sp.wait_ge(near_used, far * 2 + (NT - 2 + n))
                    sp.dma_start(near[n][:], resident(k.keys_d[bass.ds(at, E)])).then_inc(near_loaded[n], 16)

        @block.gpsimd
        def _(pool):
            pool.iota(iota_i[:, 0, :], [[1, P]], base=0, channel_multiplier=0).then_inc(iota_done, 1)
            pool.iota(iota_i[:, 1, 0:1], [[0, 1]], base=0, channel_multiplier=1).then_inc(iota_done, 1)
            def gather(i, m, first):
                n = i + 1
                await_alone(pool, k.passed_pool, idx_loaded[m], n * 16)
                if not first:
                    await_alone(pool, k.passed_pool, xin_stored[m], i * 16)
                for j in range(G):
                    pool.indirect_dma_start(xin[m][:, j, 0:D], None, io["x"],
                                            bass.IndirectOffsetOnAxis(idx[m][:, j:j + 1], 0)).then_inc(gathered[m], 16)
            for m in range(2):
                gather(0, m, True)
            with pool.Fori(1, PAIRS // 4) as i:
                for m in range(2):
                    gather(i, m, False)
            pool.wait_ge(dst_used, 1)
            pool.iota(number[:], [[1, COLS]], base=0, channel_multiplier=COLS).then_inc(iota_done, 1)
            with pool.Fori(PAIRS // 4, PAIRS) as i:
                for m in range(2):
                    gather(i, m, False)

        @block.scalar
        def _(act):
            def load(i, m):
                act.dma_start(idx[m][:], k.idx_view[bass.ds(i * 2 + m, 1), :, :].rearrange("a p j -> (a p) j")).then_inc(idx_loaded[m], 16)
                act.dma_start(view(ea[m][:], 0, [[1, G * DE]]), ea_view[bass.ds(i * 2 + m, 1), :, :].rearrange("a p j -> (a p) j")).then_inc(ea_loaded[m], 16)

            def group(i, m, first, last):
                if not (last and m == 1):
                    load(i + m, 1 - m)
                if not first:
                    act.wait_ge(xin_stored[m], i * 16)
                act.wait_ge(ea_loaded[m], (i + 1) * 16)
                nc.scalar.copy(xin[m][:, :, D:DI], ea[m][:]).then_inc(ea_copied, 1)
                act.wait_ge(gathered[m], (i + 1) * (16 * G))
                act.wait_ge(ea_copied, i * 2 + (m + 1))
                act.dma_start(k.xin_d[bass.ds(i * 2 + m, 1), :, :].rearrange("a p j -> (a p) j"),
                              view(xin[m][:], 0, [[1, G * DI]])).then_inc(xin_stored[m], 16)

            load(0, 0)
            for m in range(2):
                group(0, m, True, False)
            act.wait_ge(zero_ready, 1)
            with act.Fori(1, NCH * HG + 1) as i:
                for m in range(2):
                    group(i, m, False, False)
                act.dma_start(plane_part(k.planes[0], i - 1), zeros[:]).then_inc(planes_zeroed, 16)
            with act.Fori(NCH * HG + 1, PAIRS - 1) as i:
                for m in range(2):
                    group(i, m, False, False)
            for m in range(2):
                group(PAIRS - 1, m, False, True)
            for m in range(2):
                act.wait_ge(xin_stored[m], PAIRS * 16)
            act.wait_ge(planes_zeroed, NCH * HG * 16)

        @block.vector
        def _(dve):
            ts, tt = nc.vector.tensor_scalar, nc.vector.tensor_tensor
            nc.vector.memset(k.x[:, NB - 1, :], 0.0).then_inc(x_zero, 1)
            nc.vector.memset(minus, -1).then_inc(minus_ready, 1)
            nc.vector.memset(zeros[:].bitcast(I32), 0).then_inc(zero_ready, 1)
            nc.vector.memset(tests[:], 0.0)
            dve.wait_ge(iota_done, 2)
            nc.vector.tensor_copy(pcol[:], iota_i[:, 1, 0:1])
            nc.vector.tensor_copy(k.iota[:], iota_i[:, 0, :])
            dve.drain()
            ts(k.ident[:], k.iota[:], pcol[:, 0:1], None, ALU.is_equal)
            dve.wait_ge(edges_loaded, 32)
            ts(tb[:], src[:], NODE_BITS, None, ALU.logical_shift_left)
            dve.drain()
            tt(key[:], tb[:], dst[:], ALU.bitwise_or).then_inc(key_ready, 1)
            nc.vector.tensor_copy(near[0][:].bitcast(F32), dst[:]).then_inc(packed_ready, 1)
            pair = view(near[1][:].bitcast(BF16), 0, [[2, COLS]])
            pair_hi = view(near[1][:].bitcast(BF16), 1, [[2, COLS]])
            dve.drain()
            ts(tb[:], src[:], P - 1, None, ALU.bitwise_and)
            ts(ta[:], src[:], 7, None, ALU.logical_shift_right)
            dve.drain()
            nc.vector.tensor_copy(pair, tb[:])
            nc.vector.tensor_copy(pair_hi, ta[:])
            dve.drain().then_inc(packed_ready, 1)
            per_c = HG * P * HH * CB - CB
            per_h = P * HH * CB - HH * CB
            q = k.index
            ts(q[:], tb[:], float(HH * CB), None, ALU.mult)
            dve.drain()
            nc.vector.scalar_tensor_tensor(q[:], ta[:], float(CB), q[:], ALU.mult, ALU.add)
            dve.drain()
            ts(ta[:], ta[:], float(DIV_HH[0]), None, ALU.mult)
            dve.drain()
            ts(ta[:], ta[:], DIV_HH[1], None, ALU.logical_shift_right)
            dve.drain()
            nc.vector.scalar_tensor_tensor(q[:], ta[:], float(per_h), q[:], ALU.mult, ALU.add)
            dve.drain()
            ts(tb[:], dst[:], 7, None, ALU.logical_shift_right)
            dve.drain()
            tt(q[:], q[:], tb[:], ALU.add)
            dve.drain()
            ts(ta[:], tb[:], float(DIV_CB[0]), None, ALU.mult)
            dve.drain()
            ts(ta[:], ta[:], DIV_CB[1], None, ALU.logical_shift_right)
            dve.drain()
            nc.vector.scalar_tensor_tensor(q[:], ta[:], float(per_c), q[:], ALU.mult, ALU.add)
            dve.drain()
            ts(tb[:], dst[:], P - 1, None, ALU.bitwise_and)
            dve.drain()
            ts(q[:], q[:], 7, None, ALU.logical_shift_left)
            dve.drain()
            tt(q[:], q[:], tb[:], ALU.bitwise_or)
            dve.wait_ge(ranges_loaded, 16)
            nc.vector.tensor_reduce(rng[:, 0, :], dst_g[:], AX.X, ALU.min)
            nc.vector.tensor_reduce(rng[:, 1, :], dst_g[:], AX.X, ALU.max)
            dve.drain()
            nc.vector.tensor_copy(rng_i[:], rng[:])
            dve.drain()
            ts(rng_i[:], rng_i[:], 7, None, ALU.logical_shift_right)
            dve.drain()
            ts(rng_i[:, 1, :], rng_i[:, 1, :], 1.0, None, ALU.add).then_inc(rng_ready, 1)
            for n in range(NT + 1):
                b = near[n % 2]
                dve.wait_ge(near_loaded[n % 2], 16 * (n // 2 + 1))
                dve.drain()
                if n < NT:
                    tt(tb[:], key[:], b[:], ALU.bitwise_xor).then_inc(near_used, 1)
                    dve.drain()
                    ts(tb[:], tb[:], DST_MASK, None, ALU.bitwise_and)
                    dve.drain()
                else:
                    ts(ta[:], b[:], DST_MASK, None, ALU.bitwise_and).then_inc(near_used, 1)
                    dve.drain()
                    tt(tb[:], ta[:], dst[:], ALU.subtract)
                    dve.drain()
                nc.vector.tensor_reduce(tests[0:EP, n:n + 1], tb[:], AX.X, ALU.min)
            dve.drain()
            nc.vector.memset(behind, 0.0).then_inc(dst_used, 1)
            ts(tests[0:EP, 0:NT], tests[0:EP, 0:NT], 0.0, None, ALU.is_equal)
            ts(tests[0:EP, NT:NT + 1], tests[0:EP, NT:NT + 1], 0.0, None, ALU.is_lt).then_inc(tests_ready, 1)
            for n in range(NT):
                step = (TESTS + [E])[n + 1] - TESTS[n]
                nc.vector.memset(weights[0:1, n:n + 1], float(step))

            def over_partitions(n, count):
                dve.wait_ge(tests_turned, n)
                nc.vector.tensor_reduce(row[0:count, 16:17], tp[0:count, :], AX.X, ALU.max).then_inc(best_ready, 1)
                dve.wait_ge(best_turned, n)
            dve.drain()
            over_partitions(1, NT + 1)
            tt(row[0:1, 0:NT], tp[0:1, 0:NT], weights[0:1, 0:NT], ALU.mult)
            ts(row[0:1, NT:NT + 1], tp[0:1, NT:NT + 1], float(E), None, ALU.mult)
            dve.drain()
            nc.vector.tensor_reduce(row[0:1, NT + 1:NT + 2], row[0:1, 0:NT], AX.X, ALU.add)
            dve.drain()
            ts(row[0:1, NT + 1:NT + 2], row[0:1, NT + 1:NT + 2], float(TESTS[0]), None, ALU.add)
            dve.drain()
            tt(row[0:1, NT + 1:NT + 2], row[0:1, NT + 1:NT + 2], row[0:1, NT:NT + 1], ALU.max)
            dve.drain()
            nc.vector.tensor_copy(k.ctl[0:1, 0:1], row[0:1, NT + 1:NT + 2]).then_inc(bound_ready, 1)
            dve.drain()
            nc.vector.memset(mult, 1.0)
            dve.wait_ge(bound_ready, 1)
            bound = dve.value_load(k.ctl[0:1, 0:1], min_val=2, max_val=E)
            seen = [(NT + 2) // 2, (NT + 1) // 2]
            with dve.Fori(1, bound + 1) as far:
                for n in range(2):
                    dve.drain()
                    dve.wait_ge(near_loaded[n], (far + seen[n]) * 16)
                    tt(tb[:], key[:], near[n][:], ALU.bitwise_xor).then_inc(near_used, 1)
                    dve.drain()
                    same = behind if n == 0 else mult
                    nc.vector.scalar_tensor_tensor(same, tb[:], 0.0, same, ALU.is_equal, ALU.add)
            dve.drain()
            tt(mult, mult, behind, ALU.add)
            dve.wait_ge(iota_done, 3)
            ts(tb[:], behind, 0.0, -1.0, ALU.is_gt, ALU.mult)
            dve.drain()
            ts(number[:], number[:], SPARE, None, ALU.bitwise_or)
            dve.drain()
            tt(number[:], number[:], tb[:], ALU.bitwise_and)
            dve.drain()
            ts(tb[:], tb[:], -1, None, ALU.bitwise_xor)
            dve.drain()
            tt(q[:], q[:], tb[:], ALU.bitwise_and)
            dve.drain()
            tt(q[:], q[:], number[:], ALU.bitwise_or)
            dve.drain()
            nc.vector.tensor_reduce(tests[0:EP, 0:1], mult, AX.X, ALU.max).then_inc(tests_ready, 1)
            over_partitions(2, 1)
            nc.vector.memset(row[0:1, 0:1], 1.0)
            for d in range(1, DIGITS):
                dve.drain()
                nc.vector.scalar_tensor_tensor(row[0:1, 0:1], tp[0:1, 0:1], float(16 ** d), row[0:1, 0:1], ALU.is_ge, ALU.add)
            dve.drain()
            nc.vector.tensor_copy(k.ctl[0:1, 1:2], row[0:1, 0:1])
            nc.vector.tensor_copy(key[:], mult)
            dve.drain().then_inc(bound_ready, 1)
            dve.wait_ge(bound_ready, 2)
            planes = dve.value_load(k.ctl[0:1, 1:2], min_val=1, max_val=DIGITS)

            def digit(d):
                ts(tb[:], key[:], 4 * d, 15, ALU.logical_shift_right, ALU.bitwise_and)
                dve.drain()
                nc.vector.tensor_copy(k.digit[:, d, :].bitcast(FP8), tb[:], saturate=False)
                dve.drain()
            digit(0)
            for d in range(1, DIGITS):
                with dve.If(planes > d):
                    digit(d)

        @block.tensor
        def _(pe):
            for n, count in ((1, NT + 1), (2, 1)):
                pe.wait_ge(tests_ready, n)
                nc.tensor.matmul(tp[0:count, :], tests[:, 0:count], k.ident[:], start=True, stop=True).then_inc(tests_turned, 1)
                pe.wait_ge(best_ready, n)
                nc.tensor.matmul(tp[0:1, 0:count], row[0:count, 16:17], k.ident[0:count, 0:count], start=True, stop=True).then_inc(best_turned, 1)


def fill_nodes(nc, dve, nodes, iota):
    nc.vector.tensor_copy(nodes[:, 0:P], iota[0:EP, :])
    done = P
    while done < NPAD:
        more = min(done, NPAD - done)
        dve.drain()
        nc.vector.tensor_scalar(nodes[:, done:done + more], nodes[:, 0:more], float(done), None, ALU.add)
        done += more


class Visits:

    def __init__(self, nc, k, s, psum, name, rows):
        self.nc, self.k, self.name, self.rows = nc, k, name, rows
        self.nodes = k.sb(f"{name}_nodes", [EP, NPAD], F32, s)
        self.onehot = k.sb(f"{name}_onehot", [EP, 2, G, P], F32, s)
        self.total = k.sb(f"{name}_total", [rows, NPAD + P], F32, s)
        self.ps = k.pb(f"{name}_visit_ps", [rows, 2, 512], F32, psum)
        self.onehot_ready = k.sem(f"{name}_onehot_ready")
        self.product_done = k.sem(f"{name}_product_done")
        self.added = k.sem(f"{name}_added")
        self.rows_free = k.sem(f"{name}_rows_free")
        self.zero = k.sb(f"{name}_zero", [1, P], F32, s)
        self.zero_ready = k.sem(f"{name}_zero_ready")

    def start_dve(self, dve):
        nc = self.nc
        nc.vector.memset(self.zero[:], 0.0).then_inc(self.zero_ready, 1)
        nc.vector.memset(self.total[:], 0.0)
        fill_nodes(nc, dve, self.nodes, self.k.iota)
        dve.drain().then_inc(self.added, 1)
        self.count = dve.alloc_register(f"{self.name}_visits_dve")
        self.before = dve.alloc_register(f"{self.name}_block_before")
        dve.reg_mov(self.count, 0)
        dve.reg_mov(self.before, NB)

    def start_pe(self, pe):
        pe.wait_ge(self.zero_ready, 1)
        self.nc.tensor.matmul(self.ps[:, 1, 0:P], self.zero[0:1, 0:self.rows], self.zero[0:1, :],
                              start=True, stop=True).then_inc(self.product_done, 1)
        self.count_pe = pe.alloc_register(f"{self.name}_visits_pe")
        pe.reg_mov(self.count_pe, 0)

    def blocks(self, eng, g):
        table = self.k.table
        first = eng.value_load(table[0:1, 0, bass.ds(g, 1)], min_val=0, max_val=NB - 1)
        end = eng.value_load(table[0:1, 1, bass.ds(g, 1)], min_val=1, max_val=NB)
        return first, end

    def add(self, dve, v):
        at = dve.snap(self.before, min_val=0, max_val=NB)
        dve.wait_ge(self.product_done, v + 1)
        dve.wait_ge(self.added, v + 1)
        part = self.total[:, bass.ds(at * P, P)]
        self.nc.vector.tensor_tensor(part, part, view(self.ps[:], ((v + 1) % 2) * 512, [[1, P]]), ALU.add).then_inc(self.added, 1)

    def group_dve(self, dve, g, dst):
        first, end = self.blocks(dve, g)
        with dve.Fori(first, end) as b:
            v = dve.snap(self.count, min_val=0, max_val=NG * NB)
            self.nc.vector.tensor_tensor(view(self.onehot[:], (v % 2) * (G * P), [[P, G], [1, P]]),
                                         view(dst, 0, [[1, G], [0, P]]),
                                         view(self.nodes[:], b * P, [[0, G], [1, P]]),
                                         ALU.is_equal).then_inc(self.onehot_ready, 1)
            self.add(dve, v)
            dve.reg_mov(self.before, b)
            dve.reg_add(self.count, self.count, 1)

    def finish_dve(self, dve):
        self.add(dve, dve.snap(self.count, min_val=0, max_val=NG * NB))

    def group_pe(self, pe, g, rows):
        first, end = self.blocks(pe, g)
        with pe.Fori(first, end):
            v = pe.snap(self.count_pe, min_val=0, max_val=NG * NB)
            pe.wait_ge(self.onehot_ready, v + 1)
            pe.wait_ge(self.added, v + 1)
            for j in range(G):
                mm = self.nc.tensor.matmul(view(self.ps[:], (v % 2) * 512, [[1, P]]), rows(j),
                                           view(self.onehot[:], (v % 2) * (G * P) + j * P, [[1, P]]),
                                           start=(j == 0), stop=(j == G - 1))
            mm.then_inc(self.product_done, 1)
            pe.reg_add(self.count_pe, self.count_pe, 1)
        pe.drain().then_inc(self.rows_free, 1)


def layer_norm(nc, dve, act, k, y, scratch, mean, var, sems, turn):
    squares_ready, root_ready = sems
    per_node = lambda a: view(a[:], 0, [[1, NB], [0, D]])
    if dve is not None:
        nc.vector.tensor_reduce(mean[:], y[:], AX.X, ALU.add)
        dve.drain()
        nc.vector.tensor_scalar(mean[:], mean[:], 1.0 / D, None, ALU.mult)
        dve.drain()
        nc.vector.tensor_tensor(y[:], y[:], per_node(mean), ALU.subtract)
        dve.drain()
        nc.vector.tensor_tensor(scratch[:], y[:], y[:], ALU.mult)
        dve.drain()
        nc.vector.tensor_reduce(var[:], scratch[:], AX.X, ALU.add)
        dve.drain()
        nc.vector.tensor_scalar(var[:], var[:], 1.0 / D, EPS, ALU.mult, ALU.add).then_inc(squares_ready, 1)
        dve.wait_ge(root_ready, turn)
        nc.vector.reciprocal(var[:], var[:])
        dve.drain()
        nc.vector.tensor_tensor(y[:], y[:], per_node(var), ALU.mult)
        dve.drain()
    else:
        act.wait_ge(squares_ready, turn)
        nc.scalar.sqrt(var[:], var[:]).then_inc(root_ready, 1)


def edge_network(nc, k, s):
    sb, pb, sem, io = k.sb, k.pb, k.sem, k.io
    M1 = DH + 1
    xin = [sb(f"e_xin{m}", [EP, G, DI], F32, s) for m in range(2)]
    dst = [sb(f"e_dst{m}", [EP, G], F32, s) for m in range(2)]
    split = [sb(f"e_split{m}", [EP, G, 2], BF16, s) for m in range(2)]
    hist_lo = sb("hist_lo", [EP, G, P], BF16, s)
    hist_hi = sb("hist_hi", [EP, G, NB], BF16, s)
    iota_h = sb("iota_h", [EP, P], BF16, s)
    xt = sb("xt", [DI + 1, 2, GE], F32, s)
    hid = [sb(f"e_hidden{m}", [EP, G, M1], F32, s) for m in range(2)]
    w1a = sb("w1a", [DI + 1, DH], F32, s)
    w1b = sb("w1b", [M1, M1], F32, s)
    count_row = sb("count_row", [M1, DH], F32, s)
    w2x = sb("w2x", [D, DI], F32, s)
    w2g = sb("w2g", [DH, DI], F32, s)
    b2a = sb("b2a", [DI, 1], F32, s)
    w2b = sb("w2b", [DI + 1, D], F32, s)
    stage_i = [sb(f"stage_i{m}", [EP, BATCH], I32, s) for m in range(2)]
    stage_v = [sb(f"stage_v{m}", [EP, BATCH], U8, s) for m in range(2)]

    weights_zero, weights_loaded = sem("e_weights_zero"), sem("e_weights_loaded")
    loaded = [sem(f"e_loaded{m}") for m in range(2)]
    group_read = sem("e_group_read")
    xt_ready, xt_evac, h_ready, h_evac = (sem("e_" + x) for x in ("xt_ready", "xt_evac", "h_ready", "h_evac"))
    hist_ready, hist_done = sem("hist_ready"), sem("hist_done")
    staged = [sem(f"staged{m}") for m in range(2)]
    stored = [sem(f"digits_stored{m}") for m in range(2)]
    cleared, clear_ready = sem("cleared"), sem("clear_ready")
    SUB = [(0, 4), (4, 4), (8, 2)]
    HT = 5
    zeros = sb("e_zeros", [P, CW], U8, s)
    RC = 132
    rel = sb("rel", [EP, RC, 3], F32, s)
    square = sb("rel_square", [EP, RC, 3], F32, s)
    norm = sb("rel_norm", [EP, RC], F32, s)
    unit = sb("rel_unit", [EP, RC, 5], F32, s)
    rel_loaded, unit_stored, unit_ready, norm_ready, root_ready = (sem(x) for x in (
        "rel_loaded", "unit_stored", "unit_ready", "norm_ready", "rel_root_ready"))

    with ExitStack() as q:
        vis = Visits(nc, k, s, q, "e", M1)
        xt_ps = pb("xt_ps", [DI, 3, 512], F32, q)
        h_ps = pb("h_ps", [EP, 2, 512], F32, q)
        last_ps = pb("e_last_ps", [P, 512], F32, q)
        hist_ps = last_ps[:, 0:NB]
        node_pe, node_act, node_dve = node_network(
            nc, k, vis, w1b, count_row, w2x, w2g, b2a, w2b, s,
            (xt_ps[0:D, 0:2, :], h_ps[0:M1, :, :], vis.ps[0:DH, :, :], last_ps[:, P:512]))
        with nc.Block() as block:

            @block.gpsimd
            def _(pool):
                planes = pool.value_load(k.ctl[0:1, 1:2], min_val=1, max_val=DIGITS)
                pool.wait_ge(clear_ready, 1)
                batches = COLS // BATCH

                def store_plane(d):
                    def batch(i, m, first):
                        if not first:
                            await_alone(pool, k.passed_pool, stored[m], pool.snap(issued[m], min_val=16 * BATCH, max_val=1 << 24))
                        at = (i * 2 + m) * BATCH
                        nc.gpsimd.tensor_copy(stage_i[m][:], k.index[:, bass.ds(at, BATCH)]).then_inc(staged[m], 1)
                        nc.gpsimd.tensor_copy(stage_v[m][:], k.digit[:, d, bass.ds(at, BATCH)]).then_inc(staged[m], 1)
                        pool.reg_add(turns[m], turns[m], 2)
                        await_alone(pool, k.passed_pool, staged[m], pool.snap(turns[m], min_val=2, max_val=1 << 24))
                        for j in range(BATCH):
                            pool.indirect_dma_start(k.planes[d], bass.IndirectOffsetOnAxis(stage_i[m][:, j:j + 1], 0),
                                                    stage_v[m][:, j:j + 1], None).then_inc(stored[m], 16)
                        pool.reg_add(issued[m], issued[m], 16 * BATCH)
                    for m in range(2):
                        batch(0, m, d == 0)
                    with pool.Fori(1, batches // 2) as i:
                        for m in range(2):
                            batch(i, m, False)

                issued = [pool.alloc_register(f"issued{m}") for m in range(2)]
                turns = [pool.alloc_register(f"turns{m}") for m in range(2)]
                for r in issued + turns:
                    pool.reg_mov(r, 0)
                store_plane(0)
                for d in range(1, DIGITS):
                    with pool.If(planes > d):
                        with pool.Fori(0, NCH * HG * HH) as u:
                            part = k.planes[d][0:PLANE, :].rearrange("(u p n) o -> u p (n o)", p=P, n=CW)[bass.ds(u, 1), :, :]
                            pool.dma_start(part.rearrange("a p n -> (a p) n"), zeros[:]).then_inc(cleared, 16)
                        pool.wait_ge(cleared, NCH * HG * HH * 16 * d)
                        store_plane(d)
                for m in range(2):
                    await_alone(pool, k.passed_pool, stored[m], pool.snap(issued[m], min_val=16 * BATCH, max_val=1 << 24))

            @block.sync
            def _(sp):
                sp.wait_ge(weights_zero, 1)
                w = [(w1a[0:DI, :], io["L0_gnn_w1a"]), (w1a[DI:DI + 1, :], io["L0_gnn_b1a"].rearrange("(o n) -> o n", o=1)),
                     (w1b[0:DH, 0:DH], io["L0_gnn_w1b"]), (w1b[DH:M1, 0:DH], io["L0_gnn_b1b"].rearrange("(o n) -> o n", o=1)),
                     (w2x[:], io["L0_gnn_w2a"][0:D, :]), (w2g[:], io["L0_gnn_w2a"][D:D + DH, :]),
                     (b2a[:], io["L0_gnn_b2a"].rearrange("(n o) -> n o", o=1)),
                     (w2b[0:DI, :], io["L0_gnn_w2b"]), (w2b[DI:DI + 1, :], io["L0_gnn_b2b"].rearrange("(o n) -> o n", o=1))]
                for to, frm in w:
                    sp.dma_start(to, frm).then_inc(weights_loaded, 16)

                def columns(a, c, width):
                    return a.rearrange("(p e) f -> p (e f)", p=EP)[:, bass.ds(c * (RC * width), RC * width)]
                sp.dma_start(view(rel[:], 0, [[1, RC * 3]]), columns(io["edge_attr_3"], 0, 3)).then_inc(rel_loaded, 16)
                with sp.Fori(1, COLS // RC) as c:
                    sp.wait_ge(unit_ready, c)
                    sp.dma_start(columns(k.dir_d, c - 1, 5), view(unit[:], 0, [[1, RC * 5]])).then_inc(unit_stored, 16)
                    sp.dma_start(view(rel[:], 0, [[1, RC * 3]]), columns(io["edge_attr_3"], c, 3)).then_inc(rel_loaded, 16)
                sp.wait_ge(unit_ready, COLS // RC)
                sp.dma_start(columns(k.dir_d, COLS // RC - 1, 5), view(unit[:], 0, [[1, RC * 5]])).then_inc(unit_stored, 16)

                def load(i, m, first):
                    g = i * 2 + m
                    if not first:
                        sp.wait_ge(group_read, g - 1)
                        sp.wait_ge(xt_ready, g * 3 - 3)
                    def part(a):
                        return a[bass.ds(g, 1), :, :].rearrange("a p c -> (a p) c")
                    sp.dma_start(view(xin[m][:], 0, [[1, G * DI]]), part(k.xin_d)).then_inc(loaded[m], 16)
                    sp.dma_start(dst[m][:], part(k.dst_d.rearrange("(g p c) -> g p c", p=EP, c=G))).then_inc(loaded[m], 16)
                    sp.dma_start(view(split[m][:], 0, [[1, 2 * G]]),
                                 part(k.hist_d.rearrange("(g p c) t -> g p (c t)", p=EP, c=G))).then_inc(loaded[m], 16)
                for m in range(2):
                    load(0, m, True)
                with sp.Fori(1, PAIRS) as i:
                    for m in range(2):
                        load(i, m, False)
                sp.wait_ge(unit_stored, COLS // RC * 16)

            @block.tensor
            def _(pe):
                def group(i, m, first):
                    n = i * 2 + m
                    pe.wait_ge(loaded[m], (i + 1) * 48)
                    for b, (t0, tn) in enumerate(SUB):
                        if not first:
                            await_alone(pe, k.passed_pe, xt_evac, n * 3 + (b - 2))
                        for t in range(t0, t0 + tn):
                            mm = nc.tensor.transpose(xt_ps[:, b, (t - t0) * EP:(t - t0 + 1) * EP], xin[m][:, t, :],
                                                     k.ident[0:EP, 0:EP])
                        mm.then_inc(xt_ready, 1)
                    for b in range(2):
                        pe.wait_ge(xt_evac, n * 3 + (2 + b))
                        if not first:
                            pe.wait_ge(h_evac, n * 2 + (b - 1))
                        for t in range(HT):
                            mm = nc.tensor.matmul(h_ps[:, b, t * DH:(t + 1) * DH],
                                                  xt[:, m, (b * HT + t) * EP:(b * HT + t + 1) * EP], w1a[:],
                                                  start=True, stop=True)
                        mm.then_inc(h_ready, 1)
                    if not first:
                        pe.wait_ge(h_evac, n * 2)
                        vis.group_pe(pe, n - 1, lambda j: hid[1 - m][:, j, :])
                    pe.wait_ge(hist_ready, n + 1)
                    for j in range(G):
                        mm = nc.tensor.matmul(hist_ps, hist_lo[:, j, :], hist_hi[:, j, :], start=False,
                                              stop=False, skip_group_check=True)
                    mm.then_inc(hist_done, 1)

                pe.wait_ge(weights_loaded, 16 * 9)
                vis.start_pe(pe)
                nc.tensor.matmul(hist_ps, vis.zero[0:1, :], vis.zero[0:1, 0:NB], start=True, stop=False,
                                 skip_group_check=True)
                group(0, 0, True)
                group(0, 1, False)
                with pe.Fori(1, PAIRS) as i:
                    for m in range(2):
                        group(i, m, False)
                pe.wait_ge(h_evac, 2 * NG)
                vis.group_pe(pe, NG - 1, lambda j: hid[1][:, j, :])
                pe.wait_ge(xt_evac, 3 * NG)
                node_pe(pe)

            @block.scalar
            def _(act):
                with act.Fori(0, COLS // RC) as c:
                    act.wait_ge(norm_ready, c + 1)
                    nc.scalar.sqrt(norm[:], norm[:]).then_inc(root_ready, 1)
                act.wait_ge(weights_zero, 1)

                def group(i, m, first):
                    n = i * 2 + m
                    for b, (t0, tn) in enumerate(SUB):
                        act.wait_ge(xt_ready, n * 3 + (b + 1))
                        nc.scalar.copy(xt[0:DI, m, t0 * EP:(t0 + tn) * EP], xt_ps[:, b, 0:tn * EP]).then_inc(xt_evac, 1)
                    for b in range(2):
                        act.wait_ge(h_ready, n * 2 + (b + 1))
                        if not first and b == 0:
                            act.wait_ge(vis.rows_free, n - 1)
                        nc.scalar.activation(hid[m][:, b * HT:(b + 1) * HT, 0:DH],
                                             view(h_ps[:], b * 512, [[DH, HT], [1, DH]]), ACT.Relu).then_inc(h_evac, 1)
                for m in range(2):
                    group(0, m, True)
                with act.Fori(1, PAIRS) as i:
                    for m in range(2):
                        group(i, m, False)
                node_act(act)

            @block.vector
            def _(dve):
                tt = nc.vector.tensor_tensor
                nc.vector.memset(zeros[:].bitcast(I32), 0).then_inc(clear_ready, 1)
                for a in (w1b, count_row):
                    nc.vector.memset(a[:], 0.0)
                for a in (xt, w2b, *hid):
                    nc.vector.memset(a[:], 1.0)
                dve.drain()
                nc.vector.memset(w1b[DH:M1, DH:M1], 1.0)
                nc.vector.memset(count_row[DH:M1, :], 1.0)
                nc.vector.tensor_copy(iota_h[:], k.iota[0:EP, :])
                dve.drain().then_inc(weights_zero, 1)
                vis.start_dve(dve)

                def directions(c, first):
                    dve.wait_ge(rel_loaded, (c + 1) * 16)
                    tt(square[:], rel[:], rel[:], ALU.mult)
                    dve.drain()
                    nc.vector.tensor_reduce(norm[:], square[:], AX.X, ALU.add).then_inc(norm_ready, 1)
                    dve.wait_ge(root_ready, c + 1)
                    nc.vector.reciprocal(norm[:], norm[:])
                    dve.drain()
                    if not first:
                        dve.wait_ge(unit_stored, c * 16)
                    for to, frm, n in ((0, 1, 2), (2, 0, 1), (3, 1, 2)):
                        tt(unit[:, :, to:to + n], rel[:, :, frm:frm + n], view(norm[:], 0, [[1, RC], [0, n]]), ALU.mult)
                    dve.drain().then_inc(unit_ready, 1)
                directions(0, True)
                with dve.Fori(1, COLS // RC) as c:
                    directions(c, False)

                def group(i, m, first):
                    n = i * 2 + m
                    dve.wait_ge(loaded[m], (i + 1) * 48)
                    if not first:
                        dve.wait_ge(hist_done, n)
                    tt(hist_lo[:], view(split[m][:], 0, [[2, G], [0, P]]), view(iota_h[:], 0, [[0, G], [1, P]]), ALU.is_equal)
                    tt(hist_hi[:], view(split[m][:], 1, [[2, G], [0, NB]]), view(iota_h[:], 0, [[0, G], [1, NB]]),
                       ALU.is_equal).then_inc(hist_ready, 1)
                    vis.group_dve(dve, n, dst[m][:])
                    dve.drain().then_inc(group_read, 1)
                group(0, 0, True)
                group(0, 1, False)
                with dve.Fori(1, PAIRS) as i:
                    for m in range(2):
                        group(i, m, False)
                vis.finish_dve(dve)
                dve.wait_ge(hist_done, NG)
                nc.vector.tensor_copy(view(k.small[:], 1, [[2, NB]]), hist_ps)
                node_dve(dve)


HALVES = [(0, 4 * P), (4 * P, CW - 4 * P)]


def node_network(nc, k, vis, w1b, count_row, w2x, w2g, b2a, w2b, s, banks):
    sb, pb, sem = k.sb, k.pb, k.sem
    M1 = DH + 1
    stage = sb("x_stage", [P, CB, D], F32, s)
    x_t = sb("x_t", [D, CW], F32, s)
    agg = sb("agg_t", [M1, CW], F32, s)
    inv = sb("inv_count", [DH, CW], F32, s)
    h2 = sb("h2", [DI + 1, CW], F32, s)
    names = ("staged", "turned", "turned_copied", "sums", "sums_copied", "counts", "mean", "h2", "h2_copied", "out", "taken")
    (staged, turned, turned_copied, sums_ready, sums_copied, counts_ready, mean_ready, h2_ready, h2_copied,
     out_ready, taken) = (sem("n_" + x) for x in names)
    ones_ready, sums_final = sem("n_ones_ready"), sem("n_sums_final")
    x_ps, a_ps, c_ps, o_ps = banks

    def node_pe(pe):
        pe.wait_ge(sums_final, 1)
        def chunk(c, first):
            await_alone(pe, k.passed_pe, staged, c + 1)
            for j in range(CB):
                mm = nc.tensor.transpose(x_ps[:, j // 4, (j % 4) * P:(j % 4 + 1) * P], stage[:, j, :], k.ident[:])
            mm.then_inc(turned, 1)
            for b, (at, n) in enumerate(HALVES):
                mm = nc.tensor.matmul(a_ps[:, b, 0:n], w1b[:], vis.total[:, bass.ds(c * CW + at, n)], start=True, stop=True)
            mm.then_inc(sums_ready, 1)
            pe.wait_ge(sums_copied, c + 1)
            for b, (at, n) in enumerate(HALVES):
                mm = nc.tensor.matmul(c_ps[:, b, 0:n], count_row[:], agg[:, at:at + n], start=True, stop=True)
            mm.then_inc(counts_ready, 1)
            if not first:
                pe.wait_ge(taken, c)
            for j in range(CB):
                mm = nc.tensor.matmul(o_ps[:, CB * D + j:CB * D + j + 1], agg[:, j * P:(j + 1) * P],
                                      k.ident[0:M1, DH:M1], start=True, stop=True)
            mm.then_inc(counts_ready, 1)
            pe.wait_ge(mean_ready, c + 1)
            pe.wait_ge(turned_copied, c + 1)
            for b, (at, n) in enumerate(HALVES):
                nc.tensor.matmul(a_ps[0:DI, b, 0:n], w2g[:], agg[0:DH, at:at + n], start=True, stop=False)
                mm = nc.tensor.matmul(a_ps[0:DI, b, 0:n], w2x[:], x_t[:, at:at + n], start=False, stop=True)
            mm.then_inc(h2_ready, 1)
            pe.wait_ge(h2_copied, c + 1)
            for j in range(CB):
                mm = nc.tensor.matmul(o_ps[:, j * D:(j + 1) * D], h2[:, j * P:(j + 1) * P], w2b[:], start=True, stop=True)
            mm.then_inc(out_ready, 1)
        chunk(0, True)
        with pe.Fori(1, NCH) as c:
            chunk(c, False)

    def node_act(act):
        act.wait_ge(ones_ready, 1)
        def chunk(c, first):
            if not first:
                act.wait_ge(taken, c)
            nc.scalar.copy(stage[:], k.x[:, bass.ds(c * CB, CB), :]).then_inc(staged, 1)
            act.wait_ge(turned, c + 1)
            for b, (at, n) in enumerate(HALVES):
                cp = nc.scalar.copy(x_t[:, at:at + n], x_ps[:, b, 0:n])
            cp.then_inc(turned_copied, 1)
            act.wait_ge(sums_ready, c + 1)
            for b, (at, n) in enumerate(HALVES):
                cp = nc.scalar.copy(agg[:, at:at + n], a_ps[:, b, 0:n])
            cp.then_inc(sums_copied, 1)
            act.wait_ge(h2_ready, c + 1)
            for b, (at, n) in enumerate(HALVES):
                cp = nc.scalar.activation(h2[0:DI, at:at + n], a_ps[0:DI, b, 0:n], ACT.Relu, bias=b2a[:, 0:1])
            cp.then_inc(h2_copied, 1)
        chunk(0, True)
        with act.Fori(1, NCH) as c:
            chunk(c, False)

    def node_dve(dve):
        nc.vector.memset(h2[:], 1.0).then_inc(ones_ready, 1)
        dve.drain().then_inc(sums_final, 1)
        with dve.Fori(0, NCH) as c:
            dve.wait_ge(counts_ready, c * 2 + 2)
            for b, (at, n) in enumerate(HALVES):
                nc.vector.tensor_scalar(inv[:, at:at + n], c_ps[:, b, 0:n], 1.0, None, ALU.max)
            dve.drain()
            nc.vector.reciprocal(inv[:], inv[:])
            dve.drain()
            nc.vector.tensor_tensor(agg[0:DH, :], agg[0:DH, :], inv[:], ALU.mult).then_inc(mean_ready, 1)
            dve.wait_ge(out_ready, c + 1)
            part = k.x[:, bass.ds(c * CB, CB), :]
            nc.vector.tensor_copy(view(k.small[:], c * (2 * CB), [[2, CB]]), o_ps[:, CB * D:CB * D + CB])
            nc.vector.tensor_tensor(part, part, view(o_ps, 0, [[D, CB], [1, D]]), ALU.add)
            dve.drain().then_inc(taken, 1)
    return node_pe, node_act, node_dve


def propagate(nc, k, s):
    sb, pb, sem = k.sb, k.pb, k.sem
    passes = STEPS + 1
    slots = [sb(f"a_slot{h}", [P, HH, CW], U8, s) for h in range(HG)]
    parts = [sb(f"f_parts{t}", [P, NB, 3 * D], BF16, s) for t in range(2)]
    agg = sb("agg", [P, NB, D], F32, s)
    chunk_f = sb("chunk_f", [P, CB * D], F32, s)
    chunk_zero = sb("chunk_zero", [P, CB * D], F32, s)
    tenth = sb("x_tenth", [P, NB, D], F32, s)
    norms = sb("norms", [P, NB, 2], F32, s)
    mean, var = sb("mean", [P, NB], F32, s), sb("var", [P, NB], F32, s)
    turned = sb("turned", [3 * D, 2, CW], F32, s)
    select = sb("select", [3 * D, DIGITS * D], F32, s)
    a_loaded = [sem(f"a_loaded{h}") for h in range(HG)]
    a_used = sem("a_used")
    parts_ready = sem("parts_ready")
    product_ready, product_copied = sem("p_product_ready"), sem("p_product_copied")
    summed, taken = sem("p_summed"), sem("p_taken")
    norm_in, norm_out = sem("ln_in"), sem("ln_out")
    x_ready, x_stored = sem("p_x_ready"), sem("p_x_stored")

    with ExitStack() as q:
        prod = [pb(f"p_prod{m}", [3 * D, 2, 512], F32, q) for m in range(2)]
        back = [pb(f"p_back{m}", [P, CB * D], F32, q) for m in range(2)]
        with nc.Block() as block:

            def each_chunk(eng, u, planes, body):
                with eng.Fori(0, planes) as d:
                    with eng.Fori(0, NCH // 2) as c2:
                        n = eng.snap(u, min_val=0, max_val=passes * DIGITS * NCH)
                        body(n, d, c2)
                        eng.reg_add(u, u, 1)

            @block.sync
            def _(sp):
                planes = sp.value_load(k.ctl[0:1, 1:2], min_val=1, max_val=DIGITS)
                u = sp.alloc_register("pairs_sp")
                sp.reg_mov(u, 0)

                def load_plane(d):
                    with sp.Fori(0, NCH // 2) as c2:
                        n = sp.snap(u, min_val=0, max_val=passes * DIGITS * NCH)
                        for m in range(2):
                            for h in range(HG):
                                sp.wait_ge(a_used, n * (2 * HG) + (HG * m + h + 1))
                                sp.dma_start(view(slots[h][:], 0, [[1, HH * CW]]),
                                             plane_part(k.planes[d], c2 * (2 * HG) + (m * HG + h))).then_inc(a_loaded[h], 16)
                        sp.reg_add(u, u, 1)
                with sp.Fori(0, passes):
                    load_plane(0)
                    for d in range(1, DIGITS):
                        with sp.If(planes > d):
                            load_plane(d)
                sp.wait_ge(x_ready, 1)
                sp.dma_start(k.x3_d.rearrange("(b p) f -> p b f", p=P), k.x[:]).then_inc(x_stored, 16)
                sp.wait_ge(x_stored, 16)

            @block.tensor
            def _(pe):
                planes = pe.value_load(k.ctl[0:1, 1:2], min_val=1, max_val=DIGITS)
                u = pe.alloc_register("pairs_pe")
                pe.reg_mov(u, 0)
                pe.sem_inc(a_used, HG)
                pe.sem_inc(summed, 2)

                def product(n, m, source, p=None):
                    pe.wait_ge(product_copied, n * 2 + (m + 1))
                    for h in range(HG):
                        if p is not None:
                            await_alone(pe, k.passed_pe, parts_ready, p * HG + (h + 1))
                        await_alone(pe, k.passed_pe, a_loaded[h], n * 32 + 16 * (m + 1))
                        for j in range(HH):
                            for w in range(2):
                                mm = nc.tensor.matmul(prod[m][:, w, 0:HW], source[:, h * HH + j, :],
                                                      slots[h][:, j, w * HW:(w + 1) * HW].bitcast(FP8),
                                                      start=(h == 0 and j == 0), stop=(h == HG - 1 and j == HH - 1))
                        mm.then_inc(a_used, 1)
                    pe.drain().then_inc(product_ready, 1)

                def turn_back(n, d, m):
                    pe.wait_ge(product_copied, n * 2 + (m + 3))
                    pe.wait_ge(taken, n * 2 + (m + 1))
                    for j in range(CB):
                        mm = nc.tensor.matmul(back[m][:, j * D:(j + 1) * D], turned[:, m, j * P:(j + 1) * P],
                                              select[:, bass.ds(d * D, D)], start=True, stop=True)
                    mm.then_inc(summed, 1)

                def one_pass(p, source):
                    with pe.Fori(0, planes) as d:
                        product(pe.snap(u, min_val=0, max_val=passes * DIGITS * NCH), 0, source, p)
                        with pe.Fori(0, NCH // 2 - 1):
                            n = pe.snap(u, min_val=0, max_val=passes * DIGITS * NCH)
                            product(n, 1, source)
                            turn_back(n, d, 0)
                            product(n + 1, 0, source)
                            turn_back(n, d, 1)
                            pe.reg_add(u, u, 1)
                        n = pe.snap(u, min_val=0, max_val=passes * DIGITS * NCH)
                        product(n, 1, source)
                        turn_back(n, d, 0)
                        turn_back(n, d, 1)
                        pe.reg_add(u, u, 1)
                with pe.Fori(0, STEPS // 2) as p2:
                    for odd in range(2):
                        one_pass(p2 * 2 + odd, parts[odd])
                one_pass(STEPS, parts[0])

            @block.scalar
            def _(act):
                planes = act.value_load(k.ctl[0:1, 1:2], min_val=1, max_val=DIGITS)
                u = act.alloc_register("pairs_act")
                act.reg_mov(u, 0)
                act.sem_inc(product_copied, 2)
                layer_norm(nc, None, act, k, k.x, None, mean, var, (norm_in, norm_out), 1)
                act.wait_ge(norm_in, 2)
                nc.scalar.sqrt(norms[:], norms[:]).then_inc(norm_out, 1)

                def body(n, d, c2):
                    for m in range(2):
                        act.wait_ge(product_ready, n * 2 + (m + 1))
                        act.wait_ge(summed, n * 2 + (m + 1))
                        nc.scalar.copy(view(turned[:], m * CW, [[HW, 2], [1, HW]]),
                                       view(prod[m][:], 0, [[512, 2], [1, HW]])).then_inc(product_copied, 1)
                with act.Fori(0, STEPS):
                    each_chunk(act, u, planes, body)
                layer_norm(nc, None, act, k, k.x, None, mean, var, (norm_in, norm_out), 3)
                each_chunk(act, u, planes, body)
                layer_norm(nc, None, act, k, k.x, None, mean, var, (norm_in, norm_out), 4)

            @block.vector
            def _(dve):
                tt, ts = nc.vector.tensor_tensor, nc.vector.tensor_scalar
                planes = dve.value_load(k.ctl[0:1, 1:2], min_val=1, max_val=DIGITS)
                u = dve.alloc_register("pairs_dve")
                dve.reg_mov(u, 0)
                dve.sem_inc(taken, 2)
                for r in range(3):
                    for d in range(DIGITS):
                        ts(select[r * D:(r + 1) * D, d * D:(d + 1) * D], k.ident[r * D:(r + 1) * D, r * D:(r + 1) * D],
                           float(16 ** d), None, ALU.mult)
                nc.vector.memset(chunk_zero[:], 0.0)
                norm = lambda turn, scratch: layer_norm(nc, dve, None, k, k.x, scratch, mean, var, (norm_in, norm_out), turn)
                of_src = view(norms[:], 1, [[2, NB], [0, D]])

                def split(frm, to):
                    for r in range(3):
                        nc.vector.tensor_copy(to(r), frm)
                        if r < 2:
                            dve.drain()
                            tt(frm, frm, to(r), ALU.subtract)
                            dve.drain()

                def one_pass(finish):
                    with dve.Fori(0, planes) as d:
                        with dve.Fori(0, NCH // 2) as c2:
                            n = dve.snap(u, min_val=0, max_val=passes * DIGITS * NCH)
                            for m in range(2):
                                dve.wait_ge(summed, n * 2 + (m + 3))
                                part = view(agg[:], c2 * (2 * CB * D) + m * CB * D, [[1, CB * D]])
                                tt(part, part, back[m][:], ALU.add).then_inc(taken, 1)
                            dve.reg_add(u, u, 1)
                            if finish is not None:
                                with dve.If(planes - d == 1):
                                    for m in range(2):
                                        finish(c2 * 2 + m)
                                    if finish is not into_x:
                                        dve.drain().then_inc(parts_ready, 1)

                def new_f(c):
                    part = view(agg[:], c * (CB * D), [[1, CB * D]])
                    dve.drain()
                    tt(view(agg[:], c * (CB * D), [[D, CB], [1, D]]), view(agg[:], c * (CB * D), [[D, CB], [1, D]]),
                       view(norms[:], c * (2 * CB), [[2, CB], [0, D]]), ALU.mult)
                    dve.drain()
                    nc.vector.scalar_tensor_tensor(chunk_f[:], part, 1.0 - ALPHA, view(tenth[:], c * (CB * D), [[1, CB * D]]),
                                                   ALU.mult, ALU.add)
                    dve.drain()
                    nc.vector.tensor_copy(part, chunk_zero[:])

                def next_parts(to):
                    def finish(c):
                        new_f(c)
                        f = view(chunk_f[:], 0, [[D, CB], [1, D]])
                        tt(f, f, view(norms[:], c * (2 * CB) + 1, [[2, CB], [0, D]]), ALU.mult)
                        dve.drain()
                        split(f, lambda r: view(to[:], c * (CB * 3 * D) + r * D, [[3 * D, CB], [1, D]]))
                    return finish

                def into_x(c):
                    new_f(c)
                    part = view(k.x[:], c * (CB * D), [[1, CB * D]])
                    tt(part, part, chunk_f[:], ALU.add)

                def all_parts():
                    dve.drain()
                    split(agg[:], lambda r: parts[0][:, :, r * D:(r + 1) * D])
                    dve.drain()
                    nc.vector.memset(agg[:], 0.0)

                norm(1, agg)
                ts(norms[:], k.small[:], 1.0, None, ALU.max).then_inc(norm_in, 1)
                dve.wait_ge(norm_out, 2)
                nc.vector.reciprocal(norms[:], norms[:])
                ts(tenth[:], k.x[:], ALPHA, None, ALU.mult)
                dve.drain()
                tt(agg[:], k.x[:], of_src, ALU.mult)
                all_parts()
                dve.drain().then_inc(parts_ready, HG)
                with dve.Fori(0, STEPS // 2 - 1):
                    for odd in range(2):
                        one_pass(next_parts(parts[1 - odd]))
                one_pass(next_parts(parts[1]))
                one_pass(into_x)
                dve.drain()
                norm(3, tenth)
                nc.vector.tensor_copy(agg[:], k.x[:])
                all_parts()
                dve.drain().then_inc(parts_ready, HG)
                one_pass(None)
                dve.drain()
                tt(k.x[:], k.x[:], agg[:], ALU.add)
                dve.drain()
                norm(4, tenth)
                dve.drain().then_inc(x_ready, 1)


def tensor_messages(nc, k, s):
    sb, pb, sem, io = k.sb, k.pb, k.sem, k.io
    U = 8
    y0, c1, c2 = 0.5 / math.sqrt(math.pi), math.sqrt(3 / (4 * math.pi)), 0.5 * math.sqrt(15 / math.pi)
    norm0 = math.sqrt(4 * math.pi) / math.sqrt(2 * U)
    norm1 = math.sqrt(4 * math.pi) * math.sqrt(3) / math.sqrt(4 * U)
    RD = 6 * U * U
    raw = sb("raw_w2", [HID + 1, RD], F32, s)
    w2 = sb("radial_w2", [P, RD], F32, s)
    w1 = sb("radial_w1", [HID, 2], F32, s)
    edge_w = [sb(f"edge_w{m}", [HID, GE], F32, s) for m in range(2)]
    hid = [sb(f"radial_hidden{m}", [P, G, EP], F32, s) for m in range(2)]
    idx = [sb(f"m_idx{m}", [EP, G], I32, s) for m in range(2)]
    src = [sb(f"m_src{m}", [EP, G, D], F32, s) for m in range(2)]
    dst = [sb(f"m_dst{m}", [EP, G], F32, s) for m in range(2)]
    kept = [sb(f"m_dst_kept{m}", [EP, G], F32, s) for m in range(2)]
    unit = [sb(f"m_unit{m}", [EP, G, 5], F32, s) for m in range(2)]
    FX = 8 * U
    feat = [sb(f"m_features{m}", [EP, G, FX], F32, s) for m in range(2)]
    cyclic = [sb(f"f1_cyclic{m}", [EP, G, U, 5], F32, s) for m in range(2)]
    pool_t = [sb(f"pool_t{n}", [EP, G, U, 3], F32, s) for n in range(3)]
    CW1, CW0, CWF = 2 * U * U, 2 * U * U, 3 * U * U
    PW = CW1 + CW0 + 2 * CWF
    SUMMED = CW0 + CWF + 3 * U
    prod = [sb(f"m_products{m}", [EP, G, PW], F32, s) for m in range(2)]
    along = sb("m_along", [EP, G, U], F32, s)
    crossed = sb("m_crossed", [EP, G, 3 * U], F32, s)
    nodes = sb("m_nodes", [EP, NPAD], F32, s)
    onehot = [sb(f"m_onehot{m}", [EP, G, P], F32, s) for m in range(3)]
    difference = sb("m_difference", [EP, G, P], F32, s)
    one = sb("m_one", [EP, 1], F32, s)
    visit = sb("m_visit", [P, D], F32, s)
    sums = sb("m_sums", [P, NB + 1, D], F32, s)
    zero = sb("m_zero", [1, SUMMED], F32, s)
    mean, var = sb("m_mean", [P, NB], F32, s), sb("m_var", [P, NB], F32, s)

    w_loaded, w_ready = sem("m_w_loaded"), sem("m_w_ready")
    loaded = [sem(f"m_loaded{m}") for m in range(2)]
    idx_loaded = [sem(f"m_idx_loaded{m}") for m in range(2)]
    gathered = [sem(f"m_gathered{m}") for m in range(2)]
    hid_ready, r_ready, r_used = sem("m_hid_ready"), sem("m_r_ready"), sem("m_r_used")
    copied, pool_step, features_ready = sem("m_copied"), sem("m_pool_step"), sem("m_features_ready")
    rows_ready, features_used = sem("m_rows_ready"), sem("m_features_used")
    extra_ready, rows_free = sem("m_extra_ready"), sem("m_rows_free")
    product_done, added = sem("m_product_done"), sem("m_added")
    norm_in, norm_out = sem("m_ln_in"), sem("m_ln_out")
    out_ready, out_stored = sem("m_out_ready"), sem("m_out_stored")
    RB = 2
    NBAT = G // RB
    BETWEEN = (1, 0, 0)
    onehot_ready, difference_ready = sem("m_onehot_ready"), sem("m_difference_ready")

    def blocks(eng, g):
        first = eng.value_load(k.table[0:1, 0, bass.ds(g, 1)], min_val=0, max_val=NB - 1)
        end = eng.value_load(k.table[0:1, 1, bass.ds(g, 1)], min_val=1, max_val=NB)
        return first, end

    with ExitStack() as q:
        r_ps = pb("radial_ps", [EP, 2, RB, 512], F32, q)
        v_ps = pb("m_visit_ps", [P, 3, 512], F32, q)
        with nc.Block() as block:

            @block.gpsimd
            def _(pool):
                def gather(i, m, first):
                    await_alone(pool, k.passed_pool, idx_loaded[m], (i + 1) * 16)
                    if not first:
                        await_alone(pool, k.passed_pool, copied, i * 2 + (m - 1))
                    for j in range(G):
                        pool.indirect_dma_start(src[m][:, j, :], None, k.x3_d,
                                                bass.IndirectOffsetOnAxis(idx[m][:, j:j + 1], 0)).then_inc(gathered[m], 16)

                def features(n, turn, m, first):
                    mul = lambda to, a, b: nc.gpsimd.tensor_tensor(to, a, b, ALU.mult).then_inc(pool_step, 1)
                    shifted = lambda at: view(cyclic[m][:], at, [[5 * U, G], [5, U], [1, 3]])
                    r_o = lambda at: view(unit[m][:], at, [[5, G], [0, U], [1, 3]])
                    await_alone(pool, k.passed_pool, loaded[m], turn * 48)
                    if not first:
                        await_alone(pool, k.passed_pool, features_ready, n)
                    await_alone(pool, k.passed_pool, copied, n + 1)
                    mul(pool_t[0][:], shifted(0), r_o(0))
                    mul(pool_t[1][:], shifted(2), r_o(1))
                    mul(pool_t[2][:], shifted(1), r_o(2))
                    part = lambda i: view(pool_t[0][:], i, [[3 * U, G], [3, U]])
                    s_out = view(feat[m][:], U, [[FX, G], [1, U]])
                    await_alone(pool, k.passed_pool, pool_step, n * 5 + 3)
                    nc.gpsimd.tensor_tensor(s_out, part(0), part(1), ALU.add).then_inc(pool_step, 1)
                    nc.gpsimd.tensor_tensor(view(feat[m][:], 5 * U, [[FX, G], [3, U], [1, 3]]), pool_t[1][:], pool_t[2][:],
                                            ALU.subtract).then_inc(pool_step, 1)
                    await_alone(pool, k.passed_pool, pool_step, n * 5 + 5)
                    nc.gpsimd.tensor_tensor(s_out, s_out, part(2), ALU.add).then_inc(features_ready, 1)
                gather(0, 0, True)
                gather(0, 1, True)
                features(0, 1, 0, True)
                with pool.Fori(1, PAIRS) as i:
                    gather(i, 0, False)
                    features(i * 2 - 1, i, 1, False)
                    gather(i, 1, False)
                    features(i * 2, i + 1, 0, False)
                features(NG - 1, PAIRS, 1, False)

            @block.sync
            def _(sp):
                sp.dma_start(raw[0:HID, :], io["L3_gnn_w2"]).then_inc(w_loaded, 16)
                sp.dma_start(raw[HID:HID + 1, :], io["L3_gnn_b2"].rearrange("(o n) -> o n", o=1)).then_inc(w_loaded, 16)
                sp.dma_start(w1[:, 0:1], io["L3_gnn_w1"].rearrange("o n -> n o")).then_inc(w_loaded, 16)
                sp.dma_start(w1[:, 1:2], io["L3_gnn_b1"].rearrange("(n o) -> n o", o=1)).then_inc(w_loaded, 16)

                def load_indices(g, turn, m, first):
                    if not first:
                        sp.wait_ge(gathered[m], turn * (16 * G))
                    sp.dma_start(idx[m][:], k.idx_view[bass.ds(g, 1), :, :].rearrange("a p j -> (a p) j")).then_inc(idx_loaded[m], 16)

                def load(g, m, first):
                    if not first:
                        sp.wait_ge(hid_ready, g - 1)
                        sp.wait_ge(onehot_ready, g - 1)
                        sp.wait_ge(rows_ready, g - 1)
                    part = lambda a: a[bass.ds(g, 1), :, :].rearrange("a p c -> (a p) c")
                    sp.dma_start(edge_w[m][:], bass.AP(io["edge_weight"].tensor, g * GE, [[0, HID], [1, GE]])).then_inc(loaded[m], 16)
                    sp.dma_start(dst[m][:], part(k.dst_d.rearrange("(g p c) -> g p c", p=EP, c=G))).then_inc(loaded[m], 16)
                    sp.dma_start(view(unit[m][:], 0, [[1, 5 * G]]),
                                 part(k.dir_d.rearrange("(g p c) t -> g p (c t)", p=EP, c=G))).then_inc(loaded[m], 16)
                load_indices(0, 0, 0, True)
                load_indices(1, 0, 1, True)
                load(0, 0, True)
                load_indices(2, 1, 0, False)
                load(1, 1, True)
                load_indices(3, 1, 1, False)
                with sp.Fori(1, PAIRS - 1) as i:
                    load(i * 2, 0, False)
                    load_indices(i * 2 + 2, i + 1, 0, False)
                    load(i * 2 + 1, 1, False)
                    load_indices(i * 2 + 3, i + 1, 1, False)
                load(NG - 2, 0, False)
                load(NG - 1, 1, False)
                sp.wait_ge(out_ready, 1)
                full = (NB - 1) * P
                sp.dma_start(k.out[0:full, :].rearrange("(b p) f -> p b f", p=P), k.x[:, 0:NB - 1, :]).then_inc(out_stored, 16)
                sp.dma_start(k.out[full:N, :], k.x[0:LAST, NB - 1, :]).then_inc(out_stored, 16)
                sp.wait_ge(out_stored, 32)

            @block.scalar
            def _(act):
                act.wait_ge(w_loaded, 64)
                act.wait_ge(w_ready, 2)

                def group(i, m, first):
                    n = i * 2 + m
                    act.wait_ge(loaded[m], (i + 1) * 48)
                    if not first:
                        act.wait_ge(r_ready, n * NBAT - NBAT)
                    nc.scalar.activation(hid[m][0:HID, :, :], view(edge_w[m][:], 0, [[1, G], [G, EP]]), ACT.Relu,
                                         bias=w1[:, 1:2], scale=w1[:, 0:1]).then_inc(hid_ready, 1)
                    act.wait_ge(gathered[m], (i + 1) * (16 * G))
                    if not first:
                        act.wait_ge(features_used, n - 1)
                    f1 = view(src[m][:], U, [[D, G], [3, U], [1, 3]])
                    nc.scalar.copy(feat[m][:, :, 0:U], src[m][:, :, 0:U])
                    nc.scalar.copy(feat[m][:, :, 2 * U:5 * U], src[m][:, :, U:D])
                    nc.scalar.copy(cyclic[m][:, :, :, 0:3], f1)
                    nc.scalar.copy(cyclic[m][:, :, :, 3:5], view(src[m][:], U, [[D, G], [3, U], [1, 2]])).then_inc(copied, 1)
                    block, _ = blocks(act, n)
                    if not first:
                        act.wait_ge(rows_free, n - 1)
                    if not (first and m == 0):
                        act.wait_ge(onehot_ready, n)
                    for j in range(G):
                        last = nc.scalar.activation(difference[:, j, :], nodes[:, bass.ds(block * P, P)], ACT.Abs,
                                                    bias=dst[m][:, j:j + 1], scale=-1.0)
                    last.then_inc(difference_ready, 1)
                    act.wait_ge(difference_ready, n + 1)
                    nc.scalar.activation(onehot[m][:], difference[:], ACT.Relu, bias=one[:, 0:1], scale=-1.0).then_inc(onehot_ready, 1)
                for m in range(2):
                    group(0, m, True)
                with act.Fori(1, PAIRS) as i:
                    for m in range(2):
                        group(i, m, False)
                layer_norm(nc, None, act, k, k.x, None, mean, var, (norm_in, norm_out), 1)

            @block.tensor
            def _(pe):
                pe.wait_ge(w_ready, 2)
                count, extras = pe.alloc_register("m_visits_pe"), pe.alloc_register("m_extras_pe")
                pe.reg_mov(count, 0)
                pe.reg_mov(extras, 0)
                for bank in (1, 2):
                    nc.tensor.matmul(v_ps[:, bank, 0:SUMMED], zero[0:1, 0:P], zero[0:1, :],
                                     start=True, stop=True).then_inc(product_done, 1)

                def radial(n, m, b, first):
                    half = (m * NBAT + b) % 2
                    if not (first and b < 2):
                        pe.wait_ge(r_used, n * NBAT + (b - 1))
                    for t in range(RB):
                        mm = nc.tensor.matmul(r_ps[:, half, t, 0:RD], hid[m][:, b * RB + t, :], w2[:], start=True, stop=True)
                    mm.then_inc(r_ready, 1)

                def product(v, one, m, tiles):
                    for j in tiles:
                        mm = nc.tensor.matmul(view(v_ps[:], (v % 3) * 512, [[1, SUMMED]]), onehot[one][:, j, :],
                                              prod[m][:, j, CW1:CW1 + SUMMED], start=(j == 0), stop=(j == G - 1))
                    if G - 1 in tiles:
                        mm.then_inc(product_done, 1)
                        pe.reg_add(count, count, 1)

                def visit_number():
                    return pe.snap(count, min_val=0, max_val=NG * NB)

                def further_visits(n, m):
                    first, end = blocks(pe, n)
                    with pe.If(end - first > 1):
                        with pe.Fori(first + 1, end):
                            x = pe.snap(extras, min_val=0, max_val=NG * NB)
                            pe.wait_ge(extra_ready, x + 1)
                            pe.reg_add(extras, extras, 1)
                            v = visit_number()
                            await_alone(pe, k.passed_pe, added, v + 2)
                            product(v, 2, m, range(G))
                    pe.drain().then_inc(rows_free, 1)

                def group(n, m):
                    pe.wait_ge(hid_ready, n + 1)
                    v = visit_number()
                    done = 0
                    for b in range(NBAT):
                        radial(n, m, b, False)
                        if b == 1:
                            pe.wait_ge(rows_ready, n)
                            pe.wait_ge(onehot_ready, n)
                            await_alone(pe, k.passed_pe, added, v + 2)
                        if b >= 1:
                            tiles = range(done, G if b == NBAT - 1 else done + BETWEEN[b - 1])
                            product(v, 1 - m, 1 - m, tiles)
                            done = tiles.stop
                    further_visits(n - 1, 1 - m)
                pe.wait_ge(hid_ready, 1)
                for b in range(NBAT):
                    radial(0, 0, b, True)
                group(1, 1)
                with pe.Fori(1, PAIRS) as i:
                    for m in range(2):
                        group(i * 2 + m, m)
                pe.wait_ge(rows_ready, NG)
                pe.wait_ge(onehot_ready, NG)
                v = visit_number()
                await_alone(pe, k.passed_pe, added, v + 2)
                product(v, 1, 1, range(G))
                further_visits(NG - 1, 1)

            @block.vector
            def _(dve):
                tt, ts, red = nc.vector.tensor_tensor, nc.vector.tensor_scalar, nc.vector.tensor_reduce
                for a in hid:
                    nc.vector.memset(a[:], 1.0)
                nc.vector.memset(w2[:], 0.0)
                dve.drain().then_inc(w_ready, 1)
                dve.wait_ge(w_loaded, 64)
                s1 = norm1 * c1 / math.sqrt(3)
                k2 = norm1 * c2 / math.sqrt(10)
                uv = lambda at, step: view(raw[:], at, [[step * U, U], [step, U]])
                to = lambda part, half: view(w2[0:HID + 1, :], part * 2 * U * U + half * U, [[2 * U, U], [1, U]])
                for part, half, frm, scale in (
                        (1, 0, uv(0, 1), norm0 * y0), (1, 1, uv(U * U, 1), norm0 * c1 / math.sqrt(3)),
                        (0, 0, uv(2 * U * U, 1), s1), (0, 1, uv(3 * U * U + 2, 3), k2),
                        (2, 0, uv(3 * U * U, 3), norm1 * y0 / math.sqrt(3)), (2, 1, uv(3 * U * U + 1, 3), norm1 * c1 / math.sqrt(6))):
                    ts(to(part, half), frm, scale, None, ALU.mult)
                dve.drain()
                nc.vector.scalar_tensor_tensor(to(2, 0), uv(3 * U * U + 2, 3), -k2 / 3, to(2, 0), ALU.mult, ALU.add)
                nc.vector.memset(zero[:], 0.0)
                nc.vector.memset(one[:], 1.0)
                nc.vector.memset(sums[:], 0.0)
                fill_nodes(nc, dve, nodes, k.iota)
                dve.drain().then_inc(w_ready, 1)
                dve.sem_inc(added, 2)
                names = ("m_visits_dve", "m_block_1", "m_block_2", "m_extra_used", "m_first", "m_end")
                count, block_1, block_2, extra_used, first_r, end_r = (dve.alloc_register(x) for x in names)
                dve.reg_mov(count, 0)
                dve.reg_mov(block_1, NB)
                dve.reg_mov(block_2, NB)
                dve.reg_mov(extra_used, 2)

                def add(v, drained=False):
                    at = dve.snap(block_2, min_val=0, max_val=NB)
                    bank = ((v + 1) % 3) * 512
                    if not drained:
                        dve.drain()
                    await_alone(dve, k.passed_dve, product_done, v + 1)
                    red(visit[:, 0:U], view(v_ps[:], bank, [[2 * U, U], [1, 2 * U]]), AX.X, ALU.add)
                    red(visit[:, U:D], view(v_ps[:], bank + CW0, [[1, 3 * U], [3 * U, U + 1]]), AX.X, ALU.add)
                    dve.drain()
                    part = view(sums[:], at * D, [[1, D]])
                    tt(part, part, visit[:], ALU.add).then_inc(added, 1)
                    dve.reg_mov(block_2, block_1)

                def one_hot(to, m, b):
                    return tt(to[:], view(kept[m][:], 0, [[1, G], [0, P]]), view(nodes[:], b * P, [[0, G], [1, P]]), ALU.is_equal)

                def visits(m, drained=False):
                    add(dve.snap(count, min_val=0, max_val=NG * NB), drained)
                    dve.reg_mov(block_1, first_r)
                    dve.reg_add(count, count, 1)
                    block, end = dve.snap(first_r, min_val=0, max_val=NB - 1), dve.snap(end_r, min_val=1, max_val=NB)
                    with dve.If(end - block > 1):
                        with dve.Fori(block + 1, end) as b:
                            v = dve.snap(count, min_val=0, max_val=NG * NB)
                            dve.wait_ge(product_done, dve.snap(extra_used, min_val=2, max_val=NG * NB))
                            one_hot(onehot[2], m, b).then_inc(extra_ready, 1)
                            add(v)
                            dve.reg_mov(block_1, b)
                            dve.reg_mov(extra_used, v)
                            dve.reg_add(extra_used, extra_used, 3)
                            dve.reg_add(count, count, 1)

                def group(i, m, first):
                    n = i * 2 + m
                    fe = feat[m][:]
                    dve.wait_ge(features_ready, n + 1)
                    if not first:
                        dve.wait_ge(rows_free, n - 1)
                    for b in range(NBAT):
                        t0 = b * RB
                        at = ((m * NBAT + b) % 2) * RB * 512
                        dve.wait_ge(r_ready, n * NBAT + (b + 1))
                        tt(view(prod[m][:], t0 * PW, [[PW, RB], [2 * U, 2 * U], [1, 2 * U]]),
                           view(r_ps[:], at, [[512, RB], [2 * U, 2 * U], [1, 2 * U]]),
                           view(fe, t0 * FX, [[FX, RB], [0, 2 * U], [1, 2 * U]]), ALU.mult)
                        for t in range(RB):
                            mul = tt(view(prod[m][:], (t0 + t) * PW + CW1 + CW0, [[3, U], [1, 3], [3 * U, 2 * U]]),
                                     view(r_ps[:], at + 512 * t + 4 * U * U, [[2 * U, U], [0, 3], [1, 2 * U]]),
                                     view(fe, (t0 + t) * FX + 2 * U, [[0, U], [1, 3], [3, 2 * U]]), ALU.mult)
                        mul.then_inc(r_used, 1)
                    dve.drain().then_inc(features_used, 1)
                    red(along[:], view(prod[m][:], 0, [[PW, G], [2 * U, U], [1, 2 * U]]), AX.X, ALU.add)
                    if not (first and m == 0):
                        visits(1 - m, drained=True)
                    red(crossed[:], view(prod[m][:], CW1 + CW0 + CWF, [[PW, G], [1, 3 * U], [3 * U, U]]), AX.X, ALU.add)
                    table_first, table_end = blocks(dve, n)
                    dve.reg_mov(first_r, table_first)
                    dve.reg_mov(end_r, table_end)
                    dve.wait_ge(loaded[m], (i + 1) * 48)
                    nc.vector.tensor_copy(kept[m][:], dst[m][:])
                    dve.drain()
                    ready = view(prod[m][:], CW1 + CW0 + CWF, [[PW, G], [3, U], [1, 3]])
                    tt(ready, view(along[:], 0, [[U, G], [1, U], [0, 3]]), view(unit[m][:], 0, [[5, G], [0, U], [1, 3]]), ALU.mult)
                    dve.drain()
                    ready = view(prod[m][:], CW1 + CW0 + CWF, [[PW, G], [1, 3 * U]])
                    tt(ready, ready, crossed[:], ALU.add).then_inc(rows_ready, 1)
                group(0, 0, True)
                group(0, 1, True)
                with dve.Fori(1, PAIRS) as i:
                    for m in range(2):
                        group(i, m, False)
                visits(1)
                for last in range(2):
                    add(dve.snap(count, min_val=0, max_val=NG * NB))
                    dve.reg_mov(block_1, NB)
                    dve.reg_add(count, count, 1)
                dve.drain()
                tt(k.x[:], k.x[:], sums[:, 0:NB, :], ALU.add)
                dve.drain()
                layer_norm(nc, dve, None, k, k.x, sums[:, 0:NB, :], mean, var, (norm_in, norm_out), 1)
                dve.drain().then_inc(out_ready, 1)


_INPUTS = ["x", "src", "dst", "edge_attr_16", "edge_attr_3", "edge_weight",
           "L0_gnn_w1a", "L0_gnn_b1a", "L0_gnn_w1b", "L0_gnn_b1b", "L0_gnn_w2a", "L0_gnn_b2a", "L0_gnn_w2b", "L0_gnn_b2b",
           "L3_gnn_w1", "L3_gnn_b1", "L3_gnn_w2", "L3_gnn_b2"]


def kernel(**inputs):
    import numpy as np
    import concourse.bacc as bacc
    from concourse.bass_utils import run_bass_kernel_spmd

    nc = bacc.Bacc("TRN2", target_bir_lowering=False, num_devices=1)
    arrays, io = {}, {}
    for name in _INPUTS:
        a = np.ascontiguousarray(inputs[name])
        arrays[f"in_{name}"] = a
        io[name] = nc.dram_tensor(f"in_{name}", a.shape, mybir.dt.from_np(a.dtype), kind="ExternalInput").ap()
    out = nc.dram_tensor("out_x", (N, D), F32, kind="ExternalOutput").ap()
    build(nc, io, out)
    result = run_bass_kernel_spmd(nc, [arrays], core_ids=[0])
    return result.results[0]["out_x"]
```
